# Optimizing a Trainium2 kernel written in Bass

```python
import numpy as np
import jax
import jax.numpy as jnp

def _softmax(x, axis=-1):
    return jax.nn.softmax(x, axis=axis)

def _gelu(x):
    return jax.nn.gelu(x, approximate=True)

def _silu(x):
    return jax.nn.silu(x)

def _sigmoid(x):
    return jax.nn.sigmoid(x)

def _layernorm(x, axis=-1, eps=1e-05):
    m = jnp.mean(x, axis=axis, keepdims=True)
    v = jnp.var(x, axis=axis, keepdims=True)
    return (x - m) / jnp.sqrt(v + eps)

def _scatter_add(tgt, idx, src, axis=0):
    return tgt.at[idx].add(src)

def _segment_sum(src, seg, n):
    return jax.ops.segment_sum(src, seg, n)
kernel_name = 'mk_gnn_preln_d4_gnn_r64_5ba721'

def setup_inputs(seed: int=0):
    np.random.seed(seed)
    _w = jnp.asarray

    def _rec_inputs():
        import jax
        import jax.numpy as jnp
        _gk = jax.random.key(seed)
        x = -0.0005121 + 1.001 * jax.random.normal(jax.random.fold_in(_gk, 1), (100000, 64), jnp.float32)
        src = jax.random.randint(jax.random.fold_in(_gk, 2), (50000,), 0, 100000, jnp.int32)
        dst = jnp.minimum((100000 * jax.random.uniform(jax.random.fold_in(_gk, 3), (50000,)) ** 2.0).astype(jnp.int32), 99999)
        _o = jnp.argsort(dst, stable=True)
        src = src[_o]
        dst = dst[_o]
        edge_attr_32 = 0.000196303 + 1.00016 * jax.random.normal(jax.random.fold_in(_gk, 11), (50000, 32), jnp.float32)
        return (x, src, dst, edge_attr_32)
    x, src, dst, edge_attr_32 = _rec_inputs()

    def _L0_gnn_setup():
        import jax, jax.numpy as jnp
        import numpy as np
        N, E, D, T = (50000, 12500, 64, 4)
        FI = D // T
        FO = D // T
        NAGG, NSC = (4, 3)
        AVG_LOG = float(np.log(17.0))

        def _pna(x, recv, send, preW, preb, postW, postb, linW, linb):
            n = x.shape[0]
            xt = x.reshape(n, T, FI)
            h = jnp.concatenate([xt[recv], xt[send]], axis=-1)
            m = jnp.einsum('etf,tfg->etg', h, preW) + preb
            cnt = jax.ops.segment_sum(jnp.ones((recv.shape[0],), m.dtype), recv, n)
            deg = jnp.maximum(cnt, 1.0)[:, None, None]
            mean = jax.ops.segment_sum(m, recv, n) / deg
            mean_sq = jax.ops.segment_sum(m * m, recv, n) / deg
            std = jnp.sqrt(jnp.maximum(mean_sq - mean * mean, 0.0) + 1e-05)
            has = (cnt > 0.0)[:, None, None]
            mn = jnp.where(has, jax.ops.segment_min(m, recv, n), 0.0)
            mx = jnp.where(has, jax.ops.segment_max(m, recv, n), 0.0)
            agg = jnp.concatenate([mean, mn, mx, std], axis=-1)
            amp = jnp.log(deg + 1.0) / AVG_LOG
            out = jnp.concatenate([agg, agg * amp, agg / amp], axis=-1)
            out = jnp.concatenate([xt, out], axis=-1)
            out = jnp.einsum('ntf,tfg->ntg', out, postW) + postb
            return out.reshape(n, T * FO) @ linW + linb
        key = jax.random.key(seed)
        ks = jax.random.split(key, 12)
        rn = lambda k, s: jax.random.normal(k, s, dtype=jnp.float32) * 0.1
        z = lambda s: jnp.zeros(s, jnp.float32)
        post_in = (1 + NAGG * NSC) * FI
        return {'x': jax.random.normal(ks[0], (N, D), dtype=jnp.float32), 'edge_index': jax.random.randint(ks[1], (2, E), 0, N), 'alpha': jnp.full((1,), 0.5, dtype=jnp.float32), 'lin_self_W': rn(ks[2], (D, D)), 'lin_self_b': z((D,)), 'pre_W_s2d': rn(ks[3], (T, 2 * FI, FI)), 'pre_b_s2d': z((T, FI)), 'post_W_s2d': rn(ks[4], (T, post_in, FO)), 'post_b_s2d': z((T, FO)), 'lin_W_s2d': rn(ks[5], (T * FO, D)), 'lin_b_s2d': z((D,)), 'pre_W_d2s': rn(ks[6], (T, 2 * FI, FI)), 'pre_b_d2s': z((T, FI)), 'post_W_d2s': rn(ks[7], (T, post_in, FO)), 'post_b_d2s': z((T, FO)), 'lin_W_d2s': rn(ks[8], (T * FO, D)), 'lin_b_d2s': z((D,))}
    _L0_gnn_all = _L0_gnn_setup()
    _L0_gnn_in = {k: v for k, v in _L0_gnn_all.items() if k in ('alpha', 'lin_self_W', 'lin_self_b', 'pre_W_s2d', 'pre_b_s2d', 'post_W_s2d', 'post_b_s2d', 'lin_W_s2d', 'lin_b_s2d', 'pre_W_d2s', 'pre_b_d2s', 'post_W_d2s', 'post_b_d2s', 'lin_W_d2s', 'lin_b_d2s')}
    del _L0_gnn_all

    def _L1_gnn_setup():
        import jax, jax.numpy as jnp
        import numpy as np
        N_NODES = 100000
        N_EDGES = 15625
        IN_DIM = 64
        OUT_DIM = 64
        key = jax.random.key(seed)
        k1, k2, k3, k4, k5 = jax.random.split(key, 5)
        x = jax.random.normal(k1, (N_NODES, IN_DIM), dtype=jnp.float32)
        edge_index = jax.random.randint(k2, (2, N_EDGES), 0, N_NODES, dtype=jnp.int64)
        bound = 1.0 / np.sqrt(IN_DIM)
        W = jax.random.uniform(k3, (OUT_DIM, IN_DIM), minval=-bound, maxval=bound, dtype=jnp.float32)
        b = jax.random.uniform(k4, (OUT_DIM,), minval=-bound, maxval=bound, dtype=jnp.float32)
        return {'x': x, 'edge_index': edge_index, 'W': W, 'b': b}
    _L1_gnn_all = _L1_gnn_setup()
    _L1_gnn_in = {k: v for k, v in _L1_gnn_all.items() if k in ('W', 'b')}
    del _L1_gnn_all

    def _L2_gnn_setup():
        import jax, jax.numpy as jnp
        import numpy as np
        N_NODES = 50000
        N_EDGES = 12500
        D_NODE = 64
        D_EDGE = 32
        MSG = 16
        key = jax.random.key(seed)
        ks = jax.random.split(key, 7)
        node_features = jax.random.normal(ks[0], (N_NODES, D_NODE), dtype=jnp.float32)
        edge_node_indices = jax.random.randint(ks[1], (2, N_EDGES), 0, N_NODES, dtype=jnp.int64 if jax.config.jax_enable_x64 else jnp.int32)
        edge_features = jax.random.normal(ks[2], (N_EDGES, D_EDGE), dtype=jnp.float32)
        fe_in = 2 * D_NODE + D_EDGE
        fh_in = D_NODE + MSG
        fe_w = jax.random.normal(ks[3], (MSG, fe_in), dtype=jnp.float32) / np.sqrt(fe_in)
        fe_b = jax.random.normal(ks[4], (MSG,), dtype=jnp.float32) * 0.01
        fh_w = jax.random.normal(ks[5], (D_NODE, fh_in), dtype=jnp.float32) / np.sqrt(fh_in)
        fh_b = jax.random.normal(ks[6], (D_NODE,), dtype=jnp.float32) * 0.01
        return {'node_features': node_features, 'edge_node_indices': edge_node_indices, 'edge_features': edge_features, 'fe_w': fe_w, 'fe_b': fe_b, 'fh_w': fh_w, 'fh_b': fh_b}
    _L2_gnn_all = _L2_gnn_setup()
    _L2_gnn_in = {k: v for k, v in _L2_gnn_all.items() if k in ('fe_w', 'fe_b', 'fh_w', 'fh_b')}
    del _L2_gnn_all

    def _L3_gnn_setup():
        import jax, jax.numpy as jnp
        import numpy as np
        N_NODES = 50000
        N_EDGES = 12500
        IN_CH, HID_CH, OUT_CH, HEADS = (64, 32, 64, 8)
        NEG_SLOPE = 0.2

        def _gat_conv(x, src, dst, W, a_s, a_d, b, heads, out_ch, concat):
            n = x.shape[0]
            h = (x @ W).reshape(n, heads, out_ch)
            al_s = jnp.einsum('nhc,hc->nh', h, a_s)
            al_d = jnp.einsum('nhc,hc->nh', h, a_d)
            e = jax.nn.leaky_relu(al_s[src] + al_d[dst], NEG_SLOPE)
            m = jax.ops.segment_max(e, dst, num_segments=n)
            m = jnp.where(jnp.isfinite(m), m, 0.0)
            ex = jnp.exp(e - m[dst])
            denom = jax.ops.segment_sum(ex, dst, num_segments=n)
            alpha = ex / (denom[dst] + 1e-16)
            msg = h[src] * alpha[:, :, None]
            out = jax.ops.segment_sum(msg, dst, num_segments=n)
            out = out.reshape(n, heads * out_ch) if concat else out.mean(axis=1)
            return out + b
        key = jax.random.key(seed)
        ks = jax.random.split(key, 12)
        x = jax.random.normal(ks[0], (N_NODES, IN_CH), dtype=jnp.float32)
        src = jax.random.randint(ks[1], (N_EDGES,), 0, N_NODES)
        dst = jax.random.randint(ks[2], (N_EDGES,), 0, N_NODES)
        edge_index = jnp.stack([src, dst]).astype(jnp.int64)
        g1 = 1.0 / np.sqrt(IN_CH)
        g2 = 1.0 / np.sqrt(HID_CH * HEADS)
        W1 = jax.random.normal(ks[3], (IN_CH, HEADS * HID_CH), dtype=jnp.float32) * g1
        a1_src = jax.random.normal(ks[4], (HEADS, HID_CH), dtype=jnp.float32) * g1
        a1_dst = jax.random.normal(ks[5], (HEADS, HID_CH), dtype=jnp.float32) * g1
        b1 = jnp.zeros((HEADS * HID_CH,), dtype=jnp.float32)
        W2 = jax.random.normal(ks[6], (HEADS * HID_CH, OUT_CH), dtype=jnp.float32) * g2
        a2_src = jax.random.normal(ks[7], (1, OUT_CH), dtype=jnp.float32) * g2
        a2_dst = jax.random.normal(ks[8], (1, OUT_CH), dtype=jnp.float32) * g2
        b2 = jnp.zeros((OUT_CH,), dtype=jnp.float32)
        return {'x': x, 'edge_index': edge_index, 'W1': W1, 'a1_src': a1_src, 'a1_dst': a1_dst, 'b1': b1, 'W2': W2, 'a2_src': a2_src, 'a2_dst': a2_dst, 'b2': b2}
    _L3_gnn_all = _L3_gnn_setup()
    _L3_gnn_in = {k: v for k, v in _L3_gnn_all.items() if k in ('W1', 'a1_src', 'a1_dst', 'b1', 'W2', 'a2_src', 'a2_dst', 'b2')}
    del _L3_gnn_all
    return {'x': x, 'src': src, 'dst': dst, 'edge_attr_32': edge_attr_32, 'L0_gnn_alpha': _L0_gnn_in['alpha'], 'L0_gnn_lin_self_W': _L0_gnn_in['lin_self_W'], 'L0_gnn_lin_self_b': _L0_gnn_in['lin_self_b'], 'L0_gnn_pre_W_s2d': _L0_gnn_in['pre_W_s2d'], 'L0_gnn_pre_b_s2d': _L0_gnn_in['pre_b_s2d'], 'L0_gnn_post_W_s2d': _L0_gnn_in['post_W_s2d'], 'L0_gnn_post_b_s2d': _L0_gnn_in['post_b_s2d'], 'L0_gnn_lin_W_s2d': _L0_gnn_in['lin_W_s2d'], 'L0_gnn_lin_b_s2d': _L0_gnn_in['lin_b_s2d'], 'L0_gnn_pre_W_d2s': _L0_gnn_in['pre_W_d2s'], 'L0_gnn_pre_b_d2s': _L0_gnn_in['pre_b_d2s'], 'L0_gnn_post_W_d2s': _L0_gnn_in['post_W_d2s'], 'L0_gnn_post_b_d2s': _L0_gnn_in['post_b_d2s'], 'L0_gnn_lin_W_d2s': _L0_gnn_in['lin_W_d2s'], 'L0_gnn_lin_b_d2s': _L0_gnn_in['lin_b_d2s'], 'L1_gnn_W': _L1_gnn_in['W'], 'L1_gnn_b': _L1_gnn_in['b'], 'L2_gnn_fe_w': _L2_gnn_in['fe_w'], 'L2_gnn_fe_b': _L2_gnn_in['fe_b'], 'L2_gnn_fh_w': _L2_gnn_in['fh_w'], 'L2_gnn_fh_b': _L2_gnn_in['fh_b'], 'L3_gnn_W1': _L3_gnn_in['W1'], 'L3_gnn_a1_src': _L3_gnn_in['a1_src'], 'L3_gnn_a1_dst': _L3_gnn_in['a1_dst'], 'L3_gnn_b1': _L3_gnn_in['b1'], 'L3_gnn_W2': _L3_gnn_in['W2'], 'L3_gnn_a2_src': _L3_gnn_in['a2_src'], 'L3_gnn_a2_dst': _L3_gnn_in['a2_dst'], 'L3_gnn_b2': _L3_gnn_in['b2']}

def reference(x, src, dst, edge_attr_32, L0_gnn_alpha, L0_gnn_lin_self_W, L0_gnn_lin_self_b, L0_gnn_pre_W_s2d, L0_gnn_pre_b_s2d, L0_gnn_post_W_s2d, L0_gnn_post_b_s2d, L0_gnn_lin_W_s2d, L0_gnn_lin_b_s2d, L0_gnn_pre_W_d2s, L0_gnn_pre_b_d2s, L0_gnn_post_W_d2s, L0_gnn_post_b_d2s, L0_gnn_lin_W_d2s, L0_gnn_lin_b_d2s, L1_gnn_W, L1_gnn_b, L2_gnn_fe_w, L2_gnn_fe_b, L2_gnn_fh_w, L2_gnn_fh_b, L3_gnn_W1, L3_gnn_a1_src, L3_gnn_a1_dst, L3_gnn_b1, L3_gnn_W2, L3_gnn_a2_src, L3_gnn_a2_dst, L3_gnn_b2):
    import jax
    import jax.numpy as jnp

    def _L0_gnn_ref(x, edge_index, alpha, lin_self_W, lin_self_b, pre_W_s2d, pre_b_s2d, post_W_s2d, post_b_s2d, lin_W_s2d, lin_b_s2d, pre_W_d2s, pre_b_d2s, post_W_d2s, post_b_d2s, lin_W_d2s, lin_b_d2s):
        import jax, jax.numpy as jnp
        import numpy as np
        N, E, D, T = (50000, 12500, 64, 4)
        FI = D // T
        FO = D // T
        NAGG, NSC = (4, 3)
        AVG_LOG = float(np.log(17.0))

        def _pna(x, recv, send, preW, preb, postW, postb, linW, linb):
            n = x.shape[0]
            xt = x.reshape(n, T, FI)
            h = jnp.concatenate([xt[recv], xt[send]], axis=-1)
            m = jnp.einsum('etf,tfg->etg', h, preW) + preb
            cnt = jax.ops.segment_sum(jnp.ones((recv.shape[0],), m.dtype), recv, n)
            deg = jnp.maximum(cnt, 1.0)[:, None, None]
            mean = jax.ops.segment_sum(m, recv, n) / deg
            mean_sq = jax.ops.segment_sum(m * m, recv, n) / deg
            std = jnp.sqrt(jnp.maximum(mean_sq - mean * mean, 0.0) + 1e-05)
            has = (cnt > 0.0)[:, None, None]
            mn = jnp.where(has, jax.ops.segment_min(m, recv, n), 0.0)
            mx = jnp.where(has, jax.ops.segment_max(m, recv, n), 0.0)
            agg = jnp.concatenate([mean, mn, mx, std], axis=-1)
            amp = jnp.log(deg + 1.0) / AVG_LOG
            out = jnp.concatenate([agg, agg * amp, agg / amp], axis=-1)
            out = jnp.concatenate([xt, out], axis=-1)
            out = jnp.einsum('ntf,tfg->ntg', out, postW) + postb
            return out.reshape(n, T * FO) @ linW + linb
        src, dst = (edge_index[0], edge_index[1])
        y_self = x @ lin_self_W + lin_self_b
        y_s2d = _pna(x, dst, src, pre_W_s2d, pre_b_s2d, post_W_s2d, post_b_s2d, lin_W_s2d, lin_b_s2d)
        y_d2s = _pna(x, src, dst, pre_W_d2s, pre_b_d2s, post_W_d2s, post_b_d2s, lin_W_d2s, lin_b_d2s)
        a = alpha[0]
        return y_self + (1.0 - a) * y_s2d + a * y_d2s

    def _L1_gnn_ref(x, edge_index, W, b):
        import jax, jax.numpy as jnp
        import numpy as np
        N_NODES = 100000
        N_EDGES = 15625
        IN_DIM = 64
        OUT_DIM = 64
        num_nodes = x.shape[0]
        source, target = (edge_index[0], edge_index[1])
        deg = jax.ops.segment_sum(jnp.ones_like(target, dtype=x.dtype), target, num_segments=num_nodes)
        deg = jnp.maximum(deg, 1.0)
        deg_inv_sqrt = deg ** (-0.5)
        norm = deg_inv_sqrt[source] * deg_inv_sqrt[target]
        messages = x[source] * norm[:, None]
        aggregated = jax.ops.segment_sum(messages, target, num_segments=num_nodes)
        aggregated = aggregated + x
        return aggregated @ W.T + b

    def _L2_gnn_ref(node_features, edge_node_indices, edge_features, fe_w, fe_b, fh_w, fh_b):
        import jax, jax.numpy as jnp
        import numpy as np
        N_NODES = 50000
        N_EDGES = 12500
        D_NODE = 64
        D_EDGE = 32
        MSG = 16
        n1, n2 = (edge_node_indices[0], edge_node_indices[1])
        message_input = jnp.concatenate([node_features[n1], node_features[n2], edge_features], axis=1)
        messages = message_input @ fe_w.T + fe_b
        factors = jax.nn.softmax(jax.nn.leaky_relu(messages, 0.01), axis=1)
        sums = jax.ops.segment_sum(factors, n1, num_segments=node_features.shape[0])
        node_input = jnp.concatenate([node_features, sums], axis=1)
        z = node_input @ fh_w.T + fh_b
        return z

    def _L3_gnn_ref(x, edge_index, W1, a1_src, a1_dst, b1, W2, a2_src, a2_dst, b2):
        import jax, jax.numpy as jnp
        import numpy as np
        N_NODES = 50000
        N_EDGES = 12500
        IN_CH, HID_CH, OUT_CH, HEADS = (64, 32, 64, 8)
        NEG_SLOPE = 0.2

        def _gat_conv(x, src, dst, W, a_s, a_d, b, heads, out_ch, concat):
            n = x.shape[0]
            h = (x @ W).reshape(n, heads, out_ch)
            al_s = jnp.einsum('nhc,hc->nh', h, a_s)
            al_d = jnp.einsum('nhc,hc->nh', h, a_d)
            e = jax.nn.leaky_relu(al_s[src] + al_d[dst], NEG_SLOPE)
            m = jax.ops.segment_max(e, dst, num_segments=n)
            m = jnp.where(jnp.isfinite(m), m, 0.0)
            ex = jnp.exp(e - m[dst])
            denom = jax.ops.segment_sum(ex, dst, num_segments=n)
            alpha = ex / (denom[dst] + 1e-16)
            msg = h[src] * alpha[:, :, None]
            out = jax.ops.segment_sum(msg, dst, num_segments=n)
            out = out.reshape(n, heads * out_ch) if concat else out.mean(axis=1)
            return out + b
        n = x.shape[0]
        loops = jnp.arange(n, dtype=edge_index.dtype)
        src = jnp.concatenate([edge_index[0], loops])
        dst = jnp.concatenate([edge_index[1], loops])
        h = _gat_conv(x, src, dst, W1, a1_src, a1_dst, b1, HEADS, HID_CH, True)
        h = jax.nn.elu(h)
        return _gat_conv(h, src, dst, W2, a2_src, a2_dst, b2, 1, OUT_CH, False)
    edge_index = jnp.stack([src, dst])
    h = jnp.maximum(_layernorm(x, axis=-1), 0.0)
    x = x + _L0_gnn_ref(h, edge_index, L0_gnn_alpha, L0_gnn_lin_self_W, L0_gnn_lin_self_b, L0_gnn_pre_W_s2d, L0_gnn_pre_b_s2d, L0_gnn_post_W_s2d, L0_gnn_post_b_s2d, L0_gnn_lin_W_s2d, L0_gnn_lin_b_s2d, L0_gnn_pre_W_d2s, L0_gnn_pre_b_d2s, L0_gnn_post_W_d2s, L0_gnn_post_b_d2s, L0_gnn_lin_W_d2s, L0_gnn_lin_b_d2s)
    h = jnp.maximum(_layernorm(x, axis=-1), 0.0)
    x = x + _L1_gnn_ref(h, edge_index, L1_gnn_W, L1_gnn_b)
    h = jnp.maximum(_layernorm(x, axis=-1), 0.0)
    x = x + _L2_gnn_ref(h, edge_index, edge_attr_32, L2_gnn_fe_w, L2_gnn_fe_b, L2_gnn_fh_w, L2_gnn_fh_b)
    h = jnp.maximum(_layernorm(x, axis=-1), 0.0)
    x = x + _L3_gnn_ref(h, edge_index, L3_gnn_W1, L3_gnn_a1_src, L3_gnn_a1_dst, L3_gnn_b1, L3_gnn_W2, L3_gnn_a2_src, L3_gnn_a2_dst, L3_gnn_b2)
    return x

_drawn_inputs = setup_inputs


def setup_inputs(seed=0):
    import zlib

    import numpy as np

    out = dict(_drawn_inputs(seed))
    spreads = {'L0_gnn_lin_self_b': (0.0, 0.1),
     'L0_gnn_pre_b_s2d': (0.0, 0.1),
     'L0_gnn_post_b_s2d': (0.0, 0.278),
     'L0_gnn_lin_b_s2d': (0.0, 0.1),
     'L0_gnn_pre_b_d2s': (0.0, 0.1),
     'L0_gnn_post_b_d2s': (0.0, 0.1),
     'L0_gnn_lin_b_d2s': (0.0, 0.1),
     'L3_gnn_b1': (0.0, 0.1),
     'L3_gnn_b2': (0.0, 0.1)}
    factors = {'edge_attr_32': 8.0,
     'L2_gnn_fe_w': 7.368,
     'L2_gnn_fe_b': 8.0,
     'L2_gnn_fh_b': 7.549,
     'L3_gnn_a1_src': 5.172,
     'L3_gnn_a1_dst': 8.0,
     'L3_gnn_a2_src': 8.0,
     'L3_gnn_a2_dst': 8.0}
    for name, (base, spread) in spreads.items():
        noise = np.random.default_rng([zlib.crc32(name.encode()), seed]).standard_normal(out[name].shape)
        drawn = base * np.exp(spread * noise) if base else spread * noise
        out[name] = jnp.asarray(drawn.astype(out[name].dtype))
    for name, factor in factors.items():
        out[name] = (out[name] * factor).astype(out[name].dtype)
    return out
```

```python
from contextlib import ExitStack

import numpy as np

import concourse.bass as bass
from concourse import mybir

P = 128
D = 64
TB = 4
BS = TB * P
CJ = 16
RADIX_BITS = 9
MSG = 16
ED = 32
HEADS, HC = 8, 32
GF = HEADS * HC
HALVES = GF // P
HX = D + 2 * HEADS + D
TX = D + 2 + D
DAW = D + 1
ZW = 2 * CJ * DAW // TB
EPS = 1e-5
BIG = 1e30
SKIP = float(1 << 20)
AVG_LOG = float(np.log(17.0))

F32 = mybir.dt.float32
F16 = mybir.dt.float16
I32 = mybir.dt.int32
ALU = mybir.AluOpType
ACT = mybir.ActivationFunctionType
AX = mybir.AxisListType


class Stage(ExitStack):

    def __init__(self, nc):
        super().__init__()
        self.nc, self.counters = nc, []

    def counter(self, name):
        self.counters.append(self.nc.alloc_semaphore(name=name))
        return self.counters[-1]

    def __exit__(self, *error):
        if self.counters and error[0] is None:
            self.nc.clear_and_free_semaphores(self.counters)
            self.nc.all_engine_barrier()
        return super().__exit__(*error)


def after(eng, sem, value):
    if not isinstance(value, int) or value > 0:
        eng.wait_ge(sem, value)


def ready(eng, sem, i, per=1):
    eng.wait_ge(sem, (i + 1) * per)


def before(eng, sem, i, per=1):
    after(eng, sem, i * per)


def two_back(eng, sem, i, u):
    if not (isinstance(i, int) and i == 0):
        eng.wait_ge(sem, i * 2 + u - 1)


class Chain:

    def __init__(self, eng, sem):
        self.eng, self.sem, self.done, self.n, self.peeled, self.base = eng, sem, 0, 0, 0, 0

    def turn(self, i):
        self.done += self.n
        if isinstance(i, int):
            self.base, self.peeled = self.done, i + 1
        else:
            self.base = i * self.n + (self.done - self.peeled * self.n)
            self.per = self.n
        self.n = 0

    def end(self, count):
        if count > self.peeled:
            self.base = self.done + (count - self.peeled) * self.per
            self.done, self.n = self.base, 0

    def link(self, ins):
        self.n += 1
        ins.then_inc(self.sem, 1)
        self.eng.wait_ge(self.sem, self.base + self.n)


def skewed(eng, pairs, first, second, chain=None):
    def body(i):
        if chain:
            chain.turn(i)
        first(i * 2, 0, i)
        if not (isinstance(i, int) and i == 0):
            second(i * 2 - 1, 1, i - 1)
        first(i * 2 + 1, 1, i)
        second(i * 2, 0, i)

    turns(eng, pairs, body, peeled=2)
    if chain:
        chain.end(pairs)
    second(pairs * 2 - 1, 1, pairs - 1)


def turns(eng, count, body, peeled=1):
    for i in range(min(peeled, count)):
        body(i)
    if count > peeled:
        with eng.Fori(peeled, count) as i:
            body(i)


class Shapes:
    def __init__(self, n, e):
        self.N, self.E = n, e
        self.NJ = -(-(n + 1) // (P * 2 * CJ)) * 2 * CJ
        self.NP = P * self.NJ
        self.CH = self.NJ // CJ
        self.B = 2 * -(-e // (2 * BS))
        self.EP = self.B * BS
        self.T = self.B * TB
        self.LO = 1 << RADIX_BITS
        self.HI = max(16, ((n >> RADIX_BITS) + 16) // 16 * 16)
        assert self.B <= P and self.HI <= self.LO


def setup_constants(nc, K):
    with Stage(nc) as c:
        made = c.counter("consts_made")
        cleared = c.counter("consts_cleared")
        with nc.Block() as block:
            @block.gpsimd
            def _(pool):
                pool.memset(K.ident[:, :], 0.0).then_inc(cleared, 1)
                pool.memset(K.upper[:, :], 0.0).then_inc(cleared, 1)
                pool.memset(K.lower[:, :], 1.0).then_inc(cleared, 1)
                pool.memset(K.ones16[:, :], 1.0).then_inc(made, 1)
                pool.memset(K.ones[:, :], 1.0).then_inc(made, 1)
                pool.memset(K.zeros[:, :], 0.0).then_inc(made, 1)
                pool.iota(K.bins[:, :], [[1, K.bins.shape[1]]], base=0, channel_multiplier=0,
                          allow_small_or_imprecise_dtypes=True).then_inc(made, 1)
                pool.wait_ge(cleared, 3)
                pool.affine_select(out=K.ident[:, :], in_=K.ident[:, :], compare_op=ALU.not_equal, fill=1.0,
                                   base=0, pattern=[[-1, P]], channel_multiplier=1).then_inc(made, 1)
                pool.affine_select(out=K.upper[:, :], in_=K.upper[:, :], compare_op=ALU.is_ge, fill=1.0,
                                   base=0, pattern=[[-1, P]], channel_multiplier=1).then_inc(made, 1)
                pool.affine_select(out=K.lower[:, :], in_=K.lower[:, :], compare_op=ALU.is_ge, fill=0.0,
                                   base=0, pattern=[[-1, P]], channel_multiplier=1).then_inc(made, 1)
                pool.wait_ge(made, 7)


def sort_pass(nc, S, K, name, rows_in, rows_out, shift, bins, aside=None):
    half = S.B // 2
    with Stage(nc) as c:
        def sb(n, shape, dt):
            return c.enter_context(nc.sbuf_tensor(f"{name}_{n}", shape, dt))

        def ps(n, shape):
            return c.enter_context(nc.psum_tensor(f"{name}_{n}", shape, F32))

        def sem(n):
            return c.counter(f"{name}_{n}")

        rows = [[sb(f"rows{w}{u}", [P, TB, 4], I32) for u in range(2)] for w in range(2)]
        digit = [sb(f"digit{u}", [P, TB], I32) for u in range(2)]
        digitf = [sb(f"digitf{u}", [P, TB], F32) for u in range(2)]
        hot = [sb(f"hot{u}", [P, TB, bins], F16) for u in range(2)]
        pick = sb("pick", [P, bins], F32)
        rankf = [sb(f"rankf{u}", [P, TB], F32) for u in range(2)]
        rank = [sb(f"rank{u}", [P, TB], I32) for u in range(2)]
        start = sb("start", [P, bins], F32)
        edge = sb("edge", [2, 4], I32)
        hist = ps("hist", [P, 512])
        seen = [ps(f"seen{b}", [P, 512]) for b in range(2)]

        loaded = [[sem(f"loaded{w}{u}") for u in range(2)] for w in range(2)]
        hist_hot = sem("hist_hot")
        hist_added = sem("hist_added")
        start_made = sem("start_made")
        seeded = sem("seeded")
        hot_made = sem("hot_made")
        seen_ready = sem("seen_ready")
        rank_read = sem("rank_read")
        hot_used = sem("hot_used")
        rank_made = sem("rank_made")
        scattered = [sem(f"scattered{u}") for u in range(2)]
        chain = sem("chain")
        edge_made = sem("edge_made")
        edge_out = sem("edge_out")

        blocks_in = rows_in.rearrange("(b k p) f -> b p k f", k=TB, p=P)

        with nc.Block() as block:
            @block.scalar
            def _(act):
                if aside:
                    aside(act)

            @block.sync
            def _(sp):
                sp.wait_ge(edge_made, 1)
                sp.dma_start(rows_out[0:1, :], edge[0:1, :]).then_inc(edge_out, 16)
                sp.dma_start(rows_out[S.EP + 1:S.EP + 2, :], edge[1:2, :]).then_inc(edge_out, 16)

                def load(w):
                    def body(i):
                        for u in range(2):
                            if w == 0:
                                two_back(sp, hist_hot, i, u)
                            else:
                                before(sp, scattered[u], i, 16 * TB)
                            b = i * 2 + u
                            sp.dma_start(rows[w][u][:, :, :],
                                         blocks_in[bass.ds(b, 1)].rearrange("a p k f -> (a p) k f")
                                         ).then_inc(loaded[w][u], 16)
                    return body

                turns(sp, half, load(0))
                turns(sp, half, load(1))
                sp.wait_ge(edge_out, 32)

            @block.gpsimd
            def _(pool):
                pool.memset(edge[:, :], -1).then_inc(edge_made, 1)

                def body(i):
                    for u in range(2):
                        pool.wait_ge(rank_made, i * 2 + u + 1)
                        pool.nop(nofuse=True)
                        for k in range(TB):
                            pool.indirect_dma_start(
                                rows_out[:, :], bass.IndirectOffsetOnAxis(rank[u][:, k:k + 1], 0),
                                rows[1][u][:, k, :], None).then_inc(scattered[u], 16)

                turns(pool, half, body)
                for u in range(2):
                    pool.wait_ge(scattered[u], 16 * TB * half)

            def digits(dve, link, i, w, u):
                ready(dve, loaded[w][u], i, 16)
                link(dve.tensor_scalar(digit[u][:, :], rows[w][u][:, :, 0], shift, (1 << RADIX_BITS) - 1,
                                       ALU.arith_shift_right, ALU.bitwise_and))
                link(dve.tensor_copy(digitf[u][:, :], digit[u][:, :]))
                for k in range(TB):
                    ins = dve.tensor_scalar(hot[u][:, k, :], K.bins[:, 0:bins], digitf[u][:, k:k + 1], None,
                                            ALU.is_equal)
                return ins

            @block.vector
            def _(dve):
                own = Chain(dve, chain)

                def count(i):
                    own.turn(i)
                    for u in range(2):
                        two_back(dve, hist_added, i, u)
                        digits(dve, own.link, i, 0, u).then_inc(hist_hot, 1)

                turns(dve, half, count)
                own.end(half)
                dve.wait_ge(hist_added, 2 * half)
                dve.wait_ge(hist_hot, 2 * half)
                own.link(dve.tensor_tensor_scan(start[:, :], hist[:, 0:bins], K.zeros[:, 0:bins], 1.0, ALU.add,
                                                ALU.add))
                dve.tensor_tensor(start[:, :], start[:, :], hist[:, 0:bins], ALU.subtract).then_inc(start_made, 1)

                own2 = Chain(dve, hot_made)

                def place(i):
                    own2.turn(i)
                    for u in range(2):
                        two_back(dve, hot_used, i, u)
                        before(dve, scattered[u], i, 16 * TB)
                        own2.link(digits(dve, own2.link, i, 1, u))
                        for k in range(TB):
                            dve.wait_ge(seen_ready, (i * 2 + u) * TB + k + 1)
                            dve.tensor_tensor_reduce(pick[:, :], hot[u][:, k, :], seen[k % 2][:, 0:bins], 1.0,
                                                     0.0, ALU.mult, ALU.add, rankf[u][:, k:k + 1]
                                                     ).then_inc(rank_read, 1)
                            dve.wait_ge(rank_read, (i * 2 + u) * TB + k + 1)
                        dve.tensor_copy(rank[u][:, :], rankf[u][:, :]).then_inc(rank_made, 1)
                        dve.wait_ge(rank_made, i * 2 + u + 1)

                turns(dve, half, place)

            @block.tensor
            def _(pe):
                def count(i):
                    for u in range(2):
                        ready(pe, hist_hot, i * 2 + u)
                        for k in range(TB):
                            first = isinstance(i, int) and i == 0 and u == 0 and k == 0
                            ins = pe.matmul(hist[:, 0:bins], K.ones16[:, :], hot[u][:, k, :], start=first,
                                            stop=True, skip_group_check=True)
                        ins.then_inc(hist_added, 1)

                turns(pe, half, count)
                pe.wait_ge(start_made, 1)
                for b in range(2):
                    pe.matmul(seen[b][:, 0:bins], K.ident[:, :], start[:, :], start=True, stop=True,
                              skip_group_check=True)

                def add(b, mask, u, k):
                    return pe.matmul(seen[b][:, 0:bins], mask[:, :], hot[u][:, k, :], start=False, stop=True,
                                     skip_group_check=True)

                def place(i):
                    for u in range(2):
                        pe.wait_ge(hot_made, (i * 2 + u + 1) * 3)
                        for k in range(TB):
                            b = k % 2
                            add(b, K.upper, u, k).then_inc(seen_ready, 1)
                            if k > 0:
                                pe.wait_ge(rank_read, (i * 2 + u) * TB + k)
                                add(1 - b, K.lower, u, k - 1)
                            add(1 - b, K.ones16, u, k)
                        pe.wait_ge(rank_read, (i * 2 + u) * TB + TB)
                        add((TB - 1) % 2, K.lower, u, TB - 1).then_inc(hot_used, 1)

                turns(pe, half, place)


def prepare_order(nc, S, K, name, rows, fields, index, flags, counts):
    with Stage(nc) as c:
        def sb(n, shape, dt=F32):
            return c.enter_context(nc.sbuf_tensor(f"{name}_{n}", shape, dt))

        def sem(n):
            return c.counter(f"{name}_{n}")

        B = S.B
        cur, prv, nxt = (sb(n, [B, BS, 4], I32) for n in ("cur", "prv", "nxt"))
        key, pkey, nkey, same, end = (sb(n, [B, BS]) for n in ("key", "pkey", "nkey", "same", "end"))
        col = [sb(f"col{j}", [B, BS]) for j in range(len(fields))]
        local, unbroken, cnt, rcnt = (sb(n, [B, BS]) for n in ("local", "unbroken", "cnt", "rcnt"))
        lrow, urow, ends, carry = (sb(n, [1, B]) for n in ("lrow", "urow", "ends", "carry"))
        carry_col = sb("carry_col", [B, 1])
        turned = [c.enter_context(nc.psum_tensor(f"{name}_turned{b}", [P, TB, P], F32)) for b in range(2)]
        small = c.enter_context(nc.psum_tensor(f"{name}_small", [P, 512], F32))
        loaded, own, ends_made, ends_turned, carry_made, carry_turned, cnt_made, stored, cols_made, turned_sem, \
            taken, act_own = (sem(n) for n in (
                "loaded", "own", "ends_made", "ends_turned", "carry_made", "carry_turned", "cnt_made",
                "stored", "cols_made", "turned", "taken", "act_own"))
        todo = [*range(len(fields)), "cnt"]

        with nc.Block() as block:
            @block.sync
            def _(sp):
                for off, tile in ((1, cur), (0, prv), (2, nxt)):
                    sp.dma_start(tile[:, :, :], rows[off:off + S.EP, :].rearrange("(b s) f -> b s f", s=BS)
                                 ).then_inc(loaded, 16)
                sp.wait_ge(cnt_made, 1)
                for j, tile in enumerate((same, rcnt)):
                    sp.dma_start(flags[j, :].rearrange("(b s) -> b s", s=BS), tile[:, :]).then_inc(stored, 16)
                sp.wait_ge(stored, 32)

            @block.vector
            def _(dve):
                link = Chain(dve, own).link
                dve.wait_ge(loaded, 48)
                for tile, rows3 in ((key, cur), (pkey, prv), (nkey, nxt)):
                    link(dve.tensor_copy(tile[:, :], rows3[:, :, 0]))
                link(dve.tensor_tensor(same[:, :], key[:, :], pkey[:, :], ALU.is_equal))
                link(dve.tensor_tensor(end[:, :], key[:, :], nkey[:, :], ALU.is_equal))
                for j, f in enumerate(fields):
                    if f == "end":
                        ins = dve.scalar_tensor_tensor(col[j][:, :], end[:, :], SKIP, key[:, :], ALU.mult, ALU.add)
                    else:
                        ins = dve.tensor_copy(col[j][:, :], cur[:, :, f])
                    ins.then_inc(cols_made, 1)
                link(dve.tensor_tensor_scan(local[:, :], same[:, :], K.ones[0:B, 0:BS], 0.0, ALU.mult, ALU.add))
                dve.tensor_tensor_scan(unbroken[:, :], same[:, :], K.ones[0:B, 0:BS], 1.0, ALU.mult, ALU.mult
                                       ).then_inc(ends_made, 1)
                dve.wait_ge(ends_turned, 1)
                link(dve.tensor_copy(lrow[:, :], small[0:1, 0:B]))
                link(dve.tensor_copy(urow[:, :], small[0:1, 128:128 + B]))
                link(dve.tensor_tensor_scan(ends[:, :], urow[:, :], lrow[:, :], 0.0, ALU.mult, ALU.add))
                link(dve.memset(carry[:, :], 0.0))
                dve.tensor_copy(carry[:, 1:B], ends[:, 0:B - 1]).then_inc(carry_made, 1)
                dve.wait_ge(carry_turned, 1)
                link(dve.tensor_copy(carry_col[:, :], small[0:B, 256:257]))
                link(dve.scalar_tensor_tensor(cnt[:, :], unbroken[:, :], carry_col[:, 0:1], local[:, :],
                                              ALU.mult, ALU.add))
                dve.reciprocal(rcnt[:, :], cnt[:, :]).then_inc(cnt_made, 1)
                for n, f in enumerate(todo):
                    dve.wait_ge(turned_sem, n + 1)
                    src = turned[n % 2][:, :, 0:B]
                    dst = counts.cnt if f == "cnt" else index[:, :, TB * f:TB * f + TB]
                    dve.tensor_copy(dst.rearrange("p b k -> p k b"), src).then_inc(taken, 1)
                dve.wait_ge(taken, len(todo))
                dve.wait_ge(act_own, 3)
                link(dve.tensor_scalar(counts.amp, counts.amp, 1.0 / AVG_LOG, None, ALU.mult))
                link(dve.reciprocal(counts.ramp, counts.amp))
                if counts.dinv is not None:
                    link(dve.reciprocal(counts.dinv, counts.dinv))

            @block.scalar
            def _(act):
                act.wait_ge(taken, len(todo))
                act.activation(counts.amp, counts.cnt, ACT.Ln, bias=1.0).then_inc(act_own, 1)
                act.wait_ge(act_own, 1)
                if counts.dinv is not None:
                    act.activation(counts.dinv, counts.cnt, ACT.Sqrt).then_inc(act_own, 2)
                else:
                    act.sem_inc(act_own, 2)

            @block.tensor
            def _(pe):
                pe.wait_ge(ends_made, 1)
                pe.transpose(small[0:1, 0:B], local[:, BS - 1:BS], K.ident[0:B, 0:B])
                pe.transpose(small[0:1, 128:128 + B], unbroken[:, BS - 1:BS], K.ident[0:B, 0:B]).then_inc(ends_turned, 1)
                pe.wait_ge(carry_made, 1)
                pe.matmul(small[0:B, 256:257], carry[0:1, 0:B], K.ones[0:1, 0:1], start=True, stop=True
                          ).then_inc(carry_turned, 1)
                for n, f in enumerate(todo):
                    if f == "cnt":
                        pe.wait_ge(cnt_made, 1)
                    else:
                        pe.wait_ge(cols_made, f + 1)
                    if n >= 2:
                        pe.wait_ge(taken, n - 1)
                    src = cnt if f == "cnt" else col[f]
                    for k in range(TB):
                        ins = pe.transpose(turned[n % 2][:, k, 0:B], src[:, k * P:(k + 1) * P], K.ident[0:B, 0:B])
                    ins.then_inc(turned_sem, 1)


class Counts:

    def __init__(self, cnt, amp, ramp, dinv=None):
        self.cnt, self.amp, self.ramp, self.dinv = cnt, amp, ramp, dinv


def make_constants(nc, c):
    class K:
        pass

    def sb(n, shape, dt=F32):
        return c.enter_context(nc.sbuf_tensor(n, shape, dt))

    K.ident, K.ones, K.zeros = sb("ident", [P, P]), sb("ones", [P, 512]), sb("zeros", [P, ZW])
    K.upper, K.lower, K.ones16 = sb("upper", [P, P], F16), sb("lower", [P, P], F16), sb("ones16", [P, P], F16)
    K.bins = sb("bins", [P, 512], F16)
    setup_constants(nc, K)
    return K


STD0 = float(np.sqrt(np.float32(EPS)))
AMP0 = float(np.log(2.0)) / AVG_LOG
SCALERS = (1.0, AMP0, 1.0 / AMP0)
NS = 3 * D
XPART = 2 * D


class Side:

    def __init__(self, nc, c, name):
        def sb(n, shape):
            return c.enter_context(nc.sbuf_tensor(f"{name}_{n}", shape, F32))

        self.name = name
        self.pre = sb("pre", [P, P])
        self.bias = sb("bias", [P, 1])
        self.sbias = sb("sbias", [P, 1])
        self.nbias = sb("nbias", [D, 1])
        self.mean_std = sb("mean_std", [P, NS])
        self.max_min = sb("max_min", [P, NS])
        self.minus0 = sb("minus0", [P, D])


def pna_weights(nc, S, K, side, share, inp, shared):
    n = side.name
    with Stage(nc) as c:
        def sb(x, shape):
            return c.enter_context(nc.sbuf_tensor(f"{n}w_{x}", shape, F32))

        def ps(x, shape):
            return c.enter_context(nc.psum_tensor(f"{n}w_{x}", shape, F32))

        def sem(x):
            return c.counter(f"{n}w_{x}")

        post = sb("post", [D, XPART + 12 * D])
        lin = sb("lin", [D, D])
        postb, linb = sb("postb", [D, 1]), sb("linb", [P, D])
        postb_wide, none = sb("postb_wide", [D, P]), sb("none", [P, 3, P])
        coef, scoef = sb("coef", [P, 1]), sb("scoef", [P, 1])
        shift = sb("shift", [P, D])
        p_own, p_bias, p_none = ps("p_own", [P, 512]), ps("p_bias", [P, 512]), ps("p_none", [P, 512])
        p_ms, p_mm = ps("p_ms", [P, 512]), ps("p_mm", [P, 512])
        loaded, own, wide_made, products, scaled, none_ready = (
            sem(x) for x in ("loaded", "own", "wide_made", "products", "scaled", "none_ready"))
        loads = [(side.pre[:, :], inp[f"pre_{n}"]), (side.bias[:, :], inp[f"preb_{n}"]),
                 (post[:, :], inp[f"post_{n}"]), (lin[:, :], inp[f"lin_{n}"]),
                 (postb[:, :], inp[f"postb_{n}"]),
                 (linb[:, :], inp[f"linb_{n}"].partition_broadcast(P)),
                 (coef[:, :], inp["alpha"].partition_broadcast(P))]
        if share == 0:
            loads += [(shared.base_w[h * D:(h + 1) * D, :], inp["self_w"]) for h in range(2)]
            loads += [(shared.base_b[:, :], inp["self_b"].partition_broadcast(P))]

        with nc.Block() as block:
            @block.sync
            def _(sp):
                for dst, src in loads:
                    sp.dma_start(dst, src).then_inc(loaded, 16)

            @block.vector
            def _(dve):
                link = Chain(dve, own).link
                link(dve.memset(none[:, :, :], 0.0))
                for s in range(3):
                    link(dve.memset(none[D:P, s, :], STD0 * SCALERS[s]))
                dve.wait_ge(loaded, 16 * len(loads))
                if share == 0:
                    link(dve.tensor_scalar(coef[:, :], coef[:, :], -1.0, 1.0, ALU.mult, ALU.add))
                link(dve.tensor_copy(scoef[:, :], coef[:, :]))
                link(dve.tensor_scalar(scoef[D:P, :], coef[D:P, :], -1.0, None, ALU.mult))
                link(dve.tensor_copy(side.sbias[:, :], side.bias[:, :]))
                link(dve.tensor_scalar(side.nbias[:, :], side.bias[0:D, :], -1.0, None, ALU.mult))
                link(dve.tensor_scalar(side.sbias[D:P, :], side.bias[D:P, :], -1.0, None, ALU.mult))
                dve.tensor_scalar(postb_wide[:, :], K.ones[0:D, 0:P], postb[:, 0:1], None, ALU.mult
                                  ).then_inc(wide_made, 1)
                dve.wait_ge(products, 1)
                link(dve.tensor_scalar(side.mean_std[:, :], p_ms[:, 0:NS], coef[:, 0:1], None, ALU.mult))
                dve.tensor_scalar(side.max_min[:, :], p_mm[:, 0:NS], scoef[:, 0:1], None, ALU.mult
                                  ).then_inc(scaled, 1)
                link(dve.scalar_tensor_tensor(shared.base_w[:, :], p_own[:, 0:D], coef[:, 0:1],
                                              shared.base_w[:, :], ALU.mult, ALU.add))
                link(dve.tensor_tensor(shift[:, :], p_bias[:, 0:D], linb[:, :], ALU.add))
                link(dve.scalar_tensor_tensor(shared.base_b[:, :], shift[:, :], coef[:, 0:1],
                                              shared.base_b[:, :], ALU.mult, ALU.add))
                dve.wait_ge(none_ready, 1)
                link(dve.tensor_scalar(side.minus0[:, :], p_none[:, 0:D], -1.0, None, ALU.mult))
                link(dve.tensor_tensor(shared.base_b[:, :], shared.base_b[:, :], p_none[:, 0:D], ALU.add))

            @block.tensor
            def _(pe):
                pe.wait_ge(wide_made, 1)
                pe.wait_ge(loaded, 16 * len(loads))
                for s in range(3):
                    at = XPART + 4 * D * s
                    pe.matmul(p_ms[:, s * D:(s + 1) * D], post[:, at:at + P], lin[:, :], start=True, stop=True)
                    pe.matmul(p_mm[:, s * D:(s + 1) * D], post[:, at + P:at + 2 * P], lin[:, :], start=True, stop=True)
                pe.matmul(p_own[:, 0:D], post[:, 0:P], lin[:, :], start=True, stop=True)
                pe.matmul(p_bias[:, 0:D], postb_wide[:, :], lin[:, :], start=True, stop=True).then_inc(products, 1)
                pe.wait_ge(scaled, 1)
                for s in range(3):
                    ins = pe.matmul(p_none[:, 0:D], none[:, s, :], side.mean_std[:, s * D:(s + 1) * D],
                                    start=(s == 0), stop=(s == 2))
                ins.then_inc(none_ready, 1)


def pna_pass(nc, S, K, side, table, index, gather_fields, end_field, flags, counts, aggregates, other=None):
    n = side.name
    per = len(gather_fields)
    with Stage(nc) as c:
        def sb(x, shape, dt=F32):
            return c.enter_context(nc.sbuf_tensor(f"{n}_{x}", shape, dt))

        def ps(x, shape):
            return c.enter_context(nc.psum_tensor(f"{n}_{x}", shape, F32))

        def sem(x):
            return c.counter(f"{n}_{x}")

        ends = sb("ends", [P, TB, per, D])
        gidx, sidx = sb("gidx", [P, TB * per], I32), sb("sidx", [P, TB], I32)
        fl, pen = sb("fl", [P, 2, BS]), sb("pen", [P, BS])
        ht = sb("ht", [P, BS])
        msg, pair = sb("msg", [P, BS]), sb("pair", [P, BS])
        sums, tops, agg = sb("sums", [P, BS]), sb("tops", [P, BS]), sb("agg", [P, BS])
        square = sb("square", [P, BS])
        last_sum, last_top, sign = sb("last_sum", [P, 1]), sb("last_top", [P, 1]), sb("sign", [P, 1])
        back = sb("back", [P, TB, D])
        part = sb("part", [P, D])
        rows = sb("rows", [P, TB, DAW])
        p_t, p_m, p_b = ps("p_t", [P, BS]), ps("p_m", [P, BS]), ps("p_b", [P, TB, D])
        p_o = ps("p_o", [P, 2, 2, 256])

        gathered = [sem(f"gathered{k}") for k in range(TB)]
        turned, gidx_in, sidx_in, scattered, flags_in, ht_made, m_ready, x_made, b_ready, b_taken, \
            b_stored, pen_made, mean_made, square_made, var_made, std_made, out_ready, rows_made, own, init = (
                sem(x) for x in (
                    "turned", "gidx_in", "sidx_in", "scattered", "flags_in", "ht_made", "m_ready", "x_made",
                    "b_ready", "b_taken", "b_stored", "pen_made", "mean_made", "square_made",
                    "var_made", "std_made", "out_ready", "rows_made", "own", "init"))

        with nc.Block() as block:
            @block.gpsimd
            def _(pool):
                def gather(g):
                    for k in range(TB):
                        before(pool, gathered[k], g, 16 * per)
                    for j, f in enumerate(gather_fields):
                        ins = pool.tensor_copy(gidx[:, TB * j:TB * j + TB],
                                               index[:, bass.ds(g, 1), TB * f:TB * f + TB].rearrange("p a k -> p (a k)"))
                    ins.then_inc(gidx_in, 1)
                    ready(pool, gidx_in, g)
                    for k in range(TB):
                        after(pool, turned, (g - 1) * TB + k + 1)
                        pool.nop(nofuse=True)
                        for j in range(per):
                            pool.indirect_dma_start(
                                ends[:, k, j, :], None, table,
                                bass.IndirectOffsetOnAxis(gidx[:, TB * j + k:TB * j + k + 1], 0)
                            ).then_inc(gathered[k], 16)

                def scatter(h):
                    before(pool, scattered, h, 16 * TB)
                    pool.tensor_copy(sidx[:, :], index[:, bass.ds(h, 1), TB * end_field:TB * end_field + TB]
                                     .rearrange("p a k -> p (a k)")).then_inc(sidx_in, 1)
                    ready(pool, sidx_in, h)
                    for k in range(TB):
                        pool.wait_ge(rows_made, h * TB + k + 1)
                        pool.nop(nofuse=True)
                        pool.indirect_dma_start(aggregates, bass.IndirectOffsetOnAxis(sidx[:, k:k + 1], 0),
                                                rows[:, k, :], None, bounds_check=S.NP - 1, oob_is_err=False
                                                ).then_inc(scattered, 16)

                def body(g):
                    gather(g)
                    if not (isinstance(g, int) and g == 0):
                        scatter(g - 1)

                turns(pool, S.B, body, peeled=2)
                scatter(S.B - 1)
                pool.wait_ge(scattered, 16 * TB * S.B)

            @block.sync
            def _(sp):
                def body(g):
                    before(sp, mean_made, g)
                    sp.dma_start(fl[:, :, :], flags[:, bass.ds(g * BS, BS)].partition_broadcast(P)
                                 ).then_inc(flags_in, 16)
                    if other:
                        ready(sp, b_taken, g)
                        sp.dma_start(other[1][bass.ds(g * BS, BS), :].rearrange("(k p) f -> p k f", p=P),
                                     back[:, :, :]).then_inc(b_stored, 16)

                turns(sp, S.B, body)
                if other:
                    sp.wait_ge(b_stored, 16 * S.B)

            @block.tensor
            def _(pe):
                def body(g):
                    if other:
                        before(pe, ht_made, g)
                        for k in range(TB):
                            ready(pe, gathered[k], g, 16 * per)
                            pe.transpose(p_t[:, k * P:(k + 1) * P], ends[:, k, :, :].rearrange("p a f -> p (a f)"),
                                         K.ident[:, :]).then_inc(turned, 1)
                        ready(pe, ht_made, g)
                        before(pe, x_made, g)
                        pe.matmul(p_m[:, :], side.pre[:, :], ht[:, :], start=True, stop=True).then_inc(m_ready, 1)
                        before(pe, b_taken, g)
                        for k in range(TB):
                            ins = pe.matmul(p_b[:, k, :], ht[:, k * P:(k + 1) * P], other[0].pre[:, 0:D],
                                            start=True, stop=True)
                        ins.then_inc(b_ready, 1)
                    else:
                        before(pe, x_made, g)
                        for k in range(TB):
                            ready(pe, gathered[k], g, 16 * per)
                            pe.nop(nofuse=True)
                            pe.transpose(p_m[0:D, k * P:(k + 1) * P], ends[:, k, 0, :], K.ident[:, :]
                                         ).then_inc(turned, 1)
                    ready(pe, std_made, g)
                    before(pe, rows_made, g, TB)
                    for k in range(TB):
                        o = p_o[:, k // 2, k % 2, 0:NS]
                        pe.matmul(o, agg[:, k * P:(k + 1) * P], side.mean_std[:, :], start=True, stop=False)
                        pe.matmul(o, tops[:, k * P:(k + 1) * P], side.max_min[:, :], start=False, stop=True
                                  ).then_inc(out_ready, 1)

                turns(pe, S.B, body)

            @block.scalar
            def _(act):
                def body(g):
                    if other:
                        ready(act, turned, g, TB)
                        before(act, b_ready, g)
                        act.copy(ht[:, :], p_t[:, :]).then_inc(ht_made, 1)
                        ready(act, m_ready, g)
                    else:
                        ready(act, turned, g, TB)
                    before(act, mean_made, g)
                    if isinstance(g, int) and g == 0:
                        act.wait_ge(init, 1)
                    act.activation(msg[0:D, :], p_m[0:D, :], ACT.Identity, bias=side.bias[0:D, 0:1])
                    if other:
                        act.activation(msg[D:P, :], p_m[D:P, :], ACT.Square, bias=side.bias[D:P, 0:1])
                        act.activation(pair[:, :], p_m[:, :], ACT.Identity, bias=side.sbias[:, 0:1],
                                       scale=sign[:, 0:1]).then_inc(x_made, 1)
                    else:
                        act.activation(msg[D:P, :], p_m[0:D, :], ACT.Square, bias=side.bias[0:D, 0:1])
                        act.activation(pair[0:D, :], p_m[0:D, :], ACT.Identity, bias=side.bias[0:D, 0:1])
                        act.activation(pair[D:P, :], p_m[0:D, :], ACT.Identity, bias=side.nbias[:, 0:1],
                                       scale=-1.0).then_inc(x_made, 1)
                    ready(act, flags_in, g, 16)
                    act.activation(pen[:, :], fl[:, 0, :], ACT.Copy, bias=-BIG, scale=BIG).then_inc(pen_made, 1)
                    if other:
                        ready(act, b_ready, g)
                        before(act, b_stored, g, 16)
                        act.copy(back[:, :, :], p_b[:, :, :]).then_inc(b_taken, 1)
                    ready(act, mean_made, g)
                    act.activation(square[D:P, :], agg[0:D, :], ACT.Square).then_inc(square_made, 1)
                    ready(act, var_made, g)
                    act.activation(agg[D:P, :], agg[D:P, :], ACT.Sqrt).then_inc(std_made, 1)

                turns(act, S.B, body)

            @block.vector
            def _(dve):
                chain = Chain(dve, own)
                link = chain.link
                dve.memset(last_sum[:, :], 0.0)
                dve.memset(last_top[:, :], 0.0)
                dve.memset(sign[0:D, :], 1.0)
                dve.memset(sign[D:P, :], -1.0).then_inc(init, 1)
                dve.wait_ge(init, 1)

                def body(g):
                    chain.turn(g)
                    ready(dve, x_made, g)
                    ready(dve, flags_in, g, 16)
                    ready(dve, pen_made, g)
                    before(dve, out_ready, g, TB)
                    link(dve.tensor_tensor_scan(sums[:, :], fl[:, 0, :], msg[:, :], last_sum[:, 0:1],
                                                ALU.mult, ALU.add))
                    link(dve.tensor_tensor_scan(tops[:, :], pen[:, :], pair[:, :], last_top[:, 0:1],
                                                ALU.add, ALU.max))
                    link(dve.tensor_copy(last_sum[:, :], sums[:, BS - 1:BS]))
                    link(dve.tensor_copy(last_top[:, :], tops[:, BS - 1:BS]))
                    dve.tensor_tensor(agg[:, :], sums[:, :], fl[:, 1, :], ALU.mult).then_inc(mean_made, 1)
                    ready(dve, square_made, g)
                    link(dve.tensor_tensor(agg[D:P, :], agg[D:P, :], square[D:P, :], ALU.subtract))
                    dve.tensor_scalar(agg[D:P, :], agg[D:P, :], 0.0, EPS, ALU.max, ALU.add).then_inc(var_made, 1)
                    before(dve, scattered, g, 16 * TB)
                    link(dve.tensor_copy(rows[:, :, D:DAW], counts.cnt[:, bass.ds(g, 1), :].rearrange("p a k -> p k a")))
                    for k in range(TB):
                        if k % 2 == 0:
                            dve.wait_ge(out_ready, g * TB + k + 2)
                        o = p_o[:, k // 2, k % 2, :]
                        amp, ramp = (x[:, bass.ds(g, 1), k:k + 1].rearrange("p a k -> p (a k)")
                                     for x in (counts.amp, counts.ramp))
                        link(dve.scalar_tensor_tensor(part[:, :], o[:, D:2 * D], amp, side.minus0[:, :],
                                                      ALU.mult, ALU.add))
                        link(dve.scalar_tensor_tensor(part[:, :], o[:, 2 * D:3 * D], ramp, part[:, :],
                                                      ALU.mult, ALU.add))
                        dve.tensor_tensor(rows[:, k, 0:D], o[:, 0:D], part[:, :], ALU.add).then_inc(rows_made, 1)
                        dve.wait_ge(rows_made, g * TB + k + 1)

                turns(dve, S.B, body)


def wide(ap, n):
    return ap.unsqueeze(2).to_broadcast([P, CJ, n])


def by_node(row, n):
    return row.unsqueeze(1).to_broadcast([P, CJ, n])


def in_order(psum):
    return psum.rearrange("p q a f -> p a q f")


def by_two(tile):
    return tile[:, :, :].rearrange("p (a q) f -> p a q f", q=2)


def nothing(c, u, m):
    pass


class Norm:

    def __init__(self, nc, c, name, degrees=False):
        def sb(x, shape):
            return c.enter_context(nc.sbuf_tensor(f"{name}_{x}", shape, F32))

        def sem(x):
            return c.counter(f"{name}_{x}")

        self.w = 2 if degrees else 1
        self.sum, self.off, self.sq = sb("sum", [P, CJ]), sb("off", [P, CJ, D]), sb("sq", [P, CJ, D])
        self.var, self.dev = sb("var", [P, 2, CJ]), sb("dev", [P, 2, CJ])
        self.inv = sb("inv", [P, 2, CJ])
        self.centered, self.squared, self.var_made, self.dev_made = (
            sem(x) for x in ("centered", "squared", "var_made", "dev_made"))

    def vector(self, dve, link, c, x, out, degree=None):
        w = self.w
        link(dve.tensor_reduce(self.sum[:, :], x, AX.X, ALU.add))
        link(dve.tensor_scalar(self.sum[:, :], self.sum[:, :], 1.0 / D, None, ALU.mult))
        dve.tensor_tensor(self.off[:, :, :], x, wide(self.sum[:, :], D), ALU.subtract).then_inc(self.centered, 1)
        if degree is not None:
            link(dve.tensor_scalar(self.var[:, 1, :], degree, 1.0, None, ALU.max))
        ready(dve, self.squared, c)
        link(dve.tensor_reduce(self.var[:, 0, :], self.sq[:, :, :], AX.X, ALU.add))
        dve.tensor_scalar(self.var[:, 0, :], self.var[:, 0, :], 1.0 / D, EPS, ALU.mult, ALU.add
                          ).then_inc(self.var_made, 1)
        ready(dve, self.dev_made, c)
        link(dve.reciprocal(self.inv[:, 0:w, :], self.dev[:, 0:w, :]))
        return dve.scalar_tensor_tensor(out, self.off[:, :, :], 0.0, wide(self.inv[:, 0, :], D), ALU.max, ALU.mult)

    def scalar(self, act, c):
        ready(act, self.centered, c)
        act.activation(self.sq[:, :, :], self.off[:, :, :], ACT.Square).then_inc(self.squared, 1)
        ready(act, self.var_made, c)
        act.activation(self.dev[:, 0:self.w, :], self.var[:, 0:self.w, :], ACT.Sqrt).then_inc(self.dev_made, 1)


def chunk(S, table, c):
    return table.rearrange("(p j) f -> p j f", p=P)[:, bass.ds(c * CJ, CJ), :]


def norm_pass(nc, S, K, x, h_out):
    with Stage(nc) as c:
        xin = [c.enter_context(nc.sbuf_tensor(f"n_x{u}", [P, CJ, D], F32)) for u in range(2)]
        h = [c.enter_context(nc.sbuf_tensor(f"n_h{u}", [P, CJ, D], F32)) for u in range(2)]
        norm = Norm(nc, c, "n_norm")
        loaded = [c.counter(f"n_loaded{u}") for u in range(2)]
        stored = [c.counter(f"n_stored{u}") for u in range(2)]
        made, own = (c.counter(f"n_{x}") for x in ("made", "own"))
        pairs = S.CH // 2
        with nc.Block() as block:
            @block.sync
            def _(sp):
                def body(i):
                    for u in range(2):
                        two_back(sp, made, i, u)
                        sp.dma_start(xin[u][:, :, :], chunk(S, x, i * 2 + u)).then_inc(loaded[u], 16)
                turns(sp, pairs, body)

            @block.gpsimd
            def _(pool):
                pass

            @block.scalar
            def _(act):
                def body(i):
                    for u in range(2):
                        norm.scalar(act, i * 2 + u)
                        ready(act, made, i * 2 + u)
                        act.dma_start(chunk(S, h_out, i * 2 + u), h[u][:, :, :]).then_inc(stored[u], 16)
                turns(act, pairs, body)
                for u in range(2):
                    act.wait_ge(stored[u], 16 * pairs)

            @block.vector
            def _(dve):
                chain = Chain(dve, own)

                def body(i):
                    chain.turn(i)
                    for u in range(2):
                        ready(dve, loaded[u], i, 16)
                        before(dve, stored[u], i, 16)
                        norm.vector(dve, chain.link, i * 2 + u, xin[u][:, :, :], h[u][:, :, :]).then_inc(made, 1)
                        ready(dve, made, i * 2 + u)
                turns(dve, pairs, body)


class Turner:

    def __init__(self, nc, c, name):
        self.psum = c.enter_context(nc.psum_tensor(f"{name}_p", [P, 2, CJ // 4, P], F32))
        self.out = c.enter_context(nc.sbuf_tensor(f"{name}_t", [P, 2, CJ // 4, P], F32))
        self.turned = c.counter(f"{name}_turned")
        self.copied = c.counter(f"{name}_copied")

    def tensor(self, pe, K, c, tiles):
        before(pe, self.copied, c, 2)
        for b in range(2):
            for j in range(CJ // 4):
                ins = pe.transpose(self.psum[:, b, j, :], tiles(b * (CJ // 4) + j), K.ident[:, :])
            ins.then_inc(self.turned, 1)

    def scalar(self, act, c, products, per=1):
        before(act, products, c, per)
        for b in range(2):
            act.wait_ge(self.turned, c * 2 + b + 1)
            act.copy(self.out[:, b, :, :], self.psum[:, b, :, :]).then_inc(self.copied, 1)

    @staticmethod
    def products(pe, turn, psum, weight, done):
        for j in range(CJ):
            t, at = turn.tile(j)
            ins = pe.matmul(psum[:, j % 2, j // 2, :], t, weight[at, :], start=True, stop=True)
            if j >= CJ - 2:
                ins.then_inc(done, 1)

    def tile(self, j):
        q = j // 2
        at = slice((j % 2) * D, (j % 2) * D + D)
        return self.out[at, q // (CJ // 4), q % (CJ // 4), :], at


def pna_out_pass(nc, S, K, x, h, agg_a, agg_b, W, base_out, scaled_out):
    n = "o"
    pairs = S.CH // 2
    with Stage(nc) as c:
        def two(x, shape):
            return [c.enter_context(nc.sbuf_tensor(f"{n}_{x}{u}", shape, F32)) for u in range(2)]

        def ps(x):
            return c.enter_context(nc.psum_tensor(f"{n}_{x}", [P, 2, CJ // 2, D], F32))

        def sem(x):
            return c.counter(f"{n}_{x}")

        xin, hin, ga, gb = two("x", [P, CJ, D]), two("h", [P, CJ, D]), two("ga", [P, CJ, DAW]), two("gb", [P, CJ, DAW])
        rest, y, yb, h1, hs, z = (two(x, [P, CJ, D]) for x in ("rest", "y", "yb", "h1", "hs", "z"))
        p_y, p_z = ps("p_y"), ps("p_z")
        turn0, turn1 = Turner(nc, c, f"{n}_t0"), Turner(nc, c, f"{n}_t1")
        norm = Norm(nc, c, f"{n}_norm", degrees=True)
        loaded, stored_s, stored_z = ([sem(f"{x}{u}") for u in range(2)] for x in ("loaded", "stored_s", "stored_z"))
        own, rest_made, rest_own, y_ready, y_made, yb_made, h1_made, hs_made, z_ready, z_made = (sem(x) for x in (
            "own", "rest_made", "rest_own", "y_ready", "y_made", "yb_made", "h1_made", "hs_made", "z_ready", "z_made"))

        with nc.Block() as block:
            @block.sync
            def _(sp):
                def first(c, u, m):
                    if not (isinstance(c, int) and c < 2):
                        sp.wait_ge(h1_made, c - 1)
                    for src, dst in ((x, xin), (h, hin), (agg_a, ga), (agg_b, gb)):
                        sp.dma_start(dst[u][:, :, :], chunk(S, src, c)).then_inc(loaded[u], 16)

                skewed(sp, pairs, first, nothing)

            @block.gpsimd
            def _(pool):
                chain = Chain(pool, rest_own)

                def first(c, u, m):
                    ready(pool, loaded[u], m, 64)
                    if not (isinstance(c, int) and c < 2):
                        pool.wait_ge(y_made, c - 1)
                    chain.link(pool.tensor_tensor(rest[u][:, :, :], xin[u][:, :, :], ga[u][:, :, 0:D], ALU.add))
                    chain.link(pool.tensor_tensor(rest[u][:, :, :], rest[u][:, :, :], gb[u][:, :, 0:D], ALU.add))
                    pool.tensor_tensor(rest[u][:, :, :], rest[u][:, :, :], by_node(W.base_b[:, :], D), ALU.add
                                       ).then_inc(rest_made, 1)

                def second(c, u, m):
                    ready(pool, y_made, c)
                    if not (isinstance(c, int) and c < 2):
                        pool.wait_ge(z_made, c - 1)
                    pool.tensor_tensor(yb[u][:, :, :], y[u][:, :, :], by_node(W.gcn_b[:, :], D), ALU.add
                                       ).then_inc(yb_made, 1)

                skewed(pool, pairs, first, second, chain)

            @block.tensor
            def _(pe):
                def first(c, u, m):
                    ready(pe, loaded[u], m, 64)
                    turn0.tensor(pe, K, c, lambda j: hin[u][:, 2 * j:2 * j + 2, :].rearrange("p a f -> p (a f)"))
                    ready(pe, turn0.copied, c, 2)
                    before(pe, y_made, c)
                    Turner.products(pe, turn0, p_y, W.base_w, y_ready)

                def second(c, u, m):
                    ready(pe, h1_made, c)
                    turn1.tensor(pe, K, c, lambda j: h1[u][:, 2 * j:2 * j + 2, :].rearrange("p a f -> p (a f)"))
                    ready(pe, turn1.copied, c, 2)
                    before(pe, z_made, c)
                    Turner.products(pe, turn1, p_z, W.gcn_w, z_ready)

                skewed(pe, pairs, first, second)

            @block.scalar
            def _(act):
                def first(c, u, m):
                    turn0.scalar(act, c, y_ready, 2)
                    if not (isinstance(c, int) and c == 0):
                        turn1.scalar(act, c - 1, z_ready, 2)
                    norm.scalar(act, c)

                def store(c, u):
                    ready(act, z_made, c)
                    act.dma_start(chunk(S, base_out, c), z[u][:, :, :]).then_inc(stored_z[u], 16)

                def second(c, u, m):
                    ready(act, hs_made, c)
                    act.dma_start(chunk(S, scaled_out, c), hs[u][:, :, :]).then_inc(stored_s[u], 16)
                    if not (isinstance(c, int) and c == 0):
                        store(c - 1, 1 - u)

                skewed(act, pairs, first, second)
                turn1.scalar(act, S.CH - 1, z_ready, 2)
                store(S.CH - 1, 1)
                for u in range(2):
                    act.wait_ge(stored_s[u], 16 * pairs)
                    act.wait_ge(stored_z[u], 16 * pairs)

            @block.vector
            def _(dve):
                chain = Chain(dve, own)

                def first(c, u, m):
                    ready(dve, y_ready, c, 2)
                    ready(dve, rest_made, c)
                    if not (isinstance(c, int) and c < 2):
                        dve.wait_ge(yb_made, c - 1)
                    dve.tensor_tensor(by_two(y[u]), in_order(p_y[:, :, :, :]), by_two(rest[u]), ALU.add).then_inc(y_made, 1)
                    ready(dve, y_made, c)
                    norm.vector(dve, chain.link, c, y[u][:, :, :], h1[u][:, :, :], ga[u][:, :, D]
                                ).then_inc(h1_made, 1)
                    ready(dve, h1_made, c)
                    before(dve, stored_s[u], m, 16)
                    dve.tensor_tensor(hs[u][:, :, :], h1[u][:, :, :], wide(norm.inv[:, 1, :], D), ALU.mult
                                      ).then_inc(hs_made, 1)
                    ready(dve, hs_made, c)

                def second(c, u, m):
                    ready(dve, z_ready, c, 2)
                    ready(dve, yb_made, c)
                    before(dve, stored_z[u], m, 16)
                    dve.tensor_tensor(by_two(z[u]), in_order(p_z[:, :, :, :]), by_two(yb[u]), ALU.add).then_inc(z_made, 1)
                    ready(dve, z_made, c)

                skewed(dve, pairs, first, second, chain)


NW2 = D + 2
EW = D + 2 * MSG
FH = TB * P


class Rows:

    def __init__(self, nc, c, name, S, index, sources, target=None, per_tile=False):
        def sb(x, shape, dt=F32):
            return c.enter_context(nc.sbuf_tensor(f"{name}_{x}", shape, dt))

        def sem(x):
            return c.counter(f"{name}_{x}")

        self.S, self.index, self.sources, self.target = S, index, sources, target
        self.got = [sb(f"got{j}", [P, TB, w]) for j, (_, _, w) in enumerate(sources)]
        self.gidx = sb("gidx", [P, TB * len(sources)], I32)
        self.gathered = [sem(f"gathered{k}") for k in range(TB)]
        self.gidx_in = sem("gidx_in")
        if target:
            self.rows = sb("rows", [P, TB, target[2]])
            self.sidx = sb("sidx", [P, TB], I32)
            self.sidx_in, self.scattered = sem("sidx_in"), sem("scattered")

    def wait_gathered(self, eng, g, k):
        ready(eng, self.gathered[k], g, 16 * len(self.sources))

    def wait_scattered(self, eng, g):
        before(eng, self.scattered, g, 16 * TB)

    def run(self, pool, freed, rows_made=None):
        S, n = self.S, len(self.sources)

        def fields(tile, at, g, field):
            return pool.tensor_copy(tile[:, at:at + TB], self.index[:, bass.ds(g, 1), TB * field:TB * field + TB]
                                    .rearrange("p a k -> p (a k)"))

        def gather(g):
            for k in range(TB):
                before(pool, self.gathered[k], g, 16 * n)
            for j, (_, f, _) in enumerate(self.sources):
                ins = fields(self.gidx, TB * j, g, f)
            ins.then_inc(self.gidx_in, 1)
            ready(pool, self.gidx_in, g)
            for sem, per in freed:
                before(pool, sem, g, per)
            pool.nop(nofuse=True)
            for k in range(TB):
                for j, (table, _, _) in enumerate(self.sources):
                    pool.indirect_dma_start(
                        self.got[j][:, k, :], None, table,
                        bass.IndirectOffsetOnAxis(self.gidx[:, TB * j + k:TB * j + k + 1], 0)
                    ).then_inc(self.gathered[k], 16)

        def scatter(h):
            before(pool, self.scattered, h, 16 * TB)
            fields(self.sidx, 0, h, self.target[1]).then_inc(self.sidx_in, 1)
            ready(pool, self.sidx_in, h)
            ready(pool, rows_made, h)
            pool.nop(nofuse=True)
            for k in range(TB):
                pool.indirect_dma_start(self.target[0], bass.IndirectOffsetOnAxis(self.sidx[:, k:k + 1], 0),
                                        self.rows[:, k, :], None, bounds_check=S.NP - 1, oob_is_err=False
                                        ).then_inc(self.scattered, 16)

        if not self.target:
            turns(pool, S.B, gather, peeled=2)
            return

        def body(g):
            gather(g)
            if not (isinstance(g, int) and g == 0):
                scatter(g - 1)

        turns(pool, S.B, body, peeled=2)
        scatter(S.B - 1)
        pool.wait_ge(self.scattered, 16 * TB * S.B)


def sum_pass(nc, S, K, n, table, width, index, field, end_field, flags, weight, target, scale=None):
    with Stage(nc) as c:
        def sb(x, shape):
            return c.enter_context(nc.sbuf_tensor(f"{n}_{x}", shape, F32))

        def sem(x):
            return c.counter(f"{n}_{x}")

        rows = Rows(nc, c, n, S, index, [(table, field, width)], (target, end_field, D))
        fl, vals, sums, last = sb("fl", [width, BS]), sb("vals", [width, BS]), sb("sums", [width, BS]), sb("last", [width, 1])
        p_t = c.enter_context(nc.psum_tensor(f"{n}_p_t", [P, BS], F32))
        p_o = c.enter_context(nc.psum_tensor(f"{n}_p_o", [P, TB, D], F32))
        flags_in, turned, vals_made, sums_made, out_ready, rows_made, own = (sem(x) for x in (
            "flags_in", "turned", "vals_made", "sums_made", "out_ready", "rows_made", "own"))

        with nc.Block() as block:
            @block.gpsimd
            def _(pool):
                rows.run(pool, [(turned, 1)], rows_made)

            @block.sync
            def _(sp):
                def body(g):
                    before(sp, sums_made, g)
                    sp.dma_start(fl[:, :], flags[0, bass.ds(g * BS, BS)].partition_broadcast(width)
                                 ).then_inc(flags_in, 16)
                turns(sp, S.B, body)

            @block.tensor
            def _(pe):
                def body(g):
                    before(pe, vals_made, g)
                    for k in range(TB):
                        rows.wait_gathered(pe, g, k)
                        pe.nop(nofuse=True)
                        ins = pe.transpose(p_t[0:width, k * P:(k + 1) * P], rows.got[0][:, k, :], K.ident[:, :])
                    ins.then_inc(turned, 1)
                    ready(pe, sums_made, g)
                    before(pe, rows_made, g)
                    pe.nop(nofuse=True)
                    for k in range(TB):
                        ins = pe.matmul(p_o[:, k, :], sums[:, k * P:(k + 1) * P], weight, start=True, stop=True)
                    ins.then_inc(out_ready, 1)
                turns(pe, S.B, body)

            @block.scalar
            def _(act):
                def body(g):
                    ready(act, turned, g)
                    before(act, sums_made, g)
                    act.copy(vals[:, :], p_t[0:width, :]).then_inc(vals_made, 1)
                turns(act, S.B, body)

            @block.vector
            def _(dve):
                chain = Chain(dve, own)
                chain.link(dve.memset(last[:, :], 0.0))

                def body(g):
                    chain.turn(g)
                    ready(dve, vals_made, g)
                    ready(dve, flags_in, g, 16)
                    before(dve, out_ready, g)
                    dve.tensor_tensor_scan(sums[:, :], fl[:, :], vals[:, :], last[:, 0:1], ALU.mult, ALU.add
                                           ).then_inc(sums_made, 1)
                    ready(dve, sums_made, g)
                    chain.link(dve.tensor_copy(last[:, :], sums[:, BS - 1:BS]))
                    ready(dve, out_ready, g)
                    rows.wait_scattered(dve, g)
                    if scale is None:
                        ins = dve.tensor_copy(rows.rows[:, :, :], p_o[:, :, :])
                    else:
                        ins = dve.tensor_tensor(rows.rows[:, :, :], p_o[:, :, :],
                                                scale[:, bass.ds(g, 1), :].rearrange("p a k -> p (a k)")
                                                .unsqueeze(2).to_broadcast([P, TB, D]), ALU.mult)
                    ins.then_inc(rows_made, 1)
                    ready(dve, rows_made, g)
                turns(dve, S.B, body)


def message_pass(nc, S, K, ends, edge_attr, index, weight, factors):
    n = "m"
    with Stage(nc) as c:
        def sb(x, shape):
            return c.enter_context(nc.sbuf_tensor(f"{n}_{x}", shape, F32))

        def sem(x):
            return c.counter(f"{n}_{x}")

        rows = Rows(nc, c, n, S, index, [(ends, 1, 2 * MSG), (ends, 0, 2 * MSG), (edge_attr, 3, ED)])
        at = sb("at", [ED, BS])
        m, ex, out = sb("m", [P, TB, MSG]), sb("ex", [P, TB, MSG]), sb("out", [P, TB, MSG])
        top, total = sb("top", [P, TB]), sb("total", [P, TB])
        p_t = c.enter_context(nc.psum_tensor(f"{n}_p_t", [P, BS], F32))
        p_m = c.enter_context(nc.psum_tensor(f"{n}_p_m", [P, TB, MSG], F32))
        turned, at_made, m_ready, m_made, ex_made, out_made, stored, own = (sem(x) for x in (
            "turned", "at_made", "m_ready", "m_made", "ex_made", "out_made", "stored", "own"))

        def over(t):
            return t[:, :].unsqueeze(2).to_broadcast([P, TB, MSG])

        with nc.Block() as block:
            @block.gpsimd
            def _(pool):
                rows.run(pool, [(turned, 1), (m_made, 1)])

            @block.sync
            def _(sp):
                def body(g):
                    ready(sp, out_made, g)
                    sp.dma_start(factors[bass.ds(g * BS, BS), :].rearrange("(k p) f -> p k f", p=P),
                                 out[:, :, :]).then_inc(stored, 16)
                turns(sp, S.B, body)
                sp.wait_ge(stored, 16 * S.B)

            @block.tensor
            def _(pe):
                def body(g):
                    before(pe, at_made, g)
                    for k in range(TB):
                        rows.wait_gathered(pe, g, k)
                        pe.nop(nofuse=True)
                        ins = pe.transpose(p_t[0:ED, k * P:(k + 1) * P], rows.got[2][:, k, :], K.ident[:, :])
                    ins.then_inc(turned, 1)
                    ready(pe, at_made, g)
                    before(pe, m_made, g)
                    pe.nop(nofuse=True)
                    for k in range(TB):
                        ins = pe.matmul(p_m[:, k, :], at[:, k * P:(k + 1) * P], weight, start=True, stop=True)
                    ins.then_inc(m_ready, 1)
                turns(pe, S.B, body)

            @block.scalar
            def _(act):
                def body(g):
                    ready(act, turned, g)
                    before(act, m_ready, g)
                    act.copy(at[:, :], p_t[0:ED, :]).then_inc(at_made, 1)
                    ready(act, m_made, g)
                    act.activation(ex[:, :, :], m[:, :, :], ACT.Exp).then_inc(ex_made, 1)
                turns(act, S.B, body)

            @block.vector
            def _(dve):
                chain = Chain(dve, own)
                link = chain.link

                def body(g):
                    chain.turn(g)
                    ready(dve, m_ready, g)
                    for k in range(TB):
                        rows.wait_gathered(dve, g, k)
                    before(dve, ex_made, g)
                    link(dve.tensor_tensor(m[:, :, :], p_m[:, :, :], rows.got[0][:, :, 0:MSG], ALU.add))
                    link(dve.tensor_tensor(m[:, :, :], m[:, :, :], rows.got[1][:, :, MSG:2 * MSG], ALU.add))
                    link(dve.scalar_tensor_tensor(m[:, :, :], m[:, :, :], 0.01, m[:, :, :], ALU.mult, ALU.max))
                    link(dve.tensor_reduce(top[:, :], m[:, :, :], AX.X, ALU.max))
                    dve.tensor_tensor(m[:, :, :], m[:, :, :], over(top), ALU.subtract).then_inc(m_made, 1)
                    ready(dve, ex_made, g)
                    link(dve.tensor_reduce(total[:, :], ex[:, :, :], AX.X, ALU.add))
                    link(dve.reciprocal(total[:, :], total[:, :]))
                    before(dve, stored, g, 16)
                    dve.tensor_tensor(out[:, :, :], ex[:, :, :], over(total), ALU.mult).then_inc(out_made, 1)
                    ready(dve, out_made, g)
                turns(dve, S.B, body)


def gcn_out_pass(nc, S, K, base, delta, W, base_out, ends_out):
    n = "e"
    pairs = S.CH // 2
    with Stage(nc) as c:
        def two(x, shape):
            return [c.enter_context(nc.sbuf_tensor(f"{n}_{x}{u}", shape, F32)) for u in range(2)]

        def sem(x):
            return c.counter(f"{n}_{x}")

        xin, din, x2, xb, h = (two(x, [P, CJ, D]) for x in ("xin", "din", "x2", "xb", "h"))
        z, ends = two("z", [P, CJ, D]), two("ends", [P, CJ, 2 * MSG])
        p_z = c.enter_context(nc.psum_tensor(f"{n}_p_z", [P, 2, 2, 512], F32))
        turn = Turner(nc, c, f"{n}_t")
        norm = Norm(nc, c, f"{n}_norm")
        loaded, stored = ([sem(f"{x}{u}") for u in range(2)] for x in ("loaded", "stored"))
        own, pool_own, x2_made, h_made, z_ready, z_made = (sem(x) for x in (
            "own", "pool_own", "x2_made", "h_made", "z_ready", "z_made"))

        def product(a, b):
            return [p_z[:, q, v, 0:CJ // 4 * EW].rearrange("p (i f) -> p i f", f=EW)[:, :, a:b]
                    for q in range(2) for v in range(2)]

        def like(tile):
            t = tile[:, :, :].rearrange("p (v i q) f -> p v i q f", v=2, q=2)
            return [t[:, v, :, q, :] for q in range(2) for v in range(2)]

        with nc.Block() as block:
            @block.sync
            def _(sp):
                def first(c, u, m):
                    if not (isinstance(c, int) and c < 2):
                        sp.wait_ge(x2_made, c - 1)
                    for src, dst in ((base, xin), (delta, din)):
                        sp.dma_start(dst[u][:, :, :], chunk(S, src, c)).then_inc(loaded[u], 16)
                skewed(sp, pairs, first, nothing)

            @block.gpsimd
            def _(pool):
                chain = Chain(pool, pool_own)

                def first(c, u, m):
                    ready(pool, loaded[u], m, 32)
                    if not (isinstance(c, int) and c < 2):
                        pool.wait_ge(z_made, c - 1)
                    chain.link(pool.tensor_tensor(x2[u][:, :, :], xin[u][:, :, :], din[u][:, :, :], ALU.add))
                    pool.tensor_tensor(xb[u][:, :, :], x2[u][:, :, :], by_node(W.node_b[:, :], D), ALU.add
                                       ).then_inc(x2_made, 1)
                skewed(pool, pairs, first, nothing, chain)

            @block.tensor
            def _(pe):
                def second(c, u, m):
                    ready(pe, h_made, c)
                    turn.tensor(pe, K, c, lambda j: h[u][:, 2 * j:2 * j + 2, :].rearrange("p a f -> p (a f)"))
                    ready(pe, turn.copied, c, 2)
                    before(pe, z_made, c)
                    for j in range(CJ):
                        t, at = turn.tile(j)
                        q, i = j % 2, j // 2
                        i, v = i % (CJ // 4), i // (CJ // 4)
                        ins = pe.matmul(p_z[:, q, v, i * EW:(i + 1) * EW], t, W.node_w[at, :], start=True, stop=True)
                        if j >= CJ - 2:
                            ins.then_inc(z_ready, 1)
                skewed(pe, pairs, nothing, second)

            @block.scalar
            def _(act):
                def first(c, u, m):
                    if not (isinstance(c, int) and c == 0):
                        turn.scalar(act, c - 1, z_ready, 2)
                    norm.scalar(act, c)

                def store(c, u):
                    ready(act, z_made, c)
                    for src, dst in ((z, base_out), (ends, ends_out)):
                        act.dma_start(chunk(S, dst, c), src[u][:, :, :]).then_inc(stored[u], 16)

                def second(c, u, m):
                    if not (isinstance(c, int) and c == 0):
                        store(c - 1, 1 - u)
                skewed(act, pairs, first, second)
                turn.scalar(act, S.CH - 1, z_ready, 2)
                store(S.CH - 1, 1)
                for u in range(2):
                    act.wait_ge(stored[u], 32 * pairs)

            @block.vector
            def _(dve):
                chain = Chain(dve, own)

                def first(c, u, m):
                    ready(dve, x2_made, c)
                    norm.vector(dve, chain.link, c, x2[u][:, :, :], h[u][:, :, :]).then_inc(h_made, 1)
                    ready(dve, h_made, c)

                def second(c, u, m):
                    ready(dve, z_ready, c, 2)
                    before(dve, stored[u], m, 32)
                    for dst, src, add in zip(like(z[u]), product(0, D), like(xb[u])):
                        dve.tensor_tensor(dst, src, add, ALU.add)
                    for dst, src in zip(like(ends[u]), product(D, EW)):
                        ins = dve.tensor_tensor(dst, src, W.msg_b[:, :].unsqueeze(1)
                                                .to_broadcast([P, CJ // 4, 2 * MSG]), ALU.add)
                    ins.then_inc(z_made, 1)
                    ready(dve, z_made, c)
                skewed(dve, pairs, first, second, chain)


def gat_weights(nc, S, K, W, inp):
    n = "w"
    with Stage(nc) as c:
        def sb(x, shape):
            return c.enter_context(nc.sbuf_tensor(f"{n}_{x}", shape, F32))

        def sem(x):
            return c.counter(f"{n}_{x}")

        w1t, a1 = sb("w1t", [P, HALVES, P]), sb("a1", [P, HALVES, 2 * HEADS])
        w2t, a2 = sb("w2t", [D, GF]), sb("a2", [D, 2])
        p_al = c.enter_context(nc.psum_tensor(f"{n}_p_al", [P, 512], F32))
        p_a2 = c.enter_context(nc.psum_tensor(f"{n}_p_a2", [P, HALVES, 2], F32))
        loaded, products, own = (sem(x) for x in ("loaded", "products", "own"))
        loads = [(w1t[:, :, :], inp["w1t"].rearrange("(h p) m -> p h m", p=P)),
                 (a1[:, :, :], inp["a1"].rearrange("(h p) m -> p h m", p=P)),
                 (w2t[:, :], inp["w2t"]), (a2[:, :], inp["a2"]),
                 (W.conv2[:, :, 0:D], inp["w2"].rearrange("(h p) m -> p h m", p=P)),
                 (W.bias1[:, :], inp["b1"].rearrange("(h p) -> p h", p=P)),
                 (W.bias2[:, :], inp["b2"].partition_broadcast(P)),
                 (W.gcn_w[:, :], inp["gcn_w"]), (W.gcn_b[:, :], inp["gcn_b"].partition_broadcast(P)),
                 (W.node_w[:, :], inp["node_w"]), (W.node_b[:, :], inp["node_b"].partition_broadcast(P)),
                 (W.msg_b[:, 0:MSG], inp["msg_b"].partition_broadcast(P)),
                 (W.edge_w[:, :], inp["edge_w"]), (W.sum_w[:, :], inp["sum_w"]), (W.conv1[:, :], inp["w1"])]
        with nc.Block() as block:
            @block.sync
            def _(sp):
                with nc.allow_non_contiguous_dma(reason="a bias into two columns, 256 words"):
                    for dst, src in loads:
                        sp.dma_start(dst, src).then_inc(loaded, 16)

            @block.gpsimd
            def _(pool):
                pool.memset(W.msg_b[:, MSG:2 * MSG], 0.0)
                pool.memset(W.spread[:, :, :], 1.0).then_inc(own, 1)
                pool.wait_ge(own, 1)
                pool.affine_select(out=W.spread[:, :, :], in_=W.spread[:, :, :], compare_op=ALU.is_ge, fill=0.0,
                                   base=0, pattern=[[P, HALVES], [1, P]], channel_multiplier=-HC).then_inc(own, 1)
                pool.wait_ge(own, 2)
                pool.affine_select(out=W.spread[:, :, :], in_=W.spread[:, :, :], compare_op=ALU.is_ge, fill=0.0,
                                   base=HC - 1, pattern=[[-P, HALVES], [-1, P]], channel_multiplier=HC).then_inc(own, 1)
                pool.wait_ge(own, 3)

            @block.tensor
            def _(pe):
                pe.wait_ge(loaded, 16 * len(loads))
                for h in range(HALVES):
                    pe.matmul(p_al[:, 0:2 * HEADS], w1t[:, h, :], a1[:, h, :], start=(h == 0), stop=(h == HALVES - 1))
                for h in range(HALVES):
                    ins = pe.matmul(p_a2[:, h, :], w2t[:, h * P:(h + 1) * P], a2[:, :], start=True, stop=True)
                ins.then_inc(products, 1)

            @block.vector
            def _(dve):
                dve.wait_ge(products, 1)
                dve.tensor_copy(W.al_w[:, :], p_al[:, 0:2 * HEADS])
                dve.tensor_copy(W.conv2[:, :, D:NW2], p_a2[:, :, :])
                dve.tensor_scalar(W.nbias1[:, :], W.bias1[:, :], -1.0, None, ALU.mult)


class Elu:

    def __init__(self, nc, c, name, W):
        def sb(x):
            return [c.enter_context(nc.sbuf_tensor(f"{name}_{x}{f}", [P, BS], F32)) for f in range(HALVES)]

        self.W, self.low, self.high = W, sb("low"), sb("high")
        self.low_own = c.counter(f"{name}_low_own")
        self.made = [c.counter(f"{name}_made{f}") for f in range(HALVES)]

    def scalar(self, act, psum, f, i):
        act.activation(self.low[f][:, :], psum, ACT.Relu, bias=self.W.nbias1[:, f:f + 1], scale=-1.0
                       ).then_inc(self.low_own, 1)
        act.activation(self.high[f][:, :], psum, ACT.Relu, bias=self.W.bias1[:, f:f + 1])
        act.wait_ge(self.low_own, i + 1)
        return act.activation(self.low[f][:, :], self.low[f][:, :], ACT.Exp, scale=-1.0)

    def vector(self, dve, f, out):
        return dve.scalar_tensor_tensor(out, self.low[f][:, :], -1.0, self.high[f][:, :], ALU.add, ALU.add)


def sums_out_pass(nc, S, K, base, delta, W, hx_out, tx_out, out):
    n = "v"
    pairs = S.CH // 2
    UNITS = 4
    with Stage(nc) as c:
        def sb(x, shape):
            return c.enter_context(nc.sbuf_tensor(f"{n}_{x}", shape, F32))

        def two(x, shape):
            return [sb(f"{x}{u}", shape) for u in range(2)]

        def sem(x):
            return c.counter(f"{n}_{x}")

        xin, din, xb = (two(x, [P, CJ, D]) for x in ("xin", "din", "xb"))
        hx, tx = two("hx", [P, CJ, HX]), two("tx", [P, CJ, TX])
        hd = two("hd", [P, CJ, D])
        g = [sb(f"g{f}", [P, BS]) for f in range(HALVES)]
        ob = two("ob", [P, CJ, D])
        p_f = [c.enter_context(nc.psum_tensor(f"{n}_p_f{f}", [P, BS], F32)) for f in range(HALVES)]
        p_al = c.enter_context(nc.psum_tensor(f"{n}_p_al", [P, 2, 512], F32))
        p_o = [c.enter_context(nc.psum_tensor(f"{n}_p_o{v}", [P, 512], F32)) for v in range(2)]
        turn = Turner(nc, c, f"{n}_t")
        norm = Norm(nc, c, f"{n}_norm")
        elu = Elu(nc, c, f"{n}_elu", W)
        loaded, stored_h, stored_t = ([sem(f"{x}{u}") for u in range(2)] for x in ("loaded", "stored_h", "stored_t"))
        own, pool_own, x_made, h_made, al_ready, al_made, o_ready, tx_made, out_made, h_copied = (
            sem(x) for x in (
                "own", "pool_own", "x_made", "h_made", "al_ready", "al_made", "o_ready", "tx_made",
                "out_made", "h_copied"))
        f_ready, parts_made, g_made = ([sem(f"{x}{f}") for f in range(HALVES)] for x in (
            "f_ready", "parts_made", "g_made"))

        def unit_tiles(tile, w, a, b):
            return tile[:, :, :].rearrange("p (v i q) f -> p v i q f", v=2, q=2)[:, w // 2, :, w % 2, a:b]

        with nc.Block() as block:
            @block.sync
            def _(sp):
                def first(c, u, m):
                    if not (isinstance(c, int) and c < 2):
                        sp.wait_ge(x_made, c - 1)
                    for src, dst in ((base, xin), (delta, din)):
                        sp.dma_start(dst[u][:, :, :], chunk(S, src, c)).then_inc(loaded[u], 16)

                def second(c, u, m):
                    ready(sp, al_made, c)
                    ready(sp, h_copied, c)
                    sp.dma_start(chunk(S, hx_out, c), hx[u][:, :, :]).then_inc(stored_h[u], 16)
                    ready(sp, out_made, c)
                    for src, dst in ((tx, tx_out), (ob, out)):
                        sp.dma_start(chunk(S, dst, c), src[u][:, :, :]).then_inc(stored_t[u], 16)
                skewed(sp, pairs, first, second)
                for u in range(2):
                    sp.wait_ge(stored_h[u], 16 * pairs)
                    sp.wait_ge(stored_t[u], 32 * pairs)

            @block.gpsimd
            def _(pool):
                chain = Chain(pool, pool_own)

                def first(c, u, m):
                    ready(pool, loaded[u], m, 32)
                    before(pool, stored_h[u], m, 16)
                    before(pool, stored_t[u], m, 32)
                    chain.link(pool.tensor_tensor(hx[u][:, :, D + 2 * HEADS:HX], xin[u][:, :, :], din[u][:, :, :],
                                                  ALU.add))
                    pool.tensor_tensor(xb[u][:, :, :], hx[u][:, :, D + 2 * HEADS:HX], by_node(W.bias2[:, :], D),
                                       ALU.add)
                    pool.tensor_copy(tx[u][:, :, NW2:TX], hx[u][:, :, D + 2 * HEADS:HX]).then_inc(x_made, 1)
                skewed(pool, pairs, first, nothing, chain)

            @block.tensor
            def _(pe):
                def second(c, u, m):
                    ready(pe, h_made, c)
                    turn.tensor(pe, K, c, lambda j: hd[u][:, 2 * j:2 * j + 2, :].rearrange("p a f -> p (a f)"))
                    ready(pe, turn.copied, c, 2)
                    before(pe, al_made, c)
                    for j in range(CJ):
                        t, at = turn.tile(j)
                        ins = pe.matmul(p_al[:, j % 2, j // 2 * 2 * HEADS:(j // 2 + 1) * 2 * HEADS], t, W.al_w[at, :],
                                        start=True, stop=True)
                        if j >= CJ - 2:
                            ins.then_inc(al_ready, 1)
                    for w in range(UNITS):
                        at = slice((w % 2) * D, (w % 2) * D + D)
                        for f in range(HALVES):
                            before(pe, parts_made[f], c * UNITS + w)
                            pe.nop(nofuse=True)
                            pe.matmul(p_f[f][:, :], W.conv1[at, f * P:(f + 1) * P],
                                      turn.out[at, w // 2, :, :].rearrange("p a b -> p (a b)"), start=True, stop=True
                                      ).then_inc(f_ready[f], 1)
                        if w > 0:
                            second_conv(c, w - 1)
                    second_conv(c, UNITS - 1)

                def second_conv(c, w):
                    for f in range(HALVES):
                        ready(pe, g_made[f], c * UNITS + w)
                    after(pe, tx_made, c * UNITS + w - 1)
                    for i in range(TB):
                        for f in range(HALVES):
                            ins = pe.matmul(p_o[w % 2][:, i * NW2:(i + 1) * NW2], g[f][:, i * P:(i + 1) * P],
                                            W.conv2[:, f, :], start=(f == 0), stop=(f == HALVES - 1))
                    ins.then_inc(o_ready, 1)

                skewed(pe, pairs, nothing, second)

            @block.scalar
            def _(act):
                def elus(c):
                    for w in range(UNITS):
                        for f in range(HALVES):
                            i = c * UNITS + w
                            ready(act, f_ready[f], i)
                            before(act, g_made[f], i)
                            elu.scalar(act, p_f[f][:, :], f, i * HALVES + f).then_inc(parts_made[f], 1)

                def first(c, u, m):
                    if not (isinstance(c, int) and c == 0):
                        turn.scalar(act, c - 1, f_ready[HALVES - 1], UNITS)
                    norm.scalar(act, c)
                    ready(act, h_made, c)
                    act.copy(hx[u][:, :, 0:D], hd[u][:, :, :]).then_inc(h_copied, 1)

                def second(c, u, m):
                    if isinstance(c, int) and c == S.CH - 1:
                        turn.scalar(act, c, f_ready[HALVES - 1], UNITS)
                    elus(c)
                skewed(act, pairs, first, second)

            @block.vector
            def _(dve):
                chain = Chain(dve, own)

                def first(c, u, m):
                    ready(dve, x_made, c)
                    if not (isinstance(c, int) and c < 2):
                        dve.wait_ge(h_copied, c - 1)
                    norm.vector(dve, chain.link, c, hx[u][:, :, D + 2 * HEADS:HX], hd[u][:, :, :]
                                ).then_inc(h_made, 1)
                    ready(dve, h_made, c)

                def second(c, u, m):
                    ready(dve, al_ready, c, 2)
                    for q in range(2):
                        t = hx[u][:, :, D:D + 2 * HEADS].rearrange("p (a q) f -> p a q f", q=2)[:, :, q, :]
                        ins = dve.tensor_copy(t, p_al[:, q, 0:CJ // 2 * 2 * HEADS].rearrange("p (a f) -> p a f", f=2 * HEADS))
                    ins.then_inc(al_made, 1)
                    for w in range(UNITS):
                        i = c * UNITS + w
                        for f in range(HALVES):
                            ready(dve, parts_made[f], i)
                            before(dve, o_ready, i)
                            elu.vector(dve, f, g[f][:, :]).then_inc(g_made[f], 1)
                        if w > 0:
                            take(c, u, w - 1)
                    take(c, u, UNITS - 1)
                    before(dve, stored_t[u], m, 32)
                    dve.tensor_tensor(ob[u][:, :, :], tx[u][:, :, 0:D], xb[u][:, :, :], ALU.add).then_inc(out_made, 1)
                    ready(dve, out_made, c)

                def take(c, u, w):
                    ready(dve, o_ready, c * UNITS + w)
                    dve.tensor_copy(unit_tiles(tx[u], w, 0, NW2),
                                    p_o[w % 2][:, 0:TB * NW2].rearrange("p (i f) -> p i f", f=NW2)).then_inc(tx_made, 1)
                    ready(dve, tx_made, c * UNITS + w)
                skewed(dve, pairs, first, second, chain)


class Attention:

    def __init__(self, nc, c, name, heads, al_s, al_d):
        def sb(x, shape):
            return c.enter_context(nc.sbuf_tensor(f"{name}_{x}", shape, F32))

        def sem(x):
            return c.counter(f"{name}_{x}")

        H = self.heads = heads
        self.al_s, self.al_d = slice(al_s, al_s + H), slice(al_d, al_d + H)
        self.fl, self.pen = sb("fl", [H, BS]), sb("pen", [H, BS])
        self.e, self.et = sb("e", [P, TB, 2 * H]), sb("et", [H, BS])
        self.top, self.den, self.last = sb("top", [H, BS + 1]), sb("den", [H, BS]), sb("last", [H, 1])
        self.low = sb("low", [H, 2, BS])
        self.keep_new = [sb(f"keep_new{u}", [H, 2, BS]) for u in range(2)]
        self.topf, self.off, self.ce = sb("topf", [P, TB, H]), sb("off", [P, 2, TB, H]), sb("ce", [P, 2, TB, H])
        self.total = sb("total", [P, TB, H])
        self.coef = [sb(f"coef{u}", [P, 2, TB, H]) for u in range(2)]
        self.p_e = c.enter_context(nc.psum_tensor(f"{name}_p_e", [P, BS], F32))
        self.p_r = c.enter_context(nc.psum_tensor(f"{name}_p_r", [P, 2, TB, H], F32))
        (self.flags_in, self.pen_made, self.e_made, self.e_turned, self.et_made, self.low_made, self.kn_made,
         self.den_made, self.r_ready, self.off_made, self.ce_made, self.coef_made, self.init) = (
            sem(x) for x in (
                "flags_in", "pen_made", "e_made", "e_turned", "et_made", "low_made", "kn_made", "den_made",
                "r_ready", "off_made", "ce_made", "coef_made", "init"))

    def sync(self, sp, flags, g):
        before(sp, self.low_made, g)
        sp.dma_start(self.fl[:, :], flags[0, bass.ds(g * BS, BS)].partition_broadcast(self.heads)
                     ).then_inc(self.flags_in, 16)

    def turn_logits(self, pe, K, g):
        ready(pe, self.e_made, g)
        before(pe, self.et_made, g)
        pe.nop(nofuse=True)
        for k in range(TB):
            ins = pe.transpose(self.p_e[0:self.heads, k * P:(k + 1) * P], self.e[:, k, 0:self.heads], K.ident[:, :])
        ins.then_inc(self.e_turned, 1)

    def turn_results(self, pe, K, g):
        H = self.heads
        ready(pe, self.den_made, g)
        before(pe, self.coef_made, g)
        pe.nop(nofuse=True)
        for j, (tile, at) in enumerate(((self.top, 1), (self.den, 0))):
            for k in range(TB):
                ins = pe.transpose(self.p_r[:, j, k, :], tile[:, at + k * P:at + (k + 1) * P], K.ident[0:H, 0:H])
        ins.then_inc(self.r_ready, 1)

    def scalar(self, act, g, u, spread_ready):
        ready(act, self.flags_in, g, 16)
        before(act, self.low_made, g)
        act.activation(self.pen[:, :], self.fl[:, :], ACT.Copy, bias=-BIG, scale=BIG).then_inc(self.pen_made, 1)
        ready(act, self.e_turned, g)
        act.copy(self.et[:, :], self.p_e[0:self.heads, :]).then_inc(self.et_made, 1)
        ready(act, self.low_made, g)
        if not (isinstance(g, int) and g < 2):
            act.wait_ge(spread_ready, g - 1)
        act.activation(self.keep_new[u][:, :, :], self.low[:, :, :], ACT.Exp).then_inc(self.kn_made, 1)
        ready(act, self.off_made, g)
        act.activation(self.ce[:, :, :, :], self.off[:, :, :, :], ACT.Exp).then_inc(self.ce_made, 1)

    def start(self, dve):
        dve.memset(self.top[:, :], 0.0).then_inc(self.init, 1)
        dve.memset(self.last[:, :], 0.0).then_inc(self.init, 1)
        dve.wait_ge(self.init, 2)

    def vector(self, dve, link, g, u, src, dst, coef_used):
        H = self.heads
        top, low = self.top, self.low
        before(dve, self.e_turned, g)
        link(dve.tensor_tensor(self.e[:, :, 0:H], src[:, :, self.al_s], dst[:, :, self.al_d], ALU.add))
        link(dve.tensor_tensor(self.e[:, :, H:2 * H], dst[:, :, self.al_s], dst[:, :, self.al_d], ALU.add))
        dve.scalar_tensor_tensor(self.e[:, :, :], self.e[:, :, :], 0.2, self.e[:, :, :], ALU.mult, ALU.max
                                 ).then_inc(self.e_made, 1)
        ready(dve, self.e_made, g)
        ready(dve, self.et_made, g)
        ready(dve, self.pen_made, g)
        link(dve.tensor_tensor_scan(top[:, 1:BS + 1], self.pen[:, :], self.et[:, :], top[:, 0:1], ALU.add, ALU.max))
        link(dve.tensor_tensor(low[:, 0, :], top[:, 0:BS], self.pen[:, :], ALU.add))
        link(dve.tensor_tensor(low[:, 0, :], low[:, 0, :], top[:, 1:BS + 1], ALU.subtract))
        dve.tensor_tensor(low[:, 1, :], self.et[:, :], top[:, 1:BS + 1], ALU.subtract).then_inc(self.low_made, 1)
        ready(dve, self.kn_made, g)
        kn = self.keep_new[u]
        dve.tensor_tensor_scan(self.den[:, :], kn[:, 0, :], kn[:, 1, :], self.last[:, 0:1], ALU.mult, ALU.add
                               ).then_inc(self.den_made, 1)
        ready(dve, self.r_ready, g)
        link(dve.tensor_copy(top[:, 0:1], top[:, BS:BS + 1]))
        link(dve.tensor_copy(self.last[:, :], self.den[:, BS - 1:BS]))
        loop = self.e[:, :, H:2 * H]
        link(dve.tensor_tensor(self.topf[:, :, :], self.p_r[:, 0, :, :], loop, ALU.max))
        link(dve.tensor_tensor(self.off[:, 0, :, :], self.p_r[:, 0, :, :], self.topf[:, :, :], ALU.subtract))
        dve.tensor_tensor(self.off[:, 1, :, :], loop, self.topf[:, :, :], ALU.subtract).then_inc(self.off_made, 1)
        ready(dve, self.ce_made, g)
        link(dve.tensor_tensor(self.total[:, :, :], self.p_r[:, 1, :, :], self.ce[:, 0, :, :], ALU.mult))
        link(dve.scalar_tensor_tensor(self.total[:, :, :], self.total[:, :, :], 1e-16, self.ce[:, 1, :, :],
                                      ALU.add, ALU.add))
        link(dve.reciprocal(self.total[:, :, :], self.total[:, :, :]))
        if coef_used is not None and not (isinstance(g, int) and g < 2):
            dve.wait_ge(coef_used, g - 1)
        dve.tensor_tensor(self.coef[u][:, :, :, :], self.ce[:, :, :, :],
                          self.total[:, :, :].unsqueeze(1).to_broadcast([P, 2, TB, H]), ALU.mult
                          ).then_inc(self.coef_made, 1)
        ready(dve, self.coef_made, g)


def gat1_pass(nc, S, K, hx, index, flags, W, tx):
    n = "a"
    with Stage(nc) as c:
        def sb(x, shape):
            return c.enter_context(nc.sbuf_tensor(f"{n}_{x}", shape, F32))

        def two(x, shape):
            return [sb(f"{x}{u}", shape) for u in range(2)]

        def ps(x, shape):
            return c.enter_context(nc.psum_tensor(f"{n}_{x}", shape, F32))

        def sem(x):
            return c.counter(f"{n}_{x}")

        def halves(x):
            return [sem(f"{x}{f}") for f in range(HALVES)]

        rows = Rows(nc, c, n, S, index, [(hx, 1, HX), (hx, 0, HX)], (tx, 2, TX))
        att = Attention(nc, c, f"{n}_att", HEADS, D, D + HEADS)
        elu = Elu(nc, c, f"{n}_elu", W)
        hs, hd = two("hs", [D, BS]), two("hd", [D, BS])
        xrow = two("xrow", [P, TB, D])
        new, val = sb("new", [P, BS]), sb("val", [P, BS])
        state = [sb(f"state{f}", [P, BS]) for f in range(HALVES)]
        last = [sb(f"last{f}", [P, 1]) for f in range(HALVES)]
        edges, loop = ([sb(f"{x}{f}", [P, TB, P]) for f in range(HALVES)] for x in ("edges", "loop"))
        g2 = [sb(f"g{f}", [P, BS]) for f in range(HALVES)]
        p_h, p_k, p_n, p_v, p_s, p_d = (ps(x, [P, BS]) for x in ("p_h", "p_k", "p_n", "p_v", "p_s", "p_d"))
        h_turned, h_copied, hx_copied, o_ready, rows_made, own, init = (sem(x) for x in (
            "h_turned", "h_copied", "hx_copied", "o_ready", "rows_made", "own", "init"))
        spread_ready, new_copied, val_made, state_made, s_ready, edges_made, loop_made, sum_ready, parts_made, \
            g_made = (halves(x) for x in (
                "spread_ready", "new_copied", "val_made", "state_made", "s_ready", "edges_made", "loop_made",
                "sum_ready", "parts_made", "g_made"))

        def heads(tile):
            return tile.rearrange("p (k h c) -> p k h c", k=TB, c=HC)

        def of_half(coef, f):
            nh = HEADS // HALVES
            return coef[:, :, f * nh:(f + 1) * nh].unsqueeze(3).to_broadcast([P, TB, nh, HC])

        with nc.Block() as block:
            @block.gpsimd
            def _(pool):
                rows.run(pool, [(h_turned, 2), (att.e_made, 1), (hx_copied, 1)], rows_made)

            @block.sync
            def _(sp):
                turns(sp, S.B, lambda g: att.sync(sp, flags, g))

            @block.tensor
            def _(pe):
                def first(g, u, m):
                    for e in range(2):
                        if e == 0:
                            before(pe, h_copied, g, 2)
                            for k in range(TB):
                                rows.wait_gathered(pe, g, k)
                        else:
                            pe.wait_ge(h_copied, g * 2 + 1)
                        pe.nop(nofuse=True)
                        for k in range(TB):
                            ins = pe.transpose(p_h[0:D, k * P:(k + 1) * P], rows.got[e][:, k, 0:D], K.ident[:, :])
                        ins.then_inc(h_turned, 1)
                    att.turn_logits(pe, K, g)
                    att.turn_results(pe, K, g)

                def spread(g, u, f):
                    if f == 0:
                        before(pe, state_made[HALVES - 1], g)
                    else:
                        ready(pe, state_made[f - 1], g)
                    pe.nop(nofuse=True)
                    for j, bank in ((1, p_n), (0, p_k)):
                        pe.matmul(bank[:, :], W.spread[:, f, :], att.keep_new[u][:, j, :], start=True, stop=True)
                    pe.matmul(p_v[:, :], W.conv1[0:D, f * P:(f + 1) * P], hs[u][:, :], start=True, stop=True
                              ).then_inc(spread_ready[f], 1)

                def by_slot(g, u, f):
                    if f == 0:
                        before(pe, rows_made, g)
                        before(pe, edges_made[HALVES - 1], g)
                    else:
                        ready(pe, loop_made[f - 1], g)
                        ready(pe, edges_made[f - 1], g)
                    pe.nop(nofuse=True)
                    for k in range(TB):
                        pe.matmul(p_d[:, k * P:(k + 1) * P], hd[u][:, k * P:(k + 1) * P],
                                  W.conv1[0:D, f * P:(f + 1) * P], start=True, stop=True)
                    ready(pe, state_made[f], g)
                    pe.nop(nofuse=True)
                    for k in range(TB):
                        ins = pe.transpose(p_s[:, k * P:(k + 1) * P], state[f][:, k * P:(k + 1) * P], K.ident[:, :])
                    ins.then_inc(s_ready[f], 1)

                def by_feature(g, u, f):
                    ready(pe, loop_made[f], g)
                    if f > 0:
                        ready(pe, parts_made[f - 1], g)
                    pe.nop(nofuse=True)
                    for k in range(TB):
                        at = slice(k * P, (k + 1) * P)
                        pe.matmul(p_h[:, at], edges[f][:, k, :], K.ident[:, :], start=True, stop=False)
                        ins = pe.matmul(p_h[:, at], loop[f][:, k, :], K.ident[:, :], start=False, stop=True)
                    ins.then_inc(sum_ready[f], 1)

                def second(g, u, m):
                    spread(g, u, 0)
                    by_slot(g, u, 0)
                    spread(g, u, 1)
                    if isinstance(g, int) and g == S.B - 1:
                        ready(pe, h_copied, g, 2)
                    else:
                        ready(pe, h_copied, g + 1, 2)
                    by_feature(g, u, 0)
                    by_slot(g, u, 1)
                    by_feature(g, u, 1)
                    for f in range(HALVES):
                        ready(pe, g_made[f], g)
                    for k in range(TB):
                        for f in range(HALVES):
                            ins = pe.matmul(p_d[:, k * NW2:(k + 1) * NW2], g2[f][:, k * P:(k + 1) * P],
                                            W.conv2[:, f, :], start=(f == 0), stop=(f == HALVES - 1))
                    ins.then_inc(o_ready, 1)

                skewed(pe, S.B // 2, first, second)

            @block.scalar
            def _(act):
                def first(g, u, m):
                    for e, tile in enumerate((hs, hd)):
                        act.wait_ge(h_turned, g * 2 + e + 1)
                        if not (isinstance(g, int) and g < 2):
                            act.wait_ge(o_ready, g - 1)
                        act.copy(tile[u][:, :], p_h[0:D, :]).then_inc(h_copied, 1)
                    for k in range(TB):
                        rows.wait_gathered(act, g, k)
                    if not (isinstance(g, int) and g < 2):
                        act.wait_ge(rows_made, g - 1)
                    act.copy(xrow[u][:, :, :], rows.got[1][:, :, D + 2 * HEADS:HX]).then_inc(hx_copied, 1)
                    att.scalar(act, g, u, spread_ready[HALVES - 1])

                def second(g, u, m):
                    for f in range(HALVES):
                        ready(act, spread_ready[f], g)
                        if f == 0:
                            before(act, val_made[HALVES - 1], g)
                        else:
                            ready(act, val_made[f - 1], g)
                        act.copy(new[:, :], p_n[:, :]).then_inc(new_copied[f], 1)
                    for f in range(HALVES):
                        ready(act, sum_ready[f], g)
                        before(act, g_made[f], g)
                        elu.scalar(act, p_h[:, :], f, g * HALVES + f).then_inc(parts_made[f], 1)

                skewed(act, S.B // 2, first, second)

            @block.vector
            def _(dve):
                chain = Chain(dve, own)
                link = chain.link
                att.start(dve)
                for f in range(HALVES):
                    dve.memset(last[f][:, :], 0.0).then_inc(init, 1)
                dve.wait_ge(init, HALVES)

                def first(g, u, m):
                    for k in range(TB):
                        rows.wait_gathered(dve, g, k)
                    att.vector(dve, link, g, u, rows.got[0], rows.got[1], None)

                def scan(g, u, f):
                    ready(dve, new_copied[f], g)
                    dve.tensor_tensor(val[:, :], new[:, :], p_v[:, :], ALU.mult).then_inc(val_made[f], 1)
                    ready(dve, val_made[f], g)
                    before(dve, s_ready[f], g)
                    dve.tensor_tensor_scan(state[f][:, :], p_k[:, :], val[:, :], last[f][:, 0:1], ALU.mult, ALU.add
                                           ).then_inc(state_made[f], 1)
                    ready(dve, state_made[f], g)
                    link(dve.tensor_copy(last[f][:, :], state[f][:, BS - 1:BS]))

                def merge(g, u, f):
                    ready(dve, s_ready[f], g)
                    before(dve, sum_ready[f], g)
                    dve.tensor_tensor(edges[f][:, :, :].rearrange("p k (h c) -> p k h c", c=HC), heads(p_s[:, :]),
                                      of_half(att.coef[u][:, 0], f), ALU.mult).then_inc(edges_made[f], 1)
                    dve.tensor_tensor(loop[f][:, :, :].rearrange("p k (h c) -> p k h c", c=HC), heads(p_d[:, :]),
                                      of_half(att.coef[u][:, 1], f), ALU.mult).then_inc(loop_made[f], 1)

                def second(g, u, m):
                    scan(g, u, 0)
                    scan(g, u, 1)
                    merge(g, u, 0)
                    merge(g, u, 1)
                    for f in range(HALVES):
                        ready(dve, parts_made[f], g)
                        before(dve, o_ready, g)
                        elu.vector(dve, f, g2[f][:, :]).then_inc(g_made[f], 1)
                    ready(dve, hx_copied, g)
                    rows.wait_scattered(dve, g)
                    link(dve.tensor_copy(rows.rows[:, :, NW2:TX], xrow[u][:, :, :]))
                    ready(dve, o_ready, g)
                    dve.tensor_copy(rows.rows[:, :, 0:NW2], p_d[:, 0:TB * NW2].rearrange("p (k f) -> p k f", f=NW2)
                                    ).then_inc(rows_made, 1)
                    ready(dve, rows_made, g)

                skewed(dve, S.B // 2, first, second, chain)


def gat2_pass(nc, S, K, tx, index, flags, W, out):
    n = "b"
    with Stage(nc) as c:
        def sb(x, shape):
            return c.enter_context(nc.sbuf_tensor(f"{n}_{x}", shape, F32))

        def two(x, shape):
            return [sb(f"{x}{u}", shape) for u in range(2)]

        def ps(x, shape):
            return c.enter_context(nc.psum_tensor(f"{n}_{x}", shape, F32))

        def sem(x):
            return c.counter(f"{n}_{x}")

        rows = Rows(nc, c, n, S, index, [(tx, 1, TX), (tx, 0, TX)], (out, 2, D))
        att = Attention(nc, c, f"{n}_att", 1, D, D + 1)
        hs, rest = two("hs", [D, BS]), two("rest", [P, TB, D])
        own_part = sb("own_part", [P, TB, D])
        val, state, last = sb("val", [D, BS]), sb("state", [D, BS]), sb("last", [D, 1])
        p_h, p_k, p_n, p_s = ps("p_h", [P, BS]), ps("p_k", [P, BS]), ps("p_n", [P, BS]), ps("p_s", [P, TB, D])
        h_turned, h_copied, rest_made, spread_ready, val_made, state_made, s_ready, rows_made, own, init = (
            sem(x) for x in ("h_turned", "h_copied", "rest_made", "spread_ready", "val_made", "state_made",
                             "s_ready", "rows_made", "own", "init"))

        def over(coef):
            return coef[:, :, 0:1].to_broadcast([P, TB, D])

        with nc.Block() as block:
            @block.gpsimd
            def _(pool):
                rows.run(pool, [(h_turned, 1), (rest_made, 1)], rows_made)

            @block.sync
            def _(sp):
                turns(sp, S.B, lambda g: att.sync(sp, flags, g))

            @block.tensor
            def _(pe):
                def first(g, u, m):
                    before(pe, h_copied, g)
                    for k in range(TB):
                        rows.wait_gathered(pe, g, k)
                    pe.nop(nofuse=True)
                    for k in range(TB):
                        ins = pe.transpose(p_h[0:D, k * P:(k + 1) * P], rows.got[0][:, k, 0:D], K.ident[:, :])
                    ins.then_inc(h_turned, 1)
                    att.turn_logits(pe, K, g)
                    att.turn_results(pe, K, g)

                def second(g, u, m):
                    before(pe, state_made, g)
                    pe.nop(nofuse=True)
                    for j, bank in ((1, p_n), (0, p_k)):
                        ins = pe.matmul(bank[0:D, :], K.ones[0:1, 0:D], att.keep_new[u][:, j, :], start=True, stop=True)
                    ins.then_inc(spread_ready, 1)
                    ready(pe, state_made, g)
                    before(pe, rows_made, g)
                    pe.nop(nofuse=True)
                    for k in range(TB):
                        ins = pe.transpose(p_s[:, k, :], state[:, k * P:(k + 1) * P], K.ident[0:D, 0:D])
                    ins.then_inc(s_ready, 1)

                skewed(pe, S.B // 2, first, second)

            @block.scalar
            def _(act):
                def first(g, u, m):
                    ready(act, h_turned, g)
                    if not (isinstance(g, int) and g < 2):
                        act.wait_ge(val_made, g - 1)
                    act.copy(hs[u][:, :], p_h[0:D, :]).then_inc(h_copied, 1)
                    att.scalar(act, g, u, spread_ready)

                skewed(act, S.B // 2, first, nothing)

            @block.vector
            def _(dve):
                chain = Chain(dve, own)
                link = chain.link
                att.start(dve)
                dve.memset(last[:, :], 0.0).then_inc(init, 1)
                dve.wait_ge(init, 1)

                def first(g, u, m):
                    for k in range(TB):
                        rows.wait_gathered(dve, g, k)
                    att.vector(dve, link, g, u, rows.got[0], rows.got[1], None)
                    dst = rows.got[1]
                    link(dve.tensor_tensor(rest[u][:, :, :], dst[:, :, NW2:TX],
                                           W.bias2[:, :].unsqueeze(1).to_broadcast([P, TB, D]), ALU.add))
                    link(dve.tensor_tensor(own_part[:, :, :], dst[:, :, 0:D], over(att.coef[u][:, 1]), ALU.mult))
                    dve.tensor_tensor(rest[u][:, :, :], rest[u][:, :, :], own_part[:, :, :], ALU.add
                                      ).then_inc(rest_made, 1)
                    ready(dve, rest_made, g)

                def second(g, u, m):
                    ready(dve, spread_ready, g)
                    ready(dve, h_copied, g)
                    dve.tensor_tensor(val[:, :], p_n[0:D, :], hs[u][:, :], ALU.mult).then_inc(val_made, 1)
                    ready(dve, val_made, g)
                    before(dve, s_ready, g)
                    dve.tensor_tensor_scan(state[:, :], p_k[0:D, :], val[:, :], last[:, 0:1], ALU.mult, ALU.add
                                           ).then_inc(state_made, 1)
                    ready(dve, state_made, g)
                    link(dve.tensor_copy(last[:, :], state[:, BS - 1:BS]))
                    ready(dve, s_ready, g)
                    rows.wait_scattered(dve, g)
                    link(dve.tensor_tensor(rows.rows[:, :, :], p_s[:, :, :], over(att.coef[u][:, 0]), ALU.mult))
                    dve.tensor_tensor(rows.rows[:, :, :], rows.rows[:, :, :], rest[u][:, :, :], ALU.add
                                      ).then_inc(rows_made, 1)
                    ready(dve, rows_made, g)

                skewed(dve, S.B // 2, first, second, chain)


def zero_fill(S, K, table, width, filled):
    step = 2 * CJ * width // TB
    flat = table.rearrange("(p g a) w -> p g (a w)", p=P, a=2 * CJ)
    groups = S.NJ // (2 * CJ)

    def run(eng):
        def body(i):
            eng.dma_start(flat[:, bass.ds(i, 1), :].rearrange("p a (r s) -> p (a r) s", s=step),
                          K.zeros[:, 0:step].unsqueeze(1).to_broadcast([P, TB, step])).then_inc(filled, 16)
        turns(eng, groups, body)
        eng.wait_ge(filled, 16 * groups)
    return run


def rows_by_src(nc, S, rows_a, rows_out):
    n = "by_src"
    with Stage(nc) as c:
        def sb(x, shape):
            return c.enter_context(nc.sbuf_tensor(f"{n}_{x}", shape, I32))

        cur, out, slot = sb("cur", [S.B, BS, 4]), sb("out", [S.B, BS, 4]), sb("slot", [S.B, BS])
        loaded, made, stored, zeroed = (c.counter(f"{n}_{x}") for x in (
            "loaded", "made", "stored", "zeroed"))
        with nc.Block() as block:
            @block.sync
            def _(sp):
                sp.dma_start(cur[:, :, :], rows_a[1:S.EP + 1, :].rearrange("(b s) f -> b s f", s=BS)
                             ).then_inc(loaded, 16)
                sp.wait_ge(made, 2)
                sp.dma_start(rows_out.rearrange("(b s) f -> b s f", s=BS), out[:, :, :]).then_inc(stored, 16)
                sp.wait_ge(stored, 16)

            @block.gpsimd
            def _(pool):
                pool.iota(slot[:, :], [[1, BS]], base=0, channel_multiplier=BS).then_inc(zeroed, 1)

            @block.vector
            def _(dve):
                dve.memset(out[:, :, :], 0).then_inc(zeroed, 1)
                dve.wait_ge(zeroed, 2)
                dve.tensor_copy(out[:, :, 2], slot[:, :]).then_inc(made, 1)
                dve.wait_ge(loaded, 16)
                dve.tensor_copy(out[:, :, 0], cur[:, :, 1]).then_inc(made, 1)


def gnn_preln_d4(nc, n, e, inp, out):
    S = Shapes(n, e)

    def dram(name, shape, dt=F32):
        return nc.dram_tensor(name, shape, dt).ap()

    with Stage(nc) as c:
        def sb(x, shape, dt=F32):
            return c.enter_context(nc.sbuf_tensor(x, shape, dt))

        def wt(x, shape):
            return sb(f"weights_{x}", shape)

        class W:
            base_w, base_b = wt("base_w", [P, D]), wt("base_b", [P, D])
            gcn_w, gcn_b = wt("gcn_w", [P, D]), wt("gcn_b", [P, D])
            node_w, node_b = wt("node_w", [P, EW]), wt("node_b", [P, D])
            msg_b, edge_w, sum_w = wt("msg_b", [P, 2 * MSG]), wt("edge_w", [ED, MSG]), wt("sum_w", [MSG, D])
            conv1, al_w, conv2 = wt("conv1", [P, GF]), wt("al_w", [P, 2 * HEADS]), wt("conv2", [P, HALVES, NW2])
            bias1, nbias1, bias2 = wt("bias1", [P, HALVES]), wt("nbias1", [P, HALVES]), wt("bias2", [P, D])
            spread = wt("spread", [HEADS, HALVES, P])

        K = make_constants(nc, c)
        s2d, d2s = Side(nc, c, "s2d"), Side(nc, c, "d2s")
        pna_weights(nc, S, K, s2d, 0, inp, W)
        pna_weights(nc, S, K, d2s, 1, inp, W)
        gat_weights(nc, S, K, W, inp)

        mid_a, rows_a, mid_b, rows_b = (dram(x, [S.EP + 2, 4], I32) for x in ("mid_a", "rows_a", "mid_b", "rows_b"))
        src_rows = dram("src_rows", [S.EP, 4], I32)
        flags_a, flags_b = dram("flags_a", [2, S.EP]), dram("flags_b", [2, S.EP])
        agg_a, agg_b = dram("agg_a", [S.NP, DAW]), dram("agg_b", [S.NP, DAW])
        gcn_delta, sum_delta = dram("gcn_delta", [S.NP, D]), dram("sum_delta", [S.NP, D])
        filled = [c.counter(f"filled{j}") for j in range(4)]
        index_a, index_b = sb("index_a", [P, S.B, 4 * TB], I32), sb("index_b", [P, S.B, 2 * TB], I32)
        counts_a, counts_b = (Counts(*(sb(f"counts_{o}{j}", [P, S.B, TB])[:, :, :] for j in range(k)))
                              for o, k in (("a", 4), ("b", 3)))
        sort_pass(nc, S, K, "sort_a0", inp["edge_rows"], mid_a, 0, S.LO, zero_fill(S, K, agg_a, DAW, filled[0]))
        sort_pass(nc, S, K, "sort_a1", mid_a[1:S.EP + 1, :], rows_a, RADIX_BITS, S.HI,
                  zero_fill(S, K, agg_b, DAW, filled[1]))
        prepare_order(nc, S, K, "order_a", rows_a, [0, 1, "end", 2], index_a, flags_a, counts_a)
        rows_by_src(nc, S, rows_a, src_rows)
        sort_pass(nc, S, K, "sort_b0", src_rows, mid_b, 0, S.LO, zero_fill(S, K, gcn_delta, D, filled[2]))
        sort_pass(nc, S, K, "sort_b1", mid_b[1:S.EP + 1, :], rows_b, RADIX_BITS, S.HI,
                  zero_fill(S, K, sum_delta, D, filled[3]))
        prepare_order(nc, S, K, "order_b", rows_b, [2, "end"], index_b, flags_b, counts_b)

        h0, msgs = dram("h0", [S.NP, D]), dram("msgs", [S.EP, D])
        norm_pass(nc, S, K, inp["x"], h0)
        pna_pass(nc, S, K, s2d, h0, index_a, [0, 1], 2, flags_a, counts_a, agg_a, (d2s, msgs))
        pna_pass(nc, S, K, d2s, msgs, index_b, [0], 1, flags_b, counts_b, agg_b)

        base1, scaled1 = dram("base1", [S.NP, D]), dram("scaled1", [S.NP, D])
        pna_out_pass(nc, S, K, inp["x"], h0, agg_a, agg_b, W, base1, scaled1)
        sum_pass(nc, S, K, "gcn", scaled1, D, index_a, 1, 2, flags_a, W.gcn_w[0:D, :], gcn_delta, counts_a.dinv)

        base2, ends, factors = dram("base2", [S.NP, D]), dram("ends", [S.NP, 2 * MSG]), dram("factors", [S.EP, MSG])
        gcn_out_pass(nc, S, K, base1, gcn_delta, W, base2, ends)
        message_pass(nc, S, K, ends, inp["edge_attr"], index_a, W.edge_w[:, :], factors)
        sum_pass(nc, S, K, "fac", factors, MSG, index_b, 0, 1, flags_b, W.sum_w[:, :], sum_delta)

        hx, tx = dram("hx", [S.NP, HX]), dram("tx", [S.NP, TX])
        sums_out_pass(nc, S, K, base2, sum_delta, W, hx, tx, out)
        gat1_pass(nc, S, K, hx, index_a, flags_a, W, tx)
        gat2_pass(nc, S, K, tx, index_a, flags_a, W, out)


def laid_out(inputs):
    a = {k: np.asarray(v) for k, v in inputs.items()}
    n, e = a["x"].shape[0], a["src"].shape[0]
    S = Shapes(n, e)
    T, FI = 4, D // 4

    def padded(v, rows):
        return np.concatenate([v, np.zeros((rows - v.shape[0], v.shape[1]), v.dtype)])

    edges = np.zeros((S.EP, 4), np.int32)
    edges[:, 0:2], edges[:, 2] = n, np.arange(S.EP)
    edges[:e, 0], edges[:e, 1] = a["dst"], a["src"]
    r = {"edge_rows": edges, "x": padded(a["x"], S.NP), "edge_attr": padded(a["edge_attr_32"], S.EP)}

    for side, swap in (("s2d", 0), ("d2s", 1)):
        def w(k):
            return a[f"L0_gnn_{k}_{side}"]
        pre = np.zeros((P, D), np.float32)
        post = []
        for t in range(T):
            for h in range(2):
                at = (h ^ swap) * D + t * FI
                pre[at:at + FI, t * FI:(t + 1) * FI] = w("pre_W")[t, h * FI:(h + 1) * FI]
        for j in [0, 0] + [1 + 4 * s + agg for s in range(3) for agg in (0, 3, 2, 1)]:
            m = np.zeros((D, D), np.float32)
            for t in range(T):
                m[t * FI:(t + 1) * FI, t * FI:(t + 1) * FI] = w("post_W")[t, j * FI:(j + 1) * FI].T
            post.append(m)
        bias = w("pre_b").reshape(D, 1)
        r.update({f"pre_{side}": np.concatenate([pre, pre], 1), f"preb_{side}": np.concatenate([bias, bias]),
                  f"post_{side}": np.concatenate(post, 1), f"postb_{side}": w("post_b").reshape(D, 1),
                  f"lin_{side}": w("lin_W"), f"linb_{side}": w("lin_b")})
    r.update({"alpha": a["L0_gnn_alpha"], "self_w": a["L0_gnn_lin_self_W"], "self_b": a["L0_gnn_lin_self_b"]})

    gcn = a["L1_gnn_W"].T
    fe, fh = a["L2_gnn_fe_w"].T, a["L2_gnn_fh_w"].T
    node = np.concatenate([fh[0:D], fe[0:D], fe[D:2 * D]], 1)
    r.update({"gcn_w": np.concatenate([gcn, gcn]), "gcn_b": a["L1_gnn_b"],
              "node_w": np.concatenate([node, node]), "node_b": a["L2_gnn_fh_b"], "msg_b": a["L2_gnn_fe_b"],
              "edge_w": fe[2 * D:2 * D + ED], "sum_w": fh[D:D + MSG]})

    w1, w2 = a["L3_gnn_W1"], a["L3_gnn_W2"]
    a1 = np.zeros((GF, 2 * HEADS), np.float32)
    for h in range(HEADS):
        a1[h * HC:(h + 1) * HC, h] = a["L3_gnn_a1_src"][h]
        a1[h * HC:(h + 1) * HC, HEADS + h] = a["L3_gnn_a1_dst"][h]
    r.update({"w1": np.concatenate([w1, w1]), "w1t": np.concatenate([w1.T, w1.T], 1), "a1": a1, "w2": w2, "w2t": w2.T,
              "a2": np.concatenate([a["L3_gnn_a2_src"], a["L3_gnn_a2_dst"]]).T,
              "b1": a["L3_gnn_b1"], "b2": a["L3_gnn_b2"]})
    return n, e, {k: np.ascontiguousarray(v) for k, v in r.items()}


def kernel(**inputs):
    import concourse.bacc as _bacc
    from concourse import mybir as _mybir
    from concourse.bass_utils import run_bass_kernel_spmd as _run

    n, e, arrays = laid_out(inputs)
    nc = _bacc.Bacc("TRN2", target_bir_lowering=False, num_devices=1)
    aps = {k: nc.dram_tensor(f"in_{k}", v.shape, _mybir.dt.from_np(v.dtype), kind="ExternalInput").ap()
           for k, v in arrays.items()}
    out = nc.dram_tensor("out_nodes", [Shapes(n, e).NP, D], F32, kind="ExternalOutput").ap()
    gnn_preln_d4(nc, n, e, aps, out)
    r = _run(nc, [{f"in_{k}": v for k, v in arrays.items()}], core_ids=[0])
    return r.results[0]["out_nodes"][:n]
```

```python
from contextlib import ExitStack

import numpy as np

import concourse.bass as bass
from concourse import mybir

P = 128
D = 64
TB = 4
BS = TB * P
CJ = 16
RADIX_BITS = 9
MSG = 16
ED = 32
HEADS, HC = 8, 32
GF = HEADS * HC
HALVES = GF // P
HX = D + 2 * HEADS + D
TX = D + 2 + D
DAW = D + 1
ZW = 2 * CJ * DAW // TB
EPS = 1e-5
BIG = 1e30
SKIP = float(1 << 20)
AVG_LOG = float(np.log(17.0))

F32 = mybir.dt.float32
F16 = mybir.dt.float16
I32 = mybir.dt.int32
ALU = mybir.AluOpType
ACT = mybir.ActivationFunctionType
AX = mybir.AxisListType


class Stage(ExitStack):

    def __init__(self, nc):
        super().__init__()
        self.nc, self.counters = nc, []

    def counter(self, name):
        self.counters.append(self.nc.alloc_semaphore(name=name))
        return self.counters[-1]

    def __exit__(self, *error):
        if self.counters and error[0] is None:
            self.nc.clear_and_free_semaphores(self.counters)
            self.nc.all_engine_barrier()
        return super().__exit__(*error)


def after(eng, sem, value):
    if not isinstance(value, int) or value > 0:
        eng.wait_ge(sem, value)


def ready(eng, sem, i, per=1):
    eng.wait_ge(sem, (i + 1) * per)


def before(eng, sem, i, per=1):
    after(eng, sem, i * per)


def two_back(eng, sem, i, u):
    if not (isinstance(i, int) and i == 0):
        eng.wait_ge(sem, i * 2 + u - 1)


class Chain:

    def __init__(self, eng, sem):
        self.eng, self.sem, self.done, self.n, self.peeled, self.base = eng, sem, 0, 0, 0, 0

    def turn(self, i):
        self.done += self.n
        if isinstance(i, int):
            self.base, self.peeled = self.done, i + 1
        else:
            self.base = i * self.n + (self.done - self.peeled * self.n)
            self.per = self.n
        self.n = 0

    def end(self, count):
        if count > self.peeled:
            self.base = self.done + (count - self.peeled) * self.per
            self.done, self.n = self.base, 0

    def link(self, ins):
        self.n += 1
        ins.then_inc(self.sem, 1)
        self.eng.wait_ge(self.sem, self.base + self.n)


def nothing(c, u, m):
    pass


def skewed(eng, pairs, first, second, chain=None):
    def body(i):
        if chain:
            chain.turn(i)
        first(i * 2, 0, i)
        if not (isinstance(i, int) and i == 0):
            second(i * 2 - 1, 1, i - 1)
        first(i * 2 + 1, 1, i)
        second(i * 2, 0, i)

    turns(eng, pairs, body, peeled=2)
    if chain:
        chain.end(pairs)
    second(pairs * 2 - 1, 1, pairs - 1)


def interleaved(eng, pairs, step, chain=None):
    def body(i):
        if chain:
            chain.turn(i)
        step((i * 2, 0, i), None if isinstance(i, int) and i == 0 else (i * 2 - 1, 1, i - 1))
        step((i * 2 + 1, 1, i), (i * 2, 0, i))

    turns(eng, pairs, body, peeled=2)
    if chain:
        chain.end(pairs)
    step(None, (pairs * 2 - 1, 1, pairs - 1))


def on(block, part, *more):
    if block:
        part(*block, *more)


def turns(eng, count, body, peeled=1):
    for i in range(min(peeled, count)):
        body(i)
    if count > peeled:
        with eng.Fori(peeled, count) as i:
            body(i)


class Shapes:
    def __init__(self, n, e):
        self.N, self.E = n, e
        self.NJ = -(-(n + 1) // (P * 2 * CJ)) * 2 * CJ
        self.NP = P * self.NJ
        self.CH = self.NJ // CJ
        self.B = 2 * -(-e // (2 * BS))
        self.EP = self.B * BS
        self.T = self.B * TB
        self.LO = 1 << RADIX_BITS
        self.HI = max(16, ((n >> RADIX_BITS) + 16) // 16 * 16)
        assert self.B <= P and self.HI <= self.LO


def setup_constants(nc, K):
    with Stage(nc) as c:
        made = c.counter("consts_made")
        cleared = c.counter("consts_cleared")
        with nc.Block() as block:
            @block.gpsimd
            def _(pool):
                pool.memset(K.ident[:, :], 0.0).then_inc(cleared, 1)
                pool.memset(K.upper[:, :], 0.0).then_inc(cleared, 1)
                pool.memset(K.lower[:, :], 1.0).then_inc(cleared, 1)
                pool.memset(K.ones16[:, :], 1.0).then_inc(made, 1)
                pool.memset(K.ones[:, :], 1.0).then_inc(made, 1)
                pool.memset(K.zeros[:, :], 0.0).then_inc(made, 1)
                pool.iota(K.bins[:, :], [[1, K.bins.shape[1]]], base=0, channel_multiplier=0,
                          allow_small_or_imprecise_dtypes=True).then_inc(made, 1)
                pool.wait_ge(cleared, 3)
                pool.affine_select(out=K.ident[:, :], in_=K.ident[:, :], compare_op=ALU.not_equal, fill=1.0,
                                   base=0, pattern=[[-1, P]], channel_multiplier=1).then_inc(made, 1)
                pool.affine_select(out=K.upper[:, :], in_=K.upper[:, :], compare_op=ALU.is_ge, fill=1.0,
                                   base=0, pattern=[[-1, P]], channel_multiplier=1).then_inc(made, 1)
                pool.affine_select(out=K.lower[:, :], in_=K.lower[:, :], compare_op=ALU.is_ge, fill=0.0,
                                   base=0, pattern=[[-1, P]], channel_multiplier=1).then_inc(made, 1)
                pool.wait_ge(made, 7)


def sort_pass(nc, S, K, name, rows_in, rows_out, shift, bins, aside=None):
    half = S.B // 2
    with Stage(nc) as c:
        def sb(n, shape, dt):
            return c.enter_context(nc.sbuf_tensor(f"{name}_{n}", shape, dt))

        def ps(n, shape):
            return c.enter_context(nc.psum_tensor(f"{name}_{n}", shape, F32))

        def sem(n):
            return c.counter(f"{name}_{n}")

        rows = [[sb(f"rows{w}{u}", [P, TB, 4], I32) for u in range(2)] for w in range(2)]
        digit = [sb(f"digit{u}", [P, TB], I32) for u in range(2)]
        digitf = [sb(f"digitf{u}", [P, TB], F32) for u in range(2)]
        hot = [sb(f"hot{u}", [P, TB, bins], F16) for u in range(2)]
        pick = sb("pick", [P, bins], F32)
        rankf = [sb(f"rankf{u}", [P, TB], F32) for u in range(2)]
        rank = [sb(f"rank{u}", [P, TB], I32) for u in range(2)]
        start = sb("start", [P, bins], F32)
        edge = sb("edge", [2, 4], I32)
        hist = ps("hist", [P, 512])
        seen = [ps(f"seen{b}", [P, 512]) for b in range(2)]

        loaded = [[sem(f"loaded{w}{u}") for u in range(2)] for w in range(2)]
        hist_hot = sem("hist_hot")
        hist_added = sem("hist_added")
        start_made = sem("start_made")
        seeded = sem("seeded")
        hot_made = sem("hot_made")
        seen_ready = sem("seen_ready")
        rank_read = sem("rank_read")
        hot_used = sem("hot_used")
        rank_made = sem("rank_made")
        scattered = [sem(f"scattered{u}") for u in range(2)]
        chain = sem("chain")
        edge_made = sem("edge_made")
        edge_out = sem("edge_out")

        blocks_in = rows_in.rearrange("(b k p) f -> b p k f", k=TB, p=P)

        with nc.Block() as block:
            @block.scalar
            def _(act):
                if aside:
                    aside(act)

            @block.sync
            def _(sp):
                sp.wait_ge(edge_made, 1)
                sp.dma_start(rows_out[0:1, :], edge[0:1, :]).then_inc(edge_out, 16)
                sp.dma_start(rows_out[S.EP + 1:S.EP + 2, :], edge[1:2, :]).then_inc(edge_out, 16)

                def load(w):
                    def body(i):
                        for u in range(2):
                            if w == 0:
                                two_back(sp, hist_hot, i, u)
                            else:
                                before(sp, scattered[u], i, 16 * TB)
                            b = i * 2 + u
                            sp.dma_start(rows[w][u][:, :, :],
                                         blocks_in[bass.ds(b, 1)].rearrange("a p k f -> (a p) k f")
                                         ).then_inc(loaded[w][u], 16)
                    return body

                turns(sp, half, load(0))
                turns(sp, half, load(1))
                sp.wait_ge(edge_out, 32)

            @block.gpsimd
            def _(pool):
                pool.memset(edge[:, :], -1).then_inc(edge_made, 1)

                def body(i):
                    for u in range(2):
                        pool.wait_ge(rank_made, i * 2 + u + 1)
                        pool.nop(nofuse=True)
                        for k in range(TB):
                            pool.indirect_dma_start(
                                rows_out[:, :], bass.IndirectOffsetOnAxis(rank[u][:, k:k + 1], 0),
                                rows[1][u][:, k, :], None).then_inc(scattered[u], 16)

                turns(pool, half, body)
                for u in range(2):
                    pool.wait_ge(scattered[u], 16 * TB * half)

            def digits(dve, link, i, w, u):
                ready(dve, loaded[w][u], i, 16)
                link(dve.tensor_scalar(digit[u][:, :], rows[w][u][:, :, 0], shift, (1 << RADIX_BITS) - 1,
                                       ALU.arith_shift_right, ALU.bitwise_and))
                link(dve.tensor_copy(digitf[u][:, :], digit[u][:, :]))
                for k in range(TB):
                    ins = dve.tensor_scalar(hot[u][:, k, :], K.bins[:, 0:bins], digitf[u][:, k:k + 1], None,
                                            ALU.is_equal)
                return ins

            @block.vector
            def _(dve):
                own = Chain(dve, chain)

                def count(i):
                    own.turn(i)
                    for u in range(2):
                        two_back(dve, hist_added, i, u)
                        digits(dve, own.link, i, 0, u).then_inc(hist_hot, 1)

                turns(dve, half, count)
                own.end(half)
                dve.wait_ge(hist_added, 2 * half)
                dve.wait_ge(hist_hot, 2 * half)
                own.link(dve.tensor_tensor_scan(start[:, :], hist[:, 0:bins], K.zeros[:, 0:bins], 1.0, ALU.add,
                                                ALU.add))
                dve.tensor_tensor(start[:, :], start[:, :], hist[:, 0:bins], ALU.subtract).then_inc(start_made, 1)

                own2 = Chain(dve, hot_made)

                def place(i):
                    own2.turn(i)
                    for u in range(2):
                        two_back(dve, hot_used, i, u)
                        before(dve, scattered[u], i, 16 * TB)
                        own2.link(digits(dve, own2.link, i, 1, u))
                        for k in range(TB):
                            dve.wait_ge(seen_ready, (i * 2 + u) * TB + k + 1)
                            dve.tensor_tensor_reduce(pick[:, :], hot[u][:, k, :], seen[k % 2][:, 0:bins], 1.0,
                                                     0.0, ALU.mult, ALU.add, rankf[u][:, k:k + 1]
                                                     ).then_inc(rank_read, 1)
                            dve.wait_ge(rank_read, (i * 2 + u) * TB + k + 1)
                        dve.tensor_copy(rank[u][:, :], rankf[u][:, :]).then_inc(rank_made, 1)
                        dve.wait_ge(rank_made, i * 2 + u + 1)

                turns(dve, half, place)

            @block.tensor
            def _(pe):
                def count(i):
                    for u in range(2):
                        ready(pe, hist_hot, i * 2 + u)
                        for k in range(TB):
                            first = isinstance(i, int) and i == 0 and u == 0 and k == 0
                            ins = pe.matmul(hist[:, 0:bins], K.ones16[:, :], hot[u][:, k, :], start=first,
                                            stop=True, skip_group_check=True)
                        ins.then_inc(hist_added, 1)

                turns(pe, half, count)
                pe.wait_ge(start_made, 1)
                for b in range(2):
                    pe.matmul(seen[b][:, 0:bins], K.ident[:, :], start[:, :], start=True, stop=True,
                              skip_group_check=True)

                def add(b, mask, u, k):
                    return pe.matmul(seen[b][:, 0:bins], mask[:, :], hot[u][:, k, :], start=False, stop=True,
                                     skip_group_check=True)

                def place(i):
                    for u in range(2):
                        pe.wait_ge(hot_made, (i * 2 + u + 1) * 3)
                        for k in range(TB):
                            b = k % 2
                            add(b, K.upper, u, k).then_inc(seen_ready, 1)
                            if k > 0:
                                pe.wait_ge(rank_read, (i * 2 + u) * TB + k)
                                add(1 - b, K.lower, u, k - 1)
                            add(1 - b, K.ones16, u, k)
                        pe.wait_ge(rank_read, (i * 2 + u) * TB + TB)
                        add((TB - 1) % 2, K.lower, u, TB - 1).then_inc(hot_used, 1)

                turns(pe, half, place)


def prepare_order(nc, S, K, name, rows, fields, index, flags, counts):
    with Stage(nc) as c:
        def sb(n, shape, dt=F32):
            return c.enter_context(nc.sbuf_tensor(f"{name}_{n}", shape, dt))

        def sem(n):
            return c.counter(f"{name}_{n}")

        B = S.B
        cur, prv, nxt = (sb(n, [B, BS, 4], I32) for n in ("cur", "prv", "nxt"))
        key, pkey, nkey, same, end = (sb(n, [B, BS]) for n in ("key", "pkey", "nkey", "same", "end"))
        col = [sb(f"col{j}", [B, BS]) for j in range(len(fields))]
        local, unbroken, cnt, rcnt = (sb(n, [B, BS]) for n in ("local", "unbroken", "cnt", "rcnt"))
        lrow, urow, ends, carry = (sb(n, [1, B]) for n in ("lrow", "urow", "ends", "carry"))
        carry_col = sb("carry_col", [B, 1])
        turned = [c.enter_context(nc.psum_tensor(f"{name}_turned{b}", [P, TB, P], F32)) for b in range(2)]
        small = c.enter_context(nc.psum_tensor(f"{name}_small", [P, 512], F32))
        loaded, own, ends_made, ends_turned, carry_made, carry_turned, cnt_made, stored, cols_made, turned_sem, \
            taken, act_own = (sem(n) for n in (
                "loaded", "own", "ends_made", "ends_turned", "carry_made", "carry_turned", "cnt_made",
                "stored", "cols_made", "turned", "taken", "act_own"))
        todo = [*range(len(fields)), "cnt"]

        with nc.Block() as block:
            @block.sync
            def _(sp):
                for off, tile in ((1, cur), (0, prv), (2, nxt)):
                    sp.dma_start(tile[:, :, :], rows[off:off + S.EP, :].rearrange("(b s) f -> b s f", s=BS)
                                 ).then_inc(loaded, 16)
                sp.wait_ge(cnt_made, 1)
                for j, tile in enumerate((same, rcnt)):
                    sp.dma_start(flags[j, :].rearrange("(b s) -> b s", s=BS), tile[:, :]).then_inc(stored, 16)
                sp.wait_ge(stored, 32)

            @block.vector
            def _(dve):
                link = Chain(dve, own).link
                dve.wait_ge(loaded, 48)
                for tile, rows3 in ((key, cur), (pkey, prv), (nkey, nxt)):
                    link(dve.tensor_copy(tile[:, :], rows3[:, :, 0]))
                link(dve.tensor_tensor(same[:, :], key[:, :], pkey[:, :], ALU.is_equal))
                link(dve.tensor_tensor(end[:, :], key[:, :], nkey[:, :], ALU.is_equal))
                for j, f in enumerate(fields):
                    if f == "end":
                        ins = dve.scalar_tensor_tensor(col[j][:, :], end[:, :], SKIP, key[:, :], ALU.mult, ALU.add)
                    else:
                        ins = dve.tensor_copy(col[j][:, :], cur[:, :, f])
                    ins.then_inc(cols_made, 1)
                link(dve.tensor_tensor_scan(local[:, :], same[:, :], K.ones[0:B, 0:BS], 0.0, ALU.mult, ALU.add))
                dve.tensor_tensor_scan(unbroken[:, :], same[:, :], K.ones[0:B, 0:BS], 1.0, ALU.mult, ALU.mult
                                       ).then_inc(ends_made, 1)
                dve.wait_ge(ends_turned, 1)
                link(dve.tensor_copy(lrow[:, :], small[0:1, 0:B]))
                link(dve.tensor_copy(urow[:, :], small[0:1, 128:128 + B]))
                link(dve.tensor_tensor_scan(ends[:, :], urow[:, :], lrow[:, :], 0.0, ALU.mult, ALU.add))
                link(dve.memset(carry[:, :], 0.0))
                dve.tensor_copy(carry[:, 1:B], ends[:, 0:B - 1]).then_inc(carry_made, 1)
                dve.wait_ge(carry_turned, 1)
                link(dve.tensor_copy(carry_col[:, :], small[0:B, 256:257]))
                link(dve.scalar_tensor_tensor(cnt[:, :], unbroken[:, :], carry_col[:, 0:1], local[:, :],
                                              ALU.mult, ALU.add))
                dve.reciprocal(rcnt[:, :], cnt[:, :]).then_inc(cnt_made, 1)
                for n, f in enumerate(todo):
                    dve.wait_ge(turned_sem, n + 1)
                    src = turned[n % 2][:, :, 0:B]
                    dst = counts.cnt if f == "cnt" else index[:, :, TB * f:TB * f + TB]
                    dve.tensor_copy(dst.rearrange("p b k -> p k b"), src).then_inc(taken, 1)
                dve.wait_ge(taken, len(todo))
                dve.wait_ge(act_own, 3)
                link(dve.tensor_scalar(counts.amp, counts.amp, 1.0 / AVG_LOG, None, ALU.mult))
                link(dve.reciprocal(counts.ramp, counts.amp))
                if counts.dinv is not None:
                    link(dve.reciprocal(counts.dinv, counts.dinv))

            @block.scalar
            def _(act):
                act.wait_ge(taken, len(todo))
                act.activation(counts.amp, counts.cnt, ACT.Ln, bias=1.0).then_inc(act_own, 1)
                act.wait_ge(act_own, 1)
                if counts.dinv is not None:
                    act.activation(counts.dinv, counts.cnt, ACT.Sqrt).then_inc(act_own, 2)
                else:
                    act.sem_inc(act_own, 2)

            @block.tensor
            def _(pe):
                pe.wait_ge(ends_made, 1)
                pe.transpose(small[0:1, 0:B], local[:, BS - 1:BS], K.ident[0:B, 0:B])
                pe.transpose(small[0:1, 128:128 + B], unbroken[:, BS - 1:BS], K.ident[0:B, 0:B]).then_inc(ends_turned, 1)
                pe.wait_ge(carry_made, 1)
                pe.matmul(small[0:B, 256:257], carry[0:1, 0:B], K.ones[0:1, 0:1], start=True, stop=True
                          ).then_inc(carry_turned, 1)
                for n, f in enumerate(todo):
                    if f == "cnt":
                        pe.wait_ge(cnt_made, 1)
                    else:
                        pe.wait_ge(cols_made, f + 1)
                    if n >= 2:
                        pe.wait_ge(taken, n - 1)
                    src = cnt if f == "cnt" else col[f]
                    for k in range(TB):
                        ins = pe.transpose(turned[n % 2][:, k, 0:B], src[:, k * P:(k + 1) * P], K.ident[0:B, 0:B])
                    ins.then_inc(turned_sem, 1)


class Counts:

    def __init__(self, cnt, amp, ramp, dinv=None):
        self.cnt, self.amp, self.ramp, self.dinv = cnt, amp, ramp, dinv


def make_constants(nc, c):
    class K:
        pass

    def sb(n, shape, dt=F32):
        return c.enter_context(nc.sbuf_tensor(n, shape, dt))

    K.ident, K.ones, K.zeros = sb("ident", [P, P]), sb("ones", [P, 512]), sb("zeros", [P, ZW])
    K.upper, K.lower, K.ones16 = sb("upper", [P, P], F16), sb("lower", [P, P], F16), sb("ones16", [P, P], F16)
    K.bins = sb("bins", [P, 512], F16)
    setup_constants(nc, K)
    return K


STD0 = float(np.sqrt(np.float32(EPS)))
AMP0 = float(np.log(2.0)) / AVG_LOG
SCALERS = (1.0, AMP0, 1.0 / AMP0)
NS = 3 * D
XPART = 2 * D


class Side:

    def __init__(self, nc, c, name):
        def sb(n, shape):
            return c.enter_context(nc.sbuf_tensor(f"{name}_{n}", shape, F32))

        self.name = name
        self.pre = sb("pre", [P, P])
        self.bias = sb("bias", [P, 1])
        self.sbias = sb("sbias", [P, 1])
        self.nbias = sb("nbias", [D, 1])
        self.mean_std = sb("mean_std", [P, NS])
        self.max_min = sb("max_min", [P, NS])
        self.minus0 = sb("minus0", [P, D])


def pna_weights(nc, S, K, side, share, inp, shared):
    n = side.name
    with Stage(nc) as c:
        def sb(x, shape):
            return c.enter_context(nc.sbuf_tensor(f"{n}w_{x}", shape, F32))

        def ps(x, shape):
            return c.enter_context(nc.psum_tensor(f"{n}w_{x}", shape, F32))

        def sem(x):
            return c.counter(f"{n}w_{x}")

        post = sb("post", [D, XPART + 12 * D])
        lin = sb("lin", [D, D])
        postb, linb = sb("postb", [D, 1]), sb("linb", [P, D])
        postb_wide, none = sb("postb_wide", [D, P]), sb("none", [P, 3, P])
        coef, scoef = sb("coef", [P, 1]), sb("scoef", [P, 1])
        shift = sb("shift", [P, D])
        p_own, p_bias, p_none = ps("p_own", [P, 512]), ps("p_bias", [P, 512]), ps("p_none", [P, 512])
        p_ms, p_mm = ps("p_ms", [P, 512]), ps("p_mm", [P, 512])
        loaded, own, wide_made, products, scaled, none_ready = (
            sem(x) for x in ("loaded", "own", "wide_made", "products", "scaled", "none_ready"))
        loads = [(side.pre[:, :], inp[f"pre_{n}"]), (side.bias[:, :], inp[f"preb_{n}"]),
                 (post[:, :], inp[f"post_{n}"]), (lin[:, :], inp[f"lin_{n}"]),
                 (postb[:, :], inp[f"postb_{n}"]),
                 (linb[:, :], inp[f"linb_{n}"].partition_broadcast(P)),
                 (coef[:, :], inp["alpha"].partition_broadcast(P))]
        if share == 0:
            loads += [(shared.base_w[h * D:(h + 1) * D, :], inp["self_w"]) for h in range(2)]
            loads += [(shared.base_b[:, :], inp["self_b"].partition_broadcast(P))]

        with nc.Block() as block:
            @block.sync
            def _(sp):
                for dst, src in loads:
                    sp.dma_start(dst, src).then_inc(loaded, 16)

            @block.vector
            def _(dve):
                link = Chain(dve, own).link
                link(dve.memset(none[:, :, :], 0.0))
                for s in range(3):
                    link(dve.memset(none[D:P, s, :], STD0 * SCALERS[s]))
                dve.wait_ge(loaded, 16 * len(loads))
                if share == 0:
                    link(dve.tensor_scalar(coef[:, :], coef[:, :], -1.0, 1.0, ALU.mult, ALU.add))
                link(dve.tensor_copy(scoef[:, :], coef[:, :]))
                link(dve.tensor_scalar(scoef[D:P, :], coef[D:P, :], -1.0, None, ALU.mult))
                link(dve.tensor_copy(side.sbias[:, :], side.bias[:, :]))
                link(dve.tensor_scalar(side.nbias[:, :], side.bias[0:D, :], -1.0, None, ALU.mult))
                link(dve.tensor_scalar(side.sbias[D:P, :], side.bias[D:P, :], -1.0, None, ALU.mult))
                dve.tensor_scalar(postb_wide[:, :], K.ones[0:D, 0:P], postb[:, 0:1], None, ALU.mult
                                  ).then_inc(wide_made, 1)
                dve.wait_ge(products, 1)
                link(dve.tensor_scalar(side.mean_std[:, :], p_ms[:, 0:NS], coef[:, 0:1], None, ALU.mult))
                dve.tensor_scalar(side.max_min[:, :], p_mm[:, 0:NS], scoef[:, 0:1], None, ALU.mult
                                  ).then_inc(scaled, 1)
                link(dve.scalar_tensor_tensor(shared.base_w[:, :], p_own[:, 0:D], coef[:, 0:1],
                                              shared.base_w[:, :], ALU.mult, ALU.add))
                link(dve.tensor_tensor(shift[:, :], p_bias[:, 0:D], linb[:, :], ALU.add))
                link(dve.scalar_tensor_tensor(shared.base_b[:, :], shift[:, :], coef[:, 0:1],
                                              shared.base_b[:, :], ALU.mult, ALU.add))
                dve.wait_ge(none_ready, 1)
                link(dve.tensor_scalar(side.minus0[:, :], p_none[:, 0:D], -1.0, None, ALU.mult))
                link(dve.tensor_tensor(shared.base_b[:, :], shared.base_b[:, :], p_none[:, 0:D], ALU.add))
                if share == 1:
                    link(dve.memset(shared.base_w2[:, :], 0.0))
                    for q in range(2):
                        at = slice(q * D, (q + 1) * D)
                        dve.tensor_copy(shared.base_w2[at, at], shared.base_w[at, :])

            @block.tensor
            def _(pe):
                pe.wait_ge(wide_made, 1)
                pe.wait_ge(loaded, 16 * len(loads))
                for s in range(3):
                    at = XPART + 4 * D * s
                    pe.matmul(p_ms[:, s * D:(s + 1) * D], post[:, at:at + P], lin[:, :], start=True, stop=True)
                    pe.matmul(p_mm[:, s * D:(s + 1) * D], post[:, at + P:at + 2 * P], lin[:, :], start=True, stop=True)
                pe.matmul(p_own[:, 0:D], post[:, 0:P], lin[:, :], start=True, stop=True)
                pe.matmul(p_bias[:, 0:D], postb_wide[:, :], lin[:, :], start=True, stop=True).then_inc(products, 1)
                pe.wait_ge(scaled, 1)
                for s in range(3):
                    ins = pe.matmul(p_none[:, 0:D], none[:, s, :], side.mean_std[:, s * D:(s + 1) * D],
                                    start=(s == 0), stop=(s == 2))
                ins.then_inc(none_ready, 1)


def pna_pass(nc, S, K, side, table, index, gather_fields, end_field, flags, counts, aggregates, other=None):
    n = side.name
    per = len(gather_fields)
    with Stage(nc) as c:
        def sb(x, shape, dt=F32):
            return c.enter_context(nc.sbuf_tensor(f"{n}_{x}", shape, dt))

        def ps(x, shape):
            return c.enter_context(nc.psum_tensor(f"{n}_{x}", shape, F32))

        def sem(x):
            return c.counter(f"{n}_{x}")

        ends = sb("ends", [P, TB, per, D])
        gidx, sidx = sb("gidx", [P, TB * per], I32), sb("sidx", [P, TB], I32)
        fl, pen = [sb(f"fl{u}", [P, 2, BS]) for u in range(2)], sb("pen", [P, BS])
        ht = sb("ht", [P, BS])
        msg, pair = sb("msg", [P, BS]), sb("pair", [P, BS])
        sums = sb("sums", [P, BS])
        tops, agg = ([sb(f"{x}{u}", [P, BS]) for u in range(2)] for x in ("tops", "agg"))
        square = sb("square", [P, BS])
        last_sum, last_top, sign = sb("last_sum", [P, 1]), sb("last_top", [P, 1]), sb("sign", [P, 1])
        back = sb("back", [P, TB, D])
        part = sb("part", [P, D])
        rows = sb("rows", [P, TB, DAW])
        p_t, p_m, p_b = ps("p_t", [P, BS]), ps("p_m", [P, BS]), ps("p_b", [P, TB, D])
        p_o = ps("p_o", [P, 2, 2, 256])

        gathered = [sem(f"gathered{k}") for k in range(TB)]
        flags_in = [sem(f"flags_in{u}") for u in range(2)]
        turned, gidx_in, sidx_in, scattered, ht_made, m_ready, x_made, b_ready, b_taken, \
            b_stored, pen_made, mean_made, square_made, var_made, std_made, out_ready, rows_made, own, init = (
                sem(x) for x in (
                    "turned", "gidx_in", "sidx_in", "scattered", "ht_made", "m_ready", "x_made",
                    "b_ready", "b_taken", "b_stored", "pen_made", "mean_made", "square_made",
                    "var_made", "std_made", "out_ready", "rows_made", "own", "init"))

        with nc.Block() as block:
            @block.gpsimd
            def _(pool):
                def gather(g):
                    for k in range(TB):
                        before(pool, gathered[k], g, 16 * per)
                    for j, f in enumerate(gather_fields):
                        ins = pool.tensor_copy(gidx[:, TB * j:TB * j + TB],
                                               index[:, bass.ds(g, 1), TB * f:TB * f + TB].rearrange("p a k -> p (a k)"))
                    ins.then_inc(gidx_in, 1)
                    ready(pool, gidx_in, g)
                    for k in range(TB):
                        after(pool, turned, (g - 1) * TB + k + 1)
                        pool.nop(nofuse=True)
                        for j in range(per):
                            pool.indirect_dma_start(
                                ends[:, k, j, :], None, table,
                                bass.IndirectOffsetOnAxis(gidx[:, TB * j + k:TB * j + k + 1], 0)
                            ).then_inc(gathered[k], 16)

                def scatter(h):
                    before(pool, scattered, h, 16 * TB)
                    pool.tensor_copy(sidx[:, :], index[:, bass.ds(h, 1), TB * end_field:TB * end_field + TB]
                                     .rearrange("p a k -> p (a k)")).then_inc(sidx_in, 1)
                    ready(pool, sidx_in, h)
                    for k in range(TB):
                        pool.wait_ge(rows_made, h * TB + k + 1)
                        pool.nop(nofuse=True)
                        pool.indirect_dma_start(aggregates, bass.IndirectOffsetOnAxis(sidx[:, k:k + 1], 0),
                                                rows[:, k, :], None, bounds_check=S.NP - 1, oob_is_err=False
                                                ).then_inc(scattered, 16)

                def body(g):
                    gather(g)
                    if not (isinstance(g, int) and g < 2):
                        scatter(g - 2)

                turns(pool, S.B, body, peeled=3)
                scatter(S.B - 2)
                scatter(S.B - 1)
                pool.wait_ge(scattered, 16 * TB * S.B)

            @block.sync
            def _(sp):
                def body(g, u, m):
                    if not (isinstance(g, int) and g < 2):
                        sp.wait_ge(mean_made, g - 1)
                    sp.dma_start(fl[u][:, :, :], flags[:, bass.ds(g * BS, BS)].partition_broadcast(P)
                                 ).then_inc(flags_in[u], 16)
                    if other:
                        ready(sp, b_taken, g)
                        sp.dma_start(other[1][bass.ds(g * BS, BS), :].rearrange("(k p) f -> p k f", p=P),
                                     back[:, :, :]).then_inc(b_stored, 16)

                skewed(sp, S.B // 2, body, nothing)
                if other:
                    sp.wait_ge(b_stored, 16 * S.B)

            @block.tensor
            def _(pe):
                def messages(g, u, m):
                    if other:
                        before(pe, ht_made, g)
                        for k in range(TB):
                            ready(pe, gathered[k], g, 16 * per)
                            pe.transpose(p_t[:, k * P:(k + 1) * P], ends[:, k, :, :].rearrange("p a f -> p (a f)"),
                                         K.ident[:, :]).then_inc(turned, 1)
                        ready(pe, ht_made, g)
                        before(pe, x_made, g)
                        pe.matmul(p_m[:, :], side.pre[:, :], ht[:, :], start=True, stop=True).then_inc(m_ready, 1)
                        before(pe, b_taken, g)
                        for k in range(TB):
                            ins = pe.matmul(p_b[:, k, :], ht[:, k * P:(k + 1) * P], other[0].pre[:, 0:D],
                                            start=True, stop=True)
                        ins.then_inc(b_ready, 1)
                    else:
                        before(pe, x_made, g)
                        for k in range(TB):
                            ready(pe, gathered[k], g, 16 * per)
                            pe.nop(nofuse=True)
                            pe.transpose(p_m[0:D, k * P:(k + 1) * P], ends[:, k, 0, :], K.ident[:, :]
                                         ).then_inc(turned, 1)

                def products(g, u, m):
                    ready(pe, std_made, g)
                    before(pe, rows_made, g, TB)
                    for k in range(TB):
                        o = p_o[:, k // 2, k % 2, 0:NS]
                        pe.matmul(o, agg[u][:, k * P:(k + 1) * P], side.mean_std[:, :], start=True, stop=False)
                        pe.matmul(o, tops[u][:, k * P:(k + 1) * P], side.max_min[:, :], start=False, stop=True
                                  ).then_inc(out_ready, 1)

                skewed(pe, S.B // 2, messages, products)

            @block.scalar
            def _(act):
                def body(g, u, m):
                    if other:
                        ready(act, turned, g, TB)
                        before(act, b_ready, g)
                        act.copy(ht[:, :], p_t[:, :]).then_inc(ht_made, 1)
                        ready(act, m_ready, g)
                    else:
                        ready(act, turned, g, TB)
                    before(act, mean_made, g)
                    if isinstance(g, int) and g == 0:
                        act.wait_ge(init, 1)
                    act.activation(msg[0:D, :], p_m[0:D, :], ACT.Identity, bias=side.bias[0:D, 0:1])
                    if other:
                        act.activation(msg[D:P, :], p_m[D:P, :], ACT.Square, bias=side.bias[D:P, 0:1])
                        act.activation(pair[:, :], p_m[:, :], ACT.Identity, bias=side.sbias[:, 0:1],
                                       scale=sign[:, 0:1]).then_inc(x_made, 1)
                    else:
                        act.activation(msg[D:P, :], p_m[0:D, :], ACT.Square, bias=side.bias[0:D, 0:1])
                        act.activation(pair[0:D, :], p_m[0:D, :], ACT.Identity, bias=side.bias[0:D, 0:1])
                        act.activation(pair[D:P, :], p_m[0:D, :], ACT.Identity, bias=side.nbias[:, 0:1],
                                       scale=-1.0).then_inc(x_made, 1)
                    ready(act, flags_in[u], m, 16)
                    act.activation(pen[:, :], fl[u][:, 0, :], ACT.Copy, bias=-BIG, scale=BIG).then_inc(pen_made, 1)
                    if other:
                        ready(act, b_ready, g)
                        before(act, b_stored, g, 16)
                        act.copy(back[:, :, :], p_b[:, :, :]).then_inc(b_taken, 1)
                    ready(act, mean_made, g)
                    act.activation(square[D:P, :], agg[u][0:D, :], ACT.Square).then_inc(square_made, 1)
                    ready(act, var_made, g)
                    act.activation(agg[u][D:P, :], agg[u][D:P, :], ACT.Sqrt).then_inc(std_made, 1)

                skewed(act, S.B // 2, body, nothing)

            @block.vector
            def _(dve):
                chain = Chain(dve, own)
                link = chain.link
                dve.memset(last_sum[:, :], 0.0)
                dve.memset(last_top[:, :], 0.0)
                dve.memset(sign[0:D, :], 1.0)
                dve.memset(sign[D:P, :], -1.0).then_inc(init, 1)
                dve.wait_ge(init, 1)

                def scans(g, u, m):
                    ready(dve, x_made, g)
                    ready(dve, flags_in[u], m, 16)
                    ready(dve, pen_made, g)
                    if not (isinstance(g, int) and g < 2):
                        dve.wait_ge(out_ready, (g - 1) * TB)
                    link(dve.tensor_tensor_scan(sums[:, :], fl[u][:, 0, :], msg[:, :], last_sum[:, 0:1],
                                                ALU.mult, ALU.add))
                    link(dve.tensor_tensor_scan(tops[u][:, :], pen[:, :], pair[:, :], last_top[:, 0:1],
                                                ALU.add, ALU.max))
                    dve.tensor_copy(last_sum[:, :], sums[:, BS - 1:BS])
                    dve.tensor_copy(last_top[:, :], tops[u][:, BS - 1:BS])
                    dve.tensor_tensor(agg[u][:, :], sums[:, :], fl[u][:, 1, :], ALU.mult).then_inc(mean_made, 1)

                def variance(g, u, m):
                    ready(dve, square_made, g)
                    link(dve.tensor_tensor(agg[u][D:P, :], agg[u][D:P, :], square[D:P, :], ALU.subtract))
                    dve.tensor_scalar(agg[u][D:P, :], agg[u][D:P, :], 0.0, EPS, ALU.max, ALU.add).then_inc(var_made, 1)

                def rows_out(g, u, m):
                    before(dve, scattered, g, 16 * TB)
                    dve.tensor_copy(rows[:, :, D:DAW], counts.cnt[:, bass.ds(g, 1), :].rearrange("p a k -> p k a"))
                    for k in range(TB):
                        if k % 2 == 0:
                            dve.wait_ge(out_ready, g * TB + k + 2)
                        o = p_o[:, k // 2, k % 2, :]
                        amp, ramp = (x[:, bass.ds(g, 1), k:k + 1].rearrange("p a k -> p (a k)")
                                     for x in (counts.amp, counts.ramp))
                        link(dve.scalar_tensor_tensor(part[:, :], o[:, D:2 * D], amp, side.minus0[:, :],
                                                      ALU.mult, ALU.add))
                        link(dve.scalar_tensor_tensor(part[:, :], o[:, 2 * D:3 * D], ramp, part[:, :],
                                                      ALU.mult, ALU.add))
                        dve.tensor_tensor(rows[:, k, 0:D], o[:, 0:D], part[:, :], ALU.add).then_inc(rows_made, 1)
                        dve.wait_ge(rows_made, g * TB + k + 1)

                def step(a, b):
                    on(a, scans)
                    on(a, variance)
                    on(b, rows_out)

                interleaved(dve, S.B // 2, step, chain)


def wide(ap, n):
    return ap.unsqueeze(2).to_broadcast([P, CJ, n])


def by_node(row, n):
    return row.unsqueeze(1).to_broadcast([P, CJ, n])


def by_pairs(psum):
    return psum.rearrange("p a (q f) -> p (a q) f", q=2)


class Norm:

    def __init__(self, nc, c, name, degrees=False):
        def sb(x, shape):
            return c.enter_context(nc.sbuf_tensor(f"{name}_{x}", shape, F32))

        def sem(x):
            return c.counter(f"{name}_{x}")

        self.w = 2 if degrees else 1
        self.sum, self.off, self.sq = sb("sum", [P, CJ]), sb("off", [P, CJ, D]), sb("sq", [P, CJ, D])
        self.var, self.dev = sb("var", [P, 2, CJ]), sb("dev", [P, 2, CJ])
        self.inv = sb("inv", [P, 2, CJ])
        self.centered, self.squared, self.var_made, self.dev_made = (
            sem(x) for x in ("centered", "squared", "var_made", "dev_made"))

    def vector(self, dve, link, c, x, out, degree=None):
        self.center(dve, link, c, x)
        self.variance(dve, link, c, degree)
        return self.normed(dve, link, c, out)

    def center(self, dve, link, c, x):
        link(dve.tensor_reduce(self.sum[:, :], x, AX.X, ALU.add))
        link(dve.tensor_scalar(self.sum[:, :], self.sum[:, :], 1.0 / D, None, ALU.mult))
        dve.tensor_tensor(self.off[:, :, :], x, wide(self.sum[:, :], D), ALU.subtract).then_inc(self.centered, 1)

    def variance(self, dve, link, c, degree=None):
        if degree is not None:
            link(dve.tensor_scalar(self.var[:, 1, :], degree, 1.0, None, ALU.max))
        ready(dve, self.squared, c)
        link(dve.tensor_reduce(self.var[:, 0, :], self.sq[:, :, :], AX.X, ALU.add))
        dve.tensor_scalar(self.var[:, 0, :], self.var[:, 0, :], 1.0 / D, EPS, ALU.mult, ALU.add
                          ).then_inc(self.var_made, 1)

    def normed(self, dve, link, c, out):
        w = self.w
        ready(dve, self.dev_made, c)
        link(dve.reciprocal(self.inv[:, 0:w, :], self.dev[:, 0:w, :]))
        return dve.scalar_tensor_tensor(out, self.off[:, :, :], 0.0, wide(self.inv[:, 0, :], D), ALU.max, ALU.mult)

    def scalar(self, act, c):
        self.square(act, c)
        self.root(act, c)

    def square(self, act, c):
        ready(act, self.centered, c)
        act.activation(self.sq[:, :, :], self.off[:, :, :], ACT.Square).then_inc(self.squared, 1)

    def root(self, act, c):
        ready(act, self.var_made, c)
        act.activation(self.dev[:, 0:self.w, :], self.var[:, 0:self.w, :], ACT.Sqrt).then_inc(self.dev_made, 1)


def chunk(S, table, c):
    return table.rearrange("(p j) f -> p j f", p=P)[:, bass.ds(c * CJ, CJ), :]


def norm_pass(nc, S, K, x, h_out):
    with Stage(nc) as c:
        xin = [c.enter_context(nc.sbuf_tensor(f"n_x{u}", [P, CJ, D], F32)) for u in range(2)]
        h = [c.enter_context(nc.sbuf_tensor(f"n_h{u}", [P, CJ, D], F32)) for u in range(2)]
        norm = [Norm(nc, c, f"n_norm{u}") for u in range(2)]
        loaded = [c.counter(f"n_loaded{u}") for u in range(2)]
        stored = [c.counter(f"n_stored{u}") for u in range(2)]
        made, own = (c.counter(f"n_{x}") for x in ("made", "own"))
        pairs = S.CH // 2
        with nc.Block() as block:
            @block.sync
            def _(sp):
                def body(i):
                    for u in range(2):
                        before(sp, norm[u].centered, i)
                        sp.dma_start(xin[u][:, :, :], chunk(S, x, i * 2 + u)).then_inc(loaded[u], 16)
                turns(sp, pairs, body)

            @block.gpsimd
            def _(pool):
                pass

            @block.scalar
            def _(act):
                def first(c, u, m):
                    norm[u].square(act, m)

                def second(c, u, m):
                    norm[u].root(act, m)
                    ready(act, made, c)
                    act.dma_start(chunk(S, h_out, c), h[u][:, :, :]).then_inc(stored[u], 16)

                skewed(act, pairs, first, second)
                for u in range(2):
                    act.wait_ge(stored[u], 16 * pairs)

            @block.vector
            def _(dve):
                chain = Chain(dve, own)

                def first(c, u, m):
                    ready(dve, loaded[u], m, 16)
                    norm[u].center(dve, chain.link, m, xin[u][:, :, :])

                def second(c, u, m):
                    norm[u].variance(dve, chain.link, m)
                    before(dve, stored[u], m, 16)
                    norm[u].normed(dve, chain.link, m, h[u][:, :, :]).then_inc(made, 1)
                    ready(dve, made, c)

                skewed(dve, pairs, first, second, chain)


class Turner:

    def __init__(self, nc, c, name):
        self.psum = c.enter_context(nc.psum_tensor(f"{name}_p", [P, 2, CJ // 4, P], F32))
        self.out = c.enter_context(nc.sbuf_tensor(f"{name}_t", [P, 2, CJ // 4, P], F32))
        self.turned = c.counter(f"{name}_turned")
        self.copied = c.counter(f"{name}_copied")

    def tensor(self, pe, K, c, tiles):
        before(pe, self.copied, c, 2)
        for b in range(2):
            for j in range(CJ // 4):
                ins = pe.transpose(self.psum[:, b, j, :], tiles(b * (CJ // 4) + j), K.ident[:, :])
            ins.then_inc(self.turned, 1)

    def scalar(self, act, c, products, per=1):
        before(act, products, c, per)
        for b in range(2):
            act.wait_ge(self.turned, c * 2 + b + 1)
            act.copy(self.out[:, b, :, :], self.psum[:, b, :, :]).then_inc(self.copied, 1)

    def products(self, pe, psum, weight, done):
        for j in range(CJ // 2):
            ins = pe.matmul(psum(j), self.out[:, j // (CJ // 4), j % (CJ // 4), :], weight, start=True, stop=True)
        ins.then_inc(done, 1)


def pna_out_pass(nc, S, K, x, h, agg_a, agg_b, W, base_out, scaled_out):
    n = "o"
    pairs = S.CH // 2
    with Stage(nc) as c:
        def two(x, shape):
            return [c.enter_context(nc.sbuf_tensor(f"{n}_{x}{u}", shape, F32)) for u in range(2)]

        def ps(x):
            return c.enter_context(nc.psum_tensor(f"{n}_{x}", [P, CJ // 2, 2 * D], F32))

        def sem(x):
            return c.counter(f"{n}_{x}")

        xin, hin, ga, gb = two("x", [P, CJ, D]), two("h", [P, CJ, D]), two("ga", [P, CJ, DAW]), two("gb", [P, CJ, DAW])
        rest, y, yb, h1, hs, z = (two(x, [P, CJ, D]) for x in ("rest", "y", "yb", "h1", "hs", "z"))
        p_y, p_z = ps("p_y"), ps("p_z")
        turn0, turn1 = Turner(nc, c, f"{n}_t0"), Turner(nc, c, f"{n}_t1")
        norm = Norm(nc, c, f"{n}_norm", degrees=True)
        loaded, stored_s, stored_z = ([sem(f"{x}{u}") for u in range(2)] for x in ("loaded", "stored_s", "stored_z"))
        own, rest_made, rest_own, y_ready, y_made, yb_made, h1_made, hs_made, z_ready, z_made = (sem(x) for x in (
            "own", "rest_made", "rest_own", "y_ready", "y_made", "yb_made", "h1_made", "hs_made", "z_ready", "z_made"))

        with nc.Block() as block:
            @block.sync
            def _(sp):
                def first(c, u, m):
                    if not (isinstance(c, int) and c < 2):
                        sp.wait_ge(h1_made, c - 1)
                    for src, dst in ((x, xin), (h, hin), (agg_a, ga), (agg_b, gb)):
                        sp.dma_start(dst[u][:, :, :], chunk(S, src, c)).then_inc(loaded[u], 16)

                skewed(sp, pairs, first, nothing)

            @block.gpsimd
            def _(pool):
                chain = Chain(pool, rest_own)

                def first(c, u, m):
                    ready(pool, loaded[u], m, 64)
                    if not (isinstance(c, int) and c < 2):
                        pool.wait_ge(y_made, c - 1)
                    chain.link(pool.tensor_tensor(rest[u][:, :, :], xin[u][:, :, :], ga[u][:, :, 0:D], ALU.add))
                    chain.link(pool.tensor_tensor(rest[u][:, :, :], rest[u][:, :, :], gb[u][:, :, 0:D], ALU.add))
                    pool.tensor_tensor(rest[u][:, :, :], rest[u][:, :, :], by_node(W.base_b[:, :], D), ALU.add
                                       ).then_inc(rest_made, 1)

                def second(c, u, m):
                    ready(pool, y_made, c)
                    if not (isinstance(c, int) and c < 2):
                        pool.wait_ge(z_made, c - 1)
                    pool.tensor_tensor(yb[u][:, :, :], y[u][:, :, :], by_node(W.gcn_b[:, :], D), ALU.add
                                       ).then_inc(yb_made, 1)

                skewed(pool, pairs, first, second, chain)

            @block.tensor
            def _(pe):
                def first(c, u, m):
                    ready(pe, loaded[u], m, 64)
                    turn0.tensor(pe, K, c, lambda j: hin[u][:, 2 * j:2 * j + 2, :].rearrange("p a f -> p (a f)"))
                    ready(pe, turn0.copied, c, 2)
                    before(pe, y_made, c)
                    turn0.products(pe, lambda j: p_y[:, j, :], W.base_w2[:, :], y_ready)

                def second(c, u, m):
                    ready(pe, h1_made, c)
                    turn1.tensor(pe, K, c, lambda j: h1[u][:, 2 * j:2 * j + 2, :].rearrange("p a f -> p (a f)"))
                    ready(pe, turn1.copied, c, 2)
                    before(pe, z_made, c)
                    turn1.products(pe, lambda j: p_z[:, j, :], W.gcn_w[:, :], z_ready)

                skewed(pe, pairs, first, second)

            @block.scalar
            def _(act):
                def first(c, u, m):
                    turn0.scalar(act, c, y_ready)
                    if not (isinstance(c, int) and c == 0):
                        turn1.scalar(act, c - 1, z_ready)
                    norm.scalar(act, c)

                def store(c, u):
                    ready(act, z_made, c)
                    act.dma_start(chunk(S, base_out, c), z[u][:, :, :]).then_inc(stored_z[u], 16)

                def second(c, u, m):
                    ready(act, hs_made, c)
                    act.dma_start(chunk(S, scaled_out, c), hs[u][:, :, :]).then_inc(stored_s[u], 16)
                    if not (isinstance(c, int) and c == 0):
                        store(c - 1, 1 - u)

                skewed(act, pairs, first, second)
                turn1.scalar(act, S.CH - 1, z_ready)
                store(S.CH - 1, 1)
                for u in range(2):
                    act.wait_ge(stored_s[u], 16 * pairs)
                    act.wait_ge(stored_z[u], 16 * pairs)

            @block.vector
            def _(dve):
                chain = Chain(dve, own)

                def first(c, u, m):
                    ready(dve, y_ready, c)
                    ready(dve, rest_made, c)
                    if not (isinstance(c, int) and c < 2):
                        dve.wait_ge(yb_made, c - 1)
                    dve.tensor_tensor(y[u][:, :, :], by_pairs(p_y[:, :, :]), rest[u][:, :, :], ALU.add).then_inc(y_made, 1)
                    ready(dve, y_made, c)
                    norm.center(dve, chain.link, c, y[u][:, :, :])

                def normed(c, u, m):
                    norm.variance(dve, chain.link, c, ga[u][:, :, D])
                    norm.normed(dve, chain.link, c, h1[u][:, :, :]).then_inc(h1_made, 1)
                    ready(dve, h1_made, c)
                    before(dve, stored_s[u], m, 16)
                    dve.tensor_tensor(hs[u][:, :, :], h1[u][:, :, :], wide(norm.inv[:, 1, :], D), ALU.mult
                                      ).then_inc(hs_made, 1)
                    ready(dve, hs_made, c)

                def second(c, u, m):
                    ready(dve, z_ready, c)
                    ready(dve, yb_made, c)
                    before(dve, stored_z[u], m, 16)
                    dve.tensor_tensor(z[u][:, :, :], by_pairs(p_z[:, :, :]), yb[u][:, :, :], ALU.add).then_inc(z_made, 1)
                    ready(dve, z_made, c)

                def step(a, b):
                    on(a, first)
                    on(a, normed)
                    on(b, second)

                interleaved(dve, pairs, step, chain)


NW2 = D + 2
EW = D + 2 * MSG


class Rows:

    def __init__(self, nc, c, name, S, index, sources, target=None, lag=1):
        def sb(x, shape, dt=F32):
            return c.enter_context(nc.sbuf_tensor(f"{name}_{x}", shape, dt))

        def sem(x):
            return c.counter(f"{name}_{x}")

        self.S, self.index, self.sources, self.target, self.lag = S, index, sources, target, lag
        self.got = [[sb(f"got{j}{u}", [P, TB, w]) for j, (_, _, w) in enumerate(sources)] for u in range(2)]
        self.gidx = [sb(f"gidx{u}", [P, TB * len(sources)], I32) for u in range(2)]
        self.gathered = [[sem(f"gathered{u}{k}") for k in range(TB)] for u in range(2)]
        self.gidx_in = sem("gidx_in")
        if target:
            self.rows = sb("rows", [P, TB, target[2]])
            self.sidx = sb("sidx", [P, TB], I32)
            self.sidx_in, self.scattered = sem("sidx_in"), sem("scattered")

    def wait_gathered(self, eng, u, m, k):
        ready(eng, self.gathered[u][k], m, 16 * len(self.sources))

    def wait_scattered(self, eng, g):
        before(eng, self.scattered, g, 16 * TB)

    def run(self, pool, freed, rows_made=None):
        S, n = self.S, len(self.sources)

        def fields(tile, at, g, field):
            return pool.tensor_copy(tile[:, at:at + TB], self.index[:, bass.ds(g, 1), TB * field:TB * field + TB]
                                    .rearrange("p a k -> p (a k)"))

        def gather(g, u, m):
            for k in range(TB):
                before(pool, self.gathered[u][k], m, 16 * n)
            for j, (_, f, _) in enumerate(self.sources):
                ins = fields(self.gidx[u], TB * j, g, f)
            ins.then_inc(self.gidx_in, 1)
            ready(pool, self.gidx_in, g)
            if not (isinstance(g, int) and g < 2):
                for sem, per in freed:
                    pool.wait_ge(sem, (g - 1) * per)
            pool.nop(nofuse=True)
            for k in range(TB):
                for j, (table, _, _) in enumerate(self.sources):
                    pool.indirect_dma_start(
                        self.got[u][j][:, k, :], None, table,
                        bass.IndirectOffsetOnAxis(self.gidx[u][:, TB * j + k:TB * j + k + 1], 0)
                    ).then_inc(self.gathered[u][k], 16)

        def scatter(h):
            before(pool, self.scattered, h, 16 * TB)
            fields(self.sidx, 0, h, self.target[1]).then_inc(self.sidx_in, 1)
            ready(pool, self.sidx_in, h)
            ready(pool, rows_made, h)
            pool.nop(nofuse=True)
            for k in range(TB):
                pool.indirect_dma_start(self.target[0], bass.IndirectOffsetOnAxis(self.sidx[:, k:k + 1], 0),
                                        self.rows[:, k, :], None, bounds_check=S.NP - 1, oob_is_err=False
                                        ).then_inc(self.scattered, 16)

        def body(g, u, m):
            gather(g, u, m)
            if self.target and not (isinstance(g, int) and g < self.lag):
                scatter(g - self.lag)

        skewed(pool, S.B // 2, body, nothing)
        if self.target:
            for h in range(S.B - self.lag, S.B):
                scatter(h)
            pool.wait_ge(self.scattered, 16 * TB * S.B)


def sum_pass(nc, S, K, n, table, width, index, field, end_field, flags, weight, target, scale=None):
    with Stage(nc) as c:
        def sb(x, shape):
            return c.enter_context(nc.sbuf_tensor(f"{n}_{x}", shape, F32))

        def sem(x):
            return c.counter(f"{n}_{x}")

        rows = Rows(nc, c, n, S, index, [(table, field, width)], (target, end_field, D))
        fl = [sb(f"fl{u}", [width, BS]) for u in range(2)]
        vals, sums, last = sb("vals", [width, BS]), sb("sums", [width, BS]), sb("last", [width, 1])
        p_t = c.enter_context(nc.psum_tensor(f"{n}_p_t", [P, BS], F32))
        p_o = c.enter_context(nc.psum_tensor(f"{n}_p_o", [P, TB, D], F32))
        flags_in = [sem(f"flags_in{u}") for u in range(2)]
        turned, vals_made, sums_made, out_ready, rows_made, own = (sem(x) for x in (
            "turned", "vals_made", "sums_made", "out_ready", "rows_made", "own"))

        with nc.Block() as block:
            @block.gpsimd
            def _(pool):
                rows.run(pool, [(turned, 1)], rows_made)

            @block.sync
            def _(sp):
                def body(g, u, m):
                    if not (isinstance(g, int) and g < 2):
                        sp.wait_ge(sums_made, g - 1)
                    sp.dma_start(fl[u][:, :], flags[0, bass.ds(g * BS, BS)].partition_broadcast(width)
                                 ).then_inc(flags_in[u], 16)
                skewed(sp, S.B // 2, body, nothing)

            @block.tensor
            def _(pe):
                def body(g, u, m):
                    before(pe, vals_made, g)
                    for k in range(TB):
                        rows.wait_gathered(pe, u, m, k)
                        pe.nop(nofuse=True)
                        ins = pe.transpose(p_t[0:width, k * P:(k + 1) * P], rows.got[u][0][:, k, :], K.ident[:, :])
                    ins.then_inc(turned, 1)
                    ready(pe, sums_made, g)
                    before(pe, rows_made, g)
                    pe.nop(nofuse=True)
                    for k in range(TB):
                        ins = pe.matmul(p_o[:, k, :], sums[:, k * P:(k + 1) * P], weight, start=True, stop=True)
                    ins.then_inc(out_ready, 1)
                skewed(pe, S.B // 2, body, nothing)

            @block.scalar
            def _(act):
                def body(g, u, m):
                    ready(act, turned, g)
                    before(act, sums_made, g)
                    act.copy(vals[:, :], p_t[0:width, :]).then_inc(vals_made, 1)
                skewed(act, S.B // 2, body, nothing)

            @block.vector
            def _(dve):
                chain = Chain(dve, own)
                chain.link(dve.memset(last[:, :], 0.0))

                def body(g, u, m):
                    ready(dve, vals_made, g)
                    ready(dve, flags_in[u], m, 16)
                    before(dve, out_ready, g)
                    dve.tensor_tensor_scan(sums[:, :], fl[u][:, :], vals[:, :], last[:, 0:1], ALU.mult, ALU.add
                                           ).then_inc(sums_made, 1)
                    ready(dve, sums_made, g)
                    chain.link(dve.tensor_copy(last[:, :], sums[:, BS - 1:BS]))
                    ready(dve, out_ready, g)
                    rows.wait_scattered(dve, g)
                    if scale is None:
                        ins = dve.tensor_copy(rows.rows[:, :, :], p_o[:, :, :])
                    else:
                        ins = dve.tensor_tensor(rows.rows[:, :, :], p_o[:, :, :],
                                                scale[:, bass.ds(g, 1), :].rearrange("p a k -> p (a k)")
                                                .unsqueeze(2).to_broadcast([P, TB, D]), ALU.mult)
                    ins.then_inc(rows_made, 1)
                    ready(dve, rows_made, g)
                skewed(dve, S.B // 2, body, nothing, chain)


def attr_pass(nc, S, edge_attr, index, attr_out):
    n = "attr"
    with Stage(nc) as c:
        rows = Rows(nc, c, n, S, index, [(edge_attr, 3, ED)])
        stored = c.counter(f"{n}_stored")
        with nc.Block() as block:
            @block.gpsimd
            def _(pool):
                rows.run(pool, [(stored, 16)])

            @block.sync
            def _(sp):
                def body(g, u, m):
                    before(sp, stored, g, 16)
                    for k in range(TB):
                        rows.wait_gathered(sp, u, m, k)
                    sp.dma_start(attr_out[bass.ds(g * BS, BS), :].rearrange("(k p) f -> p k f", p=P),
                                 rows.got[u][0][:, :, :]).then_inc(stored, 16)
                skewed(sp, S.B // 2, body, nothing)
                sp.wait_ge(stored, 16 * S.B)


def message_pass(nc, S, K, ends, attr, index, weight, factors):
    n = "m"
    with Stage(nc) as c:
        def sb(x, shape):
            return c.enter_context(nc.sbuf_tensor(f"{n}_{x}", shape, F32))

        def sem(x):
            return c.counter(f"{n}_{x}")

        rows = Rows(nc, c, n, S, index, [(ends, 1, 2 * MSG), (ends, 0, 2 * MSG)])
        ein = [sb(f"ein{u}", [P, TB, ED]) for u in range(2)]
        ein_in = [sem(f"ein_in{u}") for u in range(2)]
        at = sb("at", [ED, BS])
        msg, ex, out = sb("m", [P, TB, MSG]), sb("ex", [P, TB, MSG]), sb("out", [P, TB, MSG])
        top, total = sb("top", [P, TB]), sb("total", [P, TB])
        p_t = c.enter_context(nc.psum_tensor(f"{n}_p_t", [P, BS], F32))
        p_m = c.enter_context(nc.psum_tensor(f"{n}_p_m", [P, TB, MSG], F32))
        turned, at_made, m_ready, m_made, ex_made, out_made, stored, own = (sem(x) for x in (
            "turned", "at_made", "m_ready", "m_made", "ex_made", "out_made", "stored", "own"))

        def over(t):
            return t[:, :].unsqueeze(2).to_broadcast([P, TB, MSG])

        with nc.Block() as block:
            @block.gpsimd
            def _(pool):
                rows.run(pool, [(m_made, 1)])

            @block.sync
            def _(sp):
                def body(g, u, m):
                    ready(sp, out_made, g)
                    sp.dma_start(factors[bass.ds(g * BS, BS), :].rearrange("(k p) f -> p k f", p=P),
                                 out[:, :, :]).then_inc(stored, 16)
                skewed(sp, S.B // 2, body, nothing)
                sp.wait_ge(stored, 16 * S.B)

            @block.tensor
            def _(pe):
                def body(g, u, m):
                    before(pe, at_made, g)
                    ready(pe, ein_in[u], m, 16)
                    pe.nop(nofuse=True)
                    for k in range(TB):
                        ins = pe.transpose(p_t[0:ED, k * P:(k + 1) * P], ein[u][:, k, :], K.ident[:, :])
                    ins.then_inc(turned, 1)
                    ready(pe, at_made, g)
                    before(pe, m_made, g)
                    pe.nop(nofuse=True)
                    for k in range(TB):
                        ins = pe.matmul(p_m[:, k, :], at[:, k * P:(k + 1) * P], weight, start=True, stop=True)
                    ins.then_inc(m_ready, 1)
                skewed(pe, S.B // 2, body, nothing)

            @block.scalar
            def _(act):
                def body(g, u, m):
                    if not (isinstance(g, int) and g < 2):
                        act.wait_ge(turned, g - 1)
                    act.dma_start(ein[u][:, :, :], attr[bass.ds(g * BS, BS), :].rearrange("(k p) f -> p k f", p=P)
                                  ).then_inc(ein_in[u], 16)
                    ready(act, turned, g)
                    before(act, m_ready, g)
                    act.copy(at[:, :], p_t[0:ED, :]).then_inc(at_made, 1)
                    ready(act, m_made, g)
                    act.activation(ex[:, :, :], msg[:, :, :], ACT.Exp).then_inc(ex_made, 1)
                skewed(act, S.B // 2, body, nothing)

            @block.vector
            def _(dve):
                chain = Chain(dve, own)
                link = chain.link

                def body(g, u, m):
                    ready(dve, m_ready, g)
                    for k in range(TB):
                        rows.wait_gathered(dve, u, m, k)
                    before(dve, ex_made, g)
                    link(dve.tensor_tensor(msg[:, :, :], p_m[:, :, :], rows.got[u][0][:, :, 0:MSG], ALU.add))
                    link(dve.tensor_tensor(msg[:, :, :], msg[:, :, :], rows.got[u][1][:, :, MSG:2 * MSG], ALU.add))
                    link(dve.scalar_tensor_tensor(msg[:, :, :], msg[:, :, :], 0.01, msg[:, :, :], ALU.mult, ALU.max))
                    link(dve.tensor_reduce(top[:, :], msg[:, :, :], AX.X, ALU.max))
                    dve.tensor_tensor(msg[:, :, :], msg[:, :, :], over(top), ALU.subtract).then_inc(m_made, 1)
                    ready(dve, ex_made, g)
                    link(dve.tensor_reduce(total[:, :], ex[:, :, :], AX.X, ALU.add))
                    link(dve.reciprocal(total[:, :], total[:, :]))
                    before(dve, stored, g, 16)
                    dve.tensor_tensor(out[:, :, :], ex[:, :, :], over(total), ALU.mult).then_inc(out_made, 1)
                    ready(dve, out_made, g)
                skewed(dve, S.B // 2, body, nothing, chain)


def gcn_out_pass(nc, S, K, base, delta, W, base_out, ends_out):
    n = "e"
    pairs = S.CH // 2
    with Stage(nc) as c:
        def two(x, shape):
            return [c.enter_context(nc.sbuf_tensor(f"{n}_{x}{u}", shape, F32)) for u in range(2)]

        def sem(x):
            return c.counter(f"{n}_{x}")

        xin, din, x2, xb, h = (two(x, [P, CJ, D]) for x in ("xin", "din", "x2", "xb", "h"))
        z, ends = two("z", [P, CJ, D]), two("ends", [P, CJ, 2 * MSG])
        p_z = c.enter_context(nc.psum_tensor(f"{n}_p_z", [P, CJ // 4, 2, 256], F32))
        turn = Turner(nc, c, f"{n}_t")
        norm = Norm(nc, c, f"{n}_norm")
        loaded, stored = ([sem(f"{x}{u}") for u in range(2)] for x in ("loaded", "stored"))
        own, pool_own, x2_made, h_made, z_ready, z_made = (sem(x) for x in (
            "own", "pool_own", "x2_made", "h_made", "z_ready", "z_made"))

        def product(q, a, b):
            return p_z[:, :, :, q * EW + a:q * EW + b].rearrange("p v i f -> p (v i) f")

        def of_pairs(tile, q):
            return tile[:, :, :].rearrange("p (a q) f -> p a q f", q=2)[:, :, q, :]

        with nc.Block() as block:
            @block.sync
            def _(sp):
                def first(c, u, m):
                    if not (isinstance(c, int) and c < 2):
                        sp.wait_ge(x2_made, c - 1)
                    for src, dst in ((base, xin), (delta, din)):
                        sp.dma_start(dst[u][:, :, :], chunk(S, src, c)).then_inc(loaded[u], 16)
                skewed(sp, pairs, first, nothing)

            @block.gpsimd
            def _(pool):
                chain = Chain(pool, pool_own)

                def first(c, u, m):
                    ready(pool, loaded[u], m, 32)
                    if not (isinstance(c, int) and c < 2):
                        pool.wait_ge(z_made, c - 1)
                    chain.link(pool.tensor_tensor(x2[u][:, :, :], xin[u][:, :, :], din[u][:, :, :], ALU.add))
                    pool.tensor_tensor(xb[u][:, :, :], x2[u][:, :, :], by_node(W.node_b[:, :], D), ALU.add
                                       ).then_inc(x2_made, 1)
                skewed(pool, pairs, first, nothing, chain)

            @block.tensor
            def _(pe):
                def second(c, u, m):
                    ready(pe, h_made, c)
                    turn.tensor(pe, K, c, lambda j: h[u][:, 2 * j:2 * j + 2, :].rearrange("p a f -> p (a f)"))
                    ready(pe, turn.copied, c, 2)
                    before(pe, z_made, c)
                    turn.products(pe, lambda j: p_z[:, j // 2, j % 2, 0:2 * EW], W.node_w[:, :], z_ready)
                skewed(pe, pairs, nothing, second)

            @block.scalar
            def _(act):
                def first(c, u, m):
                    if not (isinstance(c, int) and c == 0):
                        turn.scalar(act, c - 1, z_ready)
                    norm.scalar(act, c)

                def store(c, u):
                    ready(act, z_made, c)
                    for src, dst in ((z, base_out), (ends, ends_out)):
                        act.dma_start(chunk(S, dst, c), src[u][:, :, :]).then_inc(stored[u], 16)

                def second(c, u, m):
                    if not (isinstance(c, int) and c == 0):
                        store(c - 1, 1 - u)
                skewed(act, pairs, first, second)
                turn.scalar(act, S.CH - 1, z_ready)
                store(S.CH - 1, 1)
                for u in range(2):
                    act.wait_ge(stored[u], 32 * pairs)

            @block.vector
            def _(dve):
                chain = Chain(dve, own)

                def first(c, u, m):
                    ready(dve, x2_made, c)
                    norm.center(dve, chain.link, c, x2[u][:, :, :])

                def normed(c, u, m):
                    norm.variance(dve, chain.link, c)
                    norm.normed(dve, chain.link, c, h[u][:, :, :]).then_inc(h_made, 1)
                    ready(dve, h_made, c)

                def second(c, u, m):
                    ready(dve, z_ready, c)
                    before(dve, stored[u], m, 32)
                    for q in range(2):
                        dve.tensor_tensor(of_pairs(z[u], q), product(q, 0, D), of_pairs(xb[u], q), ALU.add)
                        ins = dve.tensor_tensor(of_pairs(ends[u], q), product(q, D, EW), W.msg_b[:, :].unsqueeze(1)
                                                .to_broadcast([P, CJ // 2, 2 * MSG]), ALU.add)
                    ins.then_inc(z_made, 1)
                    ready(dve, z_made, c)
                def step(a, b):
                    on(a, first)
                    on(a, normed)
                    on(b, second)

                interleaved(dve, pairs, step, chain)


def gat_weights(nc, S, K, W, inp):
    n = "w"
    with Stage(nc) as c:
        def sb(x, shape):
            return c.enter_context(nc.sbuf_tensor(f"{n}_{x}", shape, F32))

        def sem(x):
            return c.counter(f"{n}_{x}")

        w1t, a1 = sb("w1t", [P, HALVES, P]), sb("a1", [P, HALVES, 2 * HEADS])
        w2t, a2 = sb("w2t", [D, GF]), sb("a2", [D, 2])
        p_al = c.enter_context(nc.psum_tensor(f"{n}_p_al", [P, 512], F32))
        p_a2 = c.enter_context(nc.psum_tensor(f"{n}_p_a2", [P, HALVES, 2], F32))
        loaded, products, own, al_cleared = (sem(x) for x in ("loaded", "products", "own", "al_cleared"))
        loads = [(w1t[:, :, :], inp["w1t"].rearrange("(h p) m -> p h m", p=P)),
                 (a1[:, :, :], inp["a1"].rearrange("(h p) m -> p h m", p=P)),
                 (w2t[:, :], inp["w2t"]), (a2[:, :], inp["a2"]),
                 (W.conv2[:, :, 0:D], inp["w2"].rearrange("(h p) m -> p h m", p=P)),
                 (W.bias1[:, :], inp["b1"].rearrange("(h p) -> p h", p=P)),
                 (W.bias2[:, :], inp["b2"].partition_broadcast(P)),
                 (W.gcn_w[:, :], inp["gcn_w"]), (W.gcn_b[:, :], inp["gcn_b"].partition_broadcast(P)),
                 (W.node_w[:, :], inp["node_w"]), (W.node_b[:, :], inp["node_b"].partition_broadcast(P)),
                 (W.msg_b[:, 0:MSG], inp["msg_b"].partition_broadcast(P)),
                 (W.edge_w[:, :], inp["edge_w"]), (W.sum_w[:, :], inp["sum_w"]), (W.conv1[:, :], inp["w1"])]
        with nc.Block() as block:
            @block.sync
            def _(sp):
                with nc.allow_non_contiguous_dma(reason="a bias into two columns, 256 words"):
                    for dst, src in loads:
                        sp.dma_start(dst, src).then_inc(loaded, 16)

            @block.gpsimd
            def _(pool):
                pool.memset(W.al_w[:, :], 0.0).then_inc(al_cleared, 1)
                pool.memset(W.msg_b[:, MSG:2 * MSG], 0.0)
                pool.memset(W.spread[:, :, :], 1.0).then_inc(own, 1)
                pool.wait_ge(own, 1)
                pool.affine_select(out=W.spread[:, :, :], in_=W.spread[:, :, :], compare_op=ALU.is_ge, fill=0.0,
                                   base=0, pattern=[[P, HALVES], [1, P]], channel_multiplier=-HC).then_inc(own, 1)
                pool.wait_ge(own, 2)
                pool.affine_select(out=W.spread[:, :, :], in_=W.spread[:, :, :], compare_op=ALU.is_ge, fill=0.0,
                                   base=HC - 1, pattern=[[-P, HALVES], [-1, P]], channel_multiplier=HC).then_inc(own, 1)
                pool.wait_ge(own, 3)

            @block.tensor
            def _(pe):
                pe.wait_ge(loaded, 16 * len(loads))
                for h in range(HALVES):
                    pe.matmul(p_al[:, 0:2 * HEADS], w1t[:, h, :], a1[:, h, :], start=(h == 0), stop=(h == HALVES - 1))
                for h in range(HALVES):
                    ins = pe.matmul(p_a2[:, h, :], w2t[:, h * P:(h + 1) * P], a2[:, :], start=True, stop=True)
                ins.then_inc(products, 1)

            @block.vector
            def _(dve):
                dve.wait_ge(products, 1)
                dve.wait_ge(al_cleared, 1)
                for q in range(2):
                    at = slice(q * D, (q + 1) * D)
                    dve.tensor_copy(W.al_w[at, q * 2 * HEADS:(q + 1) * 2 * HEADS], p_al[at, 0:2 * HEADS])
                dve.tensor_copy(W.conv2[:, :, D:NW2], p_a2[:, :, :])
                dve.tensor_scalar(W.nbias1[:, :], W.bias1[:, :], -1.0, None, ALU.mult)


class Elu:

    def __init__(self, nc, c, name, W):
        def sb(x):
            return [c.enter_context(nc.sbuf_tensor(f"{name}_{x}{f}", [P, BS], F32)) for f in range(HALVES)]

        self.W, self.low, self.high = W, sb("low"), sb("high")
        self.low_own = c.counter(f"{name}_low_own")
        self.made = [c.counter(f"{name}_made{f}") for f in range(HALVES)]

    def scalar(self, act, psum, f, i):
        act.activation(self.low[f][:, :], psum, ACT.Relu, bias=self.W.nbias1[:, f:f + 1], scale=-1.0
                       ).then_inc(self.low_own, 1)
        act.activation(self.high[f][:, :], psum, ACT.Relu, bias=self.W.bias1[:, f:f + 1])
        act.wait_ge(self.low_own, i + 1)
        return act.activation(self.low[f][:, :], self.low[f][:, :], ACT.Exp, scale=-1.0)

    def vector(self, dve, f, out):
        return dve.scalar_tensor_tensor(out, self.low[f][:, :], -1.0, self.high[f][:, :], ALU.add, ALU.add)


def sums_out_pass(nc, S, K, base, delta, W, hx_out, tx_out, out):
    n = "v"
    pairs = S.CH // 2
    UNITS = 4
    with Stage(nc) as c:
        def sb(x, shape):
            return c.enter_context(nc.sbuf_tensor(f"{n}_{x}", shape, F32))

        def two(x, shape):
            return [sb(f"{x}{u}", shape) for u in range(2)]

        def sem(x):
            return c.counter(f"{n}_{x}")

        xin, din, x3, xb = (two(x, [P, CJ, D]) for x in ("xin", "din", "x3", "xb"))
        hx, tx = two("hx", [P, CJ, HX]), two("tx", [P, CJ, TX])
        hd = two("hd", [P, CJ, D])
        g = [sb(f"g{f}", [P, BS]) for f in range(HALVES)]
        ob = two("ob", [P, CJ, D])
        p_f = [c.enter_context(nc.psum_tensor(f"{n}_p_f{f}", [P, BS], F32)) for f in range(HALVES)]
        p_al = c.enter_context(nc.psum_tensor(f"{n}_p_al", [P, CJ // 2, 4 * HEADS], F32))
        p_o = [c.enter_context(nc.psum_tensor(f"{n}_p_o{v}", [P, 512], F32)) for v in range(2)]
        turn = Turner(nc, c, f"{n}_t")
        norm = Norm(nc, c, f"{n}_norm")
        elu = Elu(nc, c, f"{n}_elu", W)
        loaded, stored_h, stored_t = ([sem(f"{x}{u}") for u in range(2)] for x in ("loaded", "stored_h", "stored_t"))
        own, x_made, x_put, h_made, al_ready, al_made, o_ready, tx_made, out_made, h_copied = (
            sem(x) for x in (
                "own", "x_made", "x_put", "h_made", "al_ready", "al_made", "o_ready", "tx_made",
                "out_made", "h_copied"))
        f_ready, parts_made, g_made = ([sem(f"{x}{f}") for f in range(HALVES)] for x in (
            "f_ready", "parts_made", "g_made"))

        def unit_tiles(tile, w, a, b):
            return tile[:, :, :].rearrange("p (v i q) f -> p v i q f", v=2, q=2)[:, w // 2, :, w % 2, a:b]

        with nc.Block() as block:
            @block.sync
            def _(sp):
                def first(c, u, m):
                    if not (isinstance(c, int) and c < 2):
                        sp.wait_ge(x_made, c - 1)
                    for src, dst in ((base, xin), (delta, din)):
                        sp.dma_start(dst[u][:, :, :], chunk(S, src, c)).then_inc(loaded[u], 16)
                skewed(sp, pairs, first, nothing)

            @block.gpsimd
            def _(pool):
                def first(c, u, m):
                    ready(pool, loaded[u], m, 32)
                    if not (isinstance(c, int) and c < 2):
                        pool.wait_ge(h_made, c - 1)
                        pool.wait_ge(x_put, c - 1)
                    pool.tensor_tensor(x3[u][:, :, :], xin[u][:, :, :], din[u][:, :, :], ALU.add).then_inc(x_made, 1)
                    ready(pool, x_made, c)
                    before(pool, stored_h[u], m, 16)
                    before(pool, stored_t[u], m, 32)
                    pool.tensor_tensor(xb[u][:, :, :], x3[u][:, :, :], by_node(W.bias2[:, :], D), ALU.add)
                    pool.tensor_copy(hx[u][:, :, D + 2 * HEADS:HX], x3[u][:, :, :])
                    pool.tensor_copy(tx[u][:, :, NW2:TX], x3[u][:, :, :]).then_inc(x_put, 1)
                skewed(pool, pairs, first, nothing)

            @block.tensor
            def _(pe):
                def turn_h(c, u, m):
                    ready(pe, h_made, c)
                    turn.tensor(pe, K, c, lambda j: hd[u][:, 2 * j:2 * j + 2, :].rearrange("p a f -> p (a f)"))

                def logits(c, u, m):
                    ready(pe, turn.copied, c, 2)
                    before(pe, al_made, c)
                    turn.products(pe, lambda j: p_al[:, j, :], W.al_w[:, :], al_ready)

                def convolve1(c, u, m, w):
                    at = slice((w % 2) * D, (w % 2) * D + D)
                    for f in range(HALVES):
                        before(pe, parts_made[f], c * UNITS + w)
                        pe.nop(nofuse=True)
                        pe.matmul(p_f[f][:, :], W.conv1[at, f * P:(f + 1) * P],
                                  turn.out[at, w // 2, :, :].rearrange("p a b -> p (a b)"), start=True, stop=True
                                  ).then_inc(f_ready[f], 1)

                def convolve2(c, u, m, w):
                    for f in range(HALVES):
                        ready(pe, g_made[f], c * UNITS + w)
                    after(pe, tx_made, c * UNITS + w - 1)
                    for i in range(TB):
                        for f in range(HALVES):
                            ins = pe.matmul(p_o[w % 2][:, i * NW2:(i + 1) * NW2], g[f][:, i * P:(i + 1) * P],
                                            W.conv2[:, f, :], start=(f == 0), stop=(f == HALVES - 1))
                    ins.then_inc(o_ready, 1)

                def step(a, b):
                    on(b, logits)
                    on(b, convolve1, 0)
                    on(b, convolve1, 1)
                    on(b, convolve2, 0)
                    on(b, convolve1, 2)
                    on(b, convolve2, 1)
                    on(b, convolve1, 3)
                    on(a, turn_h)
                    on(b, convolve2, 2)
                    on(b, convolve2, 3)

                interleaved(pe, pairs, step)

            @block.scalar
            def _(act):
                def elus(c, u, m, w):
                    for f in range(HALVES):
                        i = c * UNITS + w
                        ready(act, f_ready[f], i)
                        before(act, g_made[f], i)
                        elu.scalar(act, p_f[f][:, :], f, i * HALVES + f).then_inc(parts_made[f], 1)

                def copy_turned(c, u, m):
                    turn.scalar(act, c, f_ready[HALVES - 1], UNITS)

                def copy_h(c, u, m):
                    ready(act, h_made, c)
                    if not (isinstance(c, int) and c < 2):
                        act.wait_ge(x_put, c + 1)
                    act.copy(hx[u][:, :, 0:D], hd[u][:, :, :]).then_inc(h_copied, 1)

                def store_h(c, u, m):
                    ready(act, x_put, c)
                    ready(act, al_made, c)
                    ready(act, h_copied, c)
                    act.dma_start(chunk(S, hx_out, c), hx[u][:, :, :]).then_inc(stored_h[u], 16)

                def store_t(c, u):
                    ready(act, out_made, c)
                    for src, dst in ((tx, tx_out), (ob, out)):
                        act.dma_start(chunk(S, dst, c), src[u][:, :, :]).then_inc(stored_t[u], 16)

                def store_last(c, u, m):
                    if not (isinstance(c, int) and c == 0):
                        store_t(c - 1, 1 - u)

                def step(a, b):
                    on(b, store_last)
                    on(b, elus, 0)
                    on(a, lambda c, u, m: norm.square(act, c))
                    on(b, elus, 1)
                    on(b, store_h)
                    on(a, lambda c, u, m: norm.root(act, c))
                    on(b, elus, 2)
                    on(a, copy_turned)
                    on(b, elus, 3)
                    on(a, copy_h)

                interleaved(act, pairs, step)
                store_t(S.CH - 1, 1)
                for u in range(2):
                    act.wait_ge(stored_h[u], 16 * pairs)
                    act.wait_ge(stored_t[u], 32 * pairs)

            @block.vector
            def _(dve):
                chain = Chain(dve, own)

                def center(c, u, m):
                    ready(dve, x_made, c)
                    norm.center(dve, chain.link, c, x3[u][:, :, :])

                def normed(c, u, m):
                    if not (isinstance(c, int) and c < 2):
                        dve.wait_ge(h_copied, c - 1)
                    norm.normed(dve, chain.link, c, hd[u][:, :, :]).then_inc(h_made, 1)
                    ready(dve, h_made, c)

                def take_logits(c, u, m):
                    ready(dve, al_ready, c)
                    ready(dve, x_put, c)
                    dve.tensor_copy(hx[u][:, :, D:D + 2 * HEADS],
                                    p_al[:, :, :].rearrange("p a (q f) -> p (a q) f", q=2)).then_inc(al_made, 1)

                def elu_sums(c, u, m, w):
                    for f in range(HALVES):
                        i = c * UNITS + w
                        ready(dve, parts_made[f], i)
                        before(dve, o_ready, i)
                        elu.vector(dve, f, g[f][:, :]).then_inc(g_made[f], 1)

                def take(c, u, m, w):
                    ready(dve, o_ready, c * UNITS + w)
                    dve.tensor_copy(unit_tiles(tx[u], w, 0, NW2),
                                    p_o[w % 2][:, 0:TB * NW2].rearrange("p (i f) -> p i f", f=NW2)).then_inc(tx_made, 1)
                    ready(dve, tx_made, c * UNITS + w)

                def add_x(c, u, m):
                    dve.tensor_tensor(ob[u][:, :, :], tx[u][:, :, 0:D], xb[u][:, :, :], ALU.add).then_inc(out_made, 1)
                    ready(dve, out_made, c)

                def step(a, b):
                    on(a, center)
                    on(b, take_logits)
                    on(b, elu_sums, 0)
                    on(a, lambda c, u, m: norm.variance(dve, chain.link, c))
                    on(b, elu_sums, 1)
                    on(b, take, 0)
                    on(a, normed)
                    on(b, elu_sums, 2)
                    on(b, take, 1)
                    on(b, elu_sums, 3)
                    on(b, take, 2)
                    on(b, take, 3)
                    on(b, add_x)

                interleaved(dve, pairs, step, chain)


class Attention:

    def __init__(self, nc, c, name, heads, al_s, al_d):
        def sb(x, shape):
            return c.enter_context(nc.sbuf_tensor(f"{name}_{x}", shape, F32))

        def sem(x):
            return c.counter(f"{name}_{x}")

        H = self.heads = heads
        self.al_s, self.al_d = slice(al_s, al_s + H), slice(al_d, al_d + H)
        self.fl, self.pen = sb("fl", [H, BS]), sb("pen", [H, BS])
        self.e, self.et = sb("e", [P, TB, 2 * H]), sb("et", [H, BS])
        self.top, self.den, self.last = sb("top", [H, BS + 1]), sb("den", [H, BS]), sb("last", [H, 1])
        self.low = sb("low", [H, 2, BS])
        self.keep_new = [sb(f"keep_new{u}", [H, 2, BS]) for u in range(2)]
        self.topf, self.off, self.ce = sb("topf", [P, TB, H]), sb("off", [P, 2, TB, H]), sb("ce", [P, 2, TB, H])
        self.total = sb("total", [P, TB, H])
        self.coef = [sb(f"coef{u}", [P, 2, TB, H]) for u in range(2)]
        self.p_e = c.enter_context(nc.psum_tensor(f"{name}_p_e", [P, BS], F32))
        self.p_r = c.enter_context(nc.psum_tensor(f"{name}_p_r", [P, 2, TB, H], F32))
        (self.flags_in, self.pen_made, self.e_made, self.e_turned, self.et_made, self.low_made, self.kn_made,
         self.den_made, self.r_ready, self.off_made, self.ce_made, self.coef_made, self.init) = (
            sem(x) for x in (
                "flags_in", "pen_made", "e_made", "e_turned", "et_made", "low_made", "kn_made", "den_made",
                "r_ready", "off_made", "ce_made", "coef_made", "init"))

    def sync(self, sp, flags, g):
        before(sp, self.low_made, g)
        sp.dma_start(self.fl[:, :], flags[0, bass.ds(g * BS, BS)].partition_broadcast(self.heads)
                     ).then_inc(self.flags_in, 16)

    def turn_logits(self, pe, K, g):
        ready(pe, self.e_made, g)
        before(pe, self.et_made, g)
        pe.nop(nofuse=True)
        for k in range(TB):
            ins = pe.transpose(self.p_e[0:self.heads, k * P:(k + 1) * P], self.e[:, k, 0:self.heads], K.ident[:, :])
        ins.then_inc(self.e_turned, 1)

    def turn_results(self, pe, K, g):
        H = self.heads
        ready(pe, self.den_made, g)
        before(pe, self.coef_made, g)
        pe.nop(nofuse=True)
        for j, (tile, at) in enumerate(((self.top, 1), (self.den, 0))):
            for k in range(TB):
                ins = pe.transpose(self.p_r[:, j, k, :], tile[:, at + k * P:at + (k + 1) * P], K.ident[0:H, 0:H])
        ins.then_inc(self.r_ready, 1)

    def scalar(self, act, g, u, spread_ready):
        self.scalar_logits(act, g)
        self.scalar_factors(act, g, u, spread_ready)
        self.scalar_offs(act, g)

    def scalar_logits(self, act, g):
        ready(act, self.flags_in, g, 16)
        before(act, self.low_made, g)
        act.activation(self.pen[:, :], self.fl[:, :], ACT.Copy, bias=-BIG, scale=BIG).then_inc(self.pen_made, 1)
        ready(act, self.e_turned, g)
        act.copy(self.et[:, :], self.p_e[0:self.heads, :]).then_inc(self.et_made, 1)

    def scalar_factors(self, act, g, u, spread_ready):
        ready(act, self.low_made, g)
        if not (isinstance(g, int) and g < 2):
            act.wait_ge(spread_ready, g - 1)
        act.activation(self.keep_new[u][:, :, :], self.low[:, :, :], ACT.Exp).then_inc(self.kn_made, 1)

    def scalar_offs(self, act, g):
        ready(act, self.off_made, g)
        act.activation(self.ce[:, :, :, :], self.off[:, :, :, :], ACT.Exp).then_inc(self.ce_made, 1)

    def start(self, dve):
        dve.memset(self.top[:, :], 0.0).then_inc(self.init, 1)
        dve.memset(self.last[:, :], 0.0).then_inc(self.init, 1)
        dve.wait_ge(self.init, 2)

    def logits(self, dve, link, g, src, dst):
        H = self.heads
        before(dve, self.e_turned, g)
        link(dve.tensor_tensor(self.e[:, :, 0:H], src[:, :, self.al_s], dst[:, :, self.al_d], ALU.add))
        link(dve.tensor_tensor(self.e[:, :, H:2 * H], dst[:, :, self.al_s], dst[:, :, self.al_d], ALU.add))
        dve.scalar_tensor_tensor(self.e[:, :, :], self.e[:, :, :], 0.2, self.e[:, :, :], ALU.mult, ALU.max
                                 ).then_inc(self.e_made, 1)
        ready(dve, self.e_made, g)

    def tops(self, dve, link, g):
        top, low = self.top, self.low
        ready(dve, self.et_made, g)
        ready(dve, self.pen_made, g)
        link(dve.tensor_tensor_scan(top[:, 1:BS + 1], self.pen[:, :], self.et[:, :], top[:, 0:1], ALU.add, ALU.max))
        link(dve.tensor_tensor(low[:, 0, :], top[:, 0:BS], self.pen[:, :], ALU.add))
        link(dve.tensor_tensor(low[:, 0, :], low[:, 0, :], top[:, 1:BS + 1], ALU.subtract))
        dve.tensor_tensor(low[:, 1, :], self.et[:, :], top[:, 1:BS + 1], ALU.subtract).then_inc(self.low_made, 1)

    def dens(self, dve, link, g, u):
        ready(dve, self.kn_made, g)
        kn = self.keep_new[u]
        dve.tensor_tensor_scan(self.den[:, :], kn[:, 0, :], kn[:, 1, :], self.last[:, 0:1], ALU.mult, ALU.add
                               ).then_inc(self.den_made, 1)

    def offs(self, dve, link, g):
        H, top = self.heads, self.top
        ready(dve, self.r_ready, g)
        link(dve.tensor_copy(top[:, 0:1], top[:, BS:BS + 1]))
        link(dve.tensor_copy(self.last[:, :], self.den[:, BS - 1:BS]))
        loop = self.e[:, :, H:2 * H]
        link(dve.tensor_tensor(self.topf[:, :, :], self.p_r[:, 0, :, :], loop, ALU.max))
        link(dve.tensor_tensor(self.off[:, 0, :, :], self.p_r[:, 0, :, :], self.topf[:, :, :], ALU.subtract))
        dve.tensor_tensor(self.off[:, 1, :, :], loop, self.topf[:, :, :], ALU.subtract).then_inc(self.off_made, 1)

    def coefs(self, dve, link, g, u):
        H = self.heads
        ready(dve, self.ce_made, g)
        link(dve.tensor_tensor(self.total[:, :, :], self.p_r[:, 1, :, :], self.ce[:, 0, :, :], ALU.mult))
        link(dve.scalar_tensor_tensor(self.total[:, :, :], self.total[:, :, :], 1e-16, self.ce[:, 1, :, :],
                                      ALU.add, ALU.add))
        link(dve.reciprocal(self.total[:, :, :], self.total[:, :, :]))
        dve.tensor_tensor(self.coef[u][:, :, :, :], self.ce[:, :, :, :],
                          self.total[:, :, :].unsqueeze(1).to_broadcast([P, 2, TB, H]), ALU.mult
                          ).then_inc(self.coef_made, 1)
        ready(dve, self.coef_made, g)


def gat1_pass(nc, S, K, hx, index, flags, W, tx):
    n = "a"
    with Stage(nc) as c:
        def sb(x, shape):
            return c.enter_context(nc.sbuf_tensor(f"{n}_{x}", shape, F32))

        def two(x, shape):
            return [sb(f"{x}{u}", shape) for u in range(2)]

        def ps(x, shape):
            return c.enter_context(nc.psum_tensor(f"{n}_{x}", shape, F32))

        def sem(x):
            return c.counter(f"{n}_{x}")

        def halves(x):
            return [sem(f"{x}{f}") for f in range(HALVES)]

        rows = Rows(nc, c, n, S, index, [(hx, 1, HX), (hx, 0, HX)], (tx, 2, TX), lag=3)
        att = Attention(nc, c, f"{n}_att", HEADS, D, D + HEADS)
        elu = Elu(nc, c, f"{n}_elu", W)
        hs, hd = two("hs", [D, BS]), two("hd", [D, BS])
        xrow = two("xrow", [P, TB, D])
        new, val = sb("new", [P, BS]), sb("val", [P, BS])
        state = [sb(f"state{f}", [P, BS]) for f in range(HALVES)]
        last = [sb(f"last{f}", [P, 1]) for f in range(HALVES)]
        edges, loop = ([sb(f"{x}{f}", [P, TB, P]) for f in range(HALVES)] for x in ("edges", "loop"))
        g2 = [sb(f"g{f}", [P, BS]) for f in range(HALVES)]
        p_h, p_k, p_n, p_v, p_s, p_d = (ps(x, [P, BS]) for x in ("p_h", "p_k", "p_n", "p_v", "p_s", "p_d"))
        h_turned, h_copied, hx_copied, o_ready, rows_made, own, init = (sem(x) for x in (
            "h_turned", "h_copied", "hx_copied", "o_ready", "rows_made", "own", "init"))
        spread_ready, new_copied, val_made, state_made, s_ready, edges_made, loop_made, sum_ready, parts_made, \
            g_made = (halves(x) for x in (
                "spread_ready", "new_copied", "val_made", "state_made", "s_ready", "edges_made", "loop_made",
                "sum_ready", "parts_made", "g_made"))

        def heads(tile):
            return tile.rearrange("p (k h c) -> p k h c", k=TB, c=HC)

        def of_half(coef, f):
            nh = HEADS // HALVES
            return coef[:, :, f * nh:(f + 1) * nh].unsqueeze(3).to_broadcast([P, TB, nh, HC])

        with nc.Block() as block:
            @block.gpsimd
            def _(pool):
                rows.run(pool, [(h_turned, 2), (att.e_made, 1), (hx_copied, 1)], rows_made)

            @block.sync
            def _(sp):
                turns(sp, S.B, lambda g: att.sync(sp, flags, g))

            @block.tensor
            def _(pe):
                def turn_ends(g, u, m, e):
                    if e == 0:
                        before(pe, h_copied, g, 2)
                        if not (isinstance(g, int) and g < 2):
                            pe.wait_ge(parts_made[HALVES - 1], g - 1)
                        for k in range(TB):
                            rows.wait_gathered(pe, u, m, k)
                    else:
                        pe.wait_ge(h_copied, g * 2 + 1)
                    pe.nop(nofuse=True)
                    for k in range(TB):
                        ins = pe.transpose(p_h[0:D, k * P:(k + 1) * P], rows.got[u][e][:, k, 0:D], K.ident[:, :])
                    ins.then_inc(h_turned, 1)

                def spread(g, u, m, f):
                    if f == 0:
                        before(pe, state_made[HALVES - 1], g)
                    else:
                        ready(pe, state_made[f - 1], g)
                    pe.nop(nofuse=True)
                    for j, bank in ((1, p_n), (0, p_k)):
                        pe.matmul(bank[:, :], W.spread[:, f, :], att.keep_new[u][:, j, :], start=True, stop=True)
                    pe.matmul(p_v[:, :], W.conv1[0:D, f * P:(f + 1) * P], hs[u][:, :], start=True, stop=True
                              ).then_inc(spread_ready[f], 1)

                def by_slot(g, u, m, f):
                    if f == 0:
                        before(pe, loop_made[HALVES - 1], g)
                        before(pe, edges_made[HALVES - 1], g)
                    else:
                        ready(pe, loop_made[f - 1], g)
                        ready(pe, edges_made[f - 1], g)
                    pe.nop(nofuse=True)
                    for k in range(TB):
                        pe.matmul(p_d[:, k * P:(k + 1) * P], hd[u][:, k * P:(k + 1) * P],
                                  W.conv1[0:D, f * P:(f + 1) * P], start=True, stop=True)
                    ready(pe, state_made[f], g)
                    pe.nop(nofuse=True)
                    for k in range(TB):
                        ins = pe.transpose(p_s[:, k * P:(k + 1) * P], state[f][:, k * P:(k + 1) * P], K.ident[:, :])
                    ins.then_inc(s_ready[f], 1)

                def by_feature(g, u, m, f):
                    ready(pe, loop_made[f], g)
                    if f == 0:
                        ready(pe, h_copied, g if isinstance(g, int) and g == S.B - 1 else g + 1, 2)
                        before(pe, rows_made, g)
                    if f > 0:
                        ready(pe, parts_made[f - 1], g)
                    pe.nop(nofuse=True)
                    for k in range(TB):
                        at = slice(k * P, (k + 1) * P)
                        pe.matmul(p_h[:, at], edges[f][:, k, :], K.ident[:, :], start=True, stop=False)
                        ins = pe.matmul(p_h[:, at], loop[f][:, k, :], K.ident[:, :], start=False, stop=True)
                    ins.then_inc(sum_ready[f], 1)

                def convolve(g, copied):
                    for f in range(HALVES):
                        ready(pe, g_made[f], g)
                    ready(pe, h_copied, copied, 2)
                    for k in range(TB):
                        for f in range(HALVES):
                            ins = pe.matmul(p_h[:, k * NW2:(k + 1) * NW2], g2[f][:, k * P:(k + 1) * P],
                                            W.conv2[:, f, :], start=(f == 0), stop=(f == HALVES - 1))
                    ins.then_inc(o_ready, 1)

                def convolve_last(g, u, m):
                    if not (isinstance(g, int) and g == 0):
                        convolve(g - 1, g if isinstance(g, int) and g == S.B - 1 else g + 1)

                def step(a, b):
                    on(a, turn_ends, 0)
                    on(a, lambda g, u, m: att.turn_logits(pe, K, g))
                    on(a, turn_ends, 1)
                    on(b, spread, 0)
                    on(b, by_slot, 0)
                    on(b, spread, 1)
                    on(b, convolve_last)
                    on(a, lambda g, u, m: att.turn_results(pe, K, g))
                    on(b, by_feature, 0)
                    on(b, by_slot, 1)
                    on(b, by_feature, 1)

                interleaved(pe, S.B // 2, step)
                convolve(S.B - 1, S.B - 1)

            @block.scalar
            def _(act):
                def copy_end(g, u, m, e):
                    act.wait_ge(h_turned, g * 2 + e + 1)
                    if not (isinstance(g, int) and g < 2):
                        act.wait_ge(sum_ready[HALVES - 1], g - 1)
                    act.copy((hs, hd)[e][u][:, :], p_h[0:D, :]).then_inc(h_copied, 1)

                def copy_x(g, u, m):
                    for k in range(TB):
                        rows.wait_gathered(act, u, m, k)
                    if not (isinstance(g, int) and g < 2):
                        act.wait_ge(rows_made, g - 1)
                    act.copy(xrow[u][:, :, :], rows.got[u][1][:, :, D + 2 * HEADS:HX]).then_inc(hx_copied, 1)

                def copy_new(g, u, m, f):
                    ready(act, spread_ready[f], g)
                    if f == 0:
                        before(act, val_made[HALVES - 1], g)
                    else:
                        ready(act, val_made[f - 1], g)
                    act.copy(new[:, :], p_n[:, :]).then_inc(new_copied[f], 1)

                def elu_parts(g, u, m, f):
                    ready(act, sum_ready[f], g)
                    before(act, g_made[f], g)
                    elu.scalar(act, p_h[:, :], f, g * HALVES + f).then_inc(parts_made[f], 1)

                def step(a, b):
                    on(a, copy_end, 0)
                    on(a, lambda g, u, m: att.scalar_logits(act, g))
                    on(a, copy_end, 1)
                    on(b, copy_new, 0)
                    on(a, lambda g, u, m: att.scalar_factors(act, g, u, spread_ready[HALVES - 1]))
                    on(b, copy_new, 1)
                    on(a, copy_x)
                    on(a, lambda g, u, m: att.scalar_offs(act, g))
                    on(b, elu_parts, 0)
                    on(b, elu_parts, 1)

                interleaved(act, S.B // 2, step)

            @block.vector
            def _(dve):
                chain = Chain(dve, own)
                link = chain.link
                att.start(dve)
                for f in range(HALVES):
                    dve.memset(last[f][:, :], 0.0).then_inc(init, 1)
                dve.wait_ge(init, HALVES)

                def logits(g, u, m):
                    for k in range(TB):
                        rows.wait_gathered(dve, u, m, k)
                    att.logits(dve, link, g, rows.got[u][0], rows.got[u][1])

                def scan(g, u, m, f):
                    ready(dve, new_copied[f], g)
                    dve.tensor_tensor(val[:, :], new[:, :], p_v[:, :], ALU.mult).then_inc(val_made[f], 1)
                    ready(dve, val_made[f], g)
                    before(dve, s_ready[f], g)
                    dve.tensor_tensor_scan(state[f][:, :], p_k[:, :], val[:, :], last[f][:, 0:1], ALU.mult, ALU.add
                                           ).then_inc(state_made[f], 1)
                    ready(dve, state_made[f], g)
                    link(dve.tensor_copy(last[f][:, :], state[f][:, BS - 1:BS]))

                def merge(g, u, m, f):
                    ready(dve, s_ready[f], g)
                    before(dve, sum_ready[f], g)
                    dve.tensor_tensor(edges[f][:, :, :].rearrange("p k (h c) -> p k h c", c=HC), heads(p_s[:, :]),
                                      of_half(att.coef[u][:, 0], f), ALU.mult).then_inc(edges_made[f], 1)
                    dve.tensor_tensor(loop[f][:, :, :].rearrange("p k (h c) -> p k h c", c=HC), heads(p_d[:, :]),
                                      of_half(att.coef[u][:, 1], f), ALU.mult).then_inc(loop_made[f], 1)

                def elu_sum(g, u, m, f):
                    ready(dve, parts_made[f], g)
                    before(dve, o_ready, g)
                    elu.vector(dve, f, g2[f][:, :]).then_inc(g_made[f], 1)

                def take(g, u):
                    ready(dve, hx_copied, g)
                    rows.wait_scattered(dve, g)
                    link(dve.tensor_copy(rows.rows[:, :, NW2:TX], xrow[u][:, :, :]))
                    ready(dve, o_ready, g)
                    dve.tensor_copy(rows.rows[:, :, 0:NW2], p_h[:, 0:TB * NW2].rearrange("p (k f) -> p k f", f=NW2)
                                    ).then_inc(rows_made, 1)
                    ready(dve, rows_made, g)

                def take_last(g, u, m):
                    if not (isinstance(g, int) and g == 0):
                        take(g - 1, 1 - u)

                def step(a, b):
                    on(a, logits)
                    on(b, scan, 0)
                    on(a, lambda g, u, m: att.tops(dve, link, g))
                    on(b, scan, 1)
                    on(a, lambda g, u, m: att.dens(dve, link, g, u))
                    on(b, take_last)
                    on(b, merge, 0)
                    on(a, lambda g, u, m: att.offs(dve, link, g))
                    on(b, merge, 1)
                    on(a, lambda g, u, m: att.coefs(dve, link, g, u))
                    on(b, elu_sum, 0)
                    on(b, elu_sum, 1)

                interleaved(dve, S.B // 2, step, chain)
                take(S.B - 1, 1)


def gat2_pass(nc, S, K, tx, index, flags, W, out):
    n = "b"
    with Stage(nc) as c:
        def sb(x, shape):
            return c.enter_context(nc.sbuf_tensor(f"{n}_{x}", shape, F32))

        def two(x, shape):
            return [sb(f"{x}{u}", shape) for u in range(2)]

        def ps(x, shape):
            return c.enter_context(nc.psum_tensor(f"{n}_{x}", shape, F32))

        def sem(x):
            return c.counter(f"{n}_{x}")

        rows = Rows(nc, c, n, S, index, [(tx, 1, TX), (tx, 0, TX)], (out, 2, D), lag=2)
        att = Attention(nc, c, f"{n}_att", 1, D, D + 1)
        hs, rest = two("hs", [D, BS]), two("rest", [P, TB, D])
        own_part = sb("own_part", [P, TB, D])
        val, state, last = sb("val", [D, BS]), sb("state", [D, BS]), sb("last", [D, 1])
        p_h, p_k, p_n, p_s = ps("p_h", [P, BS]), ps("p_k", [P, BS]), ps("p_n", [P, BS]), ps("p_s", [P, TB, D])
        h_turned, h_copied, rest_made, spread_ready, val_made, state_made, s_ready, rows_made, own, init = (
            sem(x) for x in ("h_turned", "h_copied", "rest_made", "spread_ready", "val_made", "state_made",
                             "s_ready", "rows_made", "own", "init"))

        def over(coef):
            return coef[:, :, 0:1].to_broadcast([P, TB, D])

        with nc.Block() as block:
            @block.gpsimd
            def _(pool):
                rows.run(pool, [(h_turned, 1), (rest_made, 1)], rows_made)

            @block.sync
            def _(sp):
                turns(sp, S.B, lambda g: att.sync(sp, flags, g))

            @block.tensor
            def _(pe):
                def first(g, u, m):
                    before(pe, h_copied, g)
                    for k in range(TB):
                        rows.wait_gathered(pe, u, m, k)
                    pe.nop(nofuse=True)
                    for k in range(TB):
                        ins = pe.transpose(p_h[0:D, k * P:(k + 1) * P], rows.got[u][0][:, k, 0:D], K.ident[:, :])
                    ins.then_inc(h_turned, 1)
                    att.turn_logits(pe, K, g)

                def second(g, u, m):
                    before(pe, state_made, g)
                    pe.nop(nofuse=True)
                    for j, bank in ((1, p_n), (0, p_k)):
                        ins = pe.matmul(bank[0:D, :], K.ones[0:1, 0:D], att.keep_new[u][:, j, :], start=True, stop=True)
                    ins.then_inc(spread_ready, 1)
                    ready(pe, state_made, g)
                    before(pe, rows_made, g)
                    pe.nop(nofuse=True)
                    for k in range(TB):
                        ins = pe.transpose(p_s[:, k, :], state[:, k * P:(k + 1) * P], K.ident[0:D, 0:D])
                    ins.then_inc(s_ready, 1)

                def step(a, b):
                    on(a, first)
                    on(a, lambda g, u, m: att.turn_results(pe, K, g))
                    on(b, second)

                interleaved(pe, S.B // 2, step)

            @block.scalar
            def _(act):
                def first(g, u, m):
                    ready(act, h_turned, g)
                    if not (isinstance(g, int) and g < 2):
                        act.wait_ge(val_made, g - 1)
                    act.copy(hs[u][:, :], p_h[0:D, :]).then_inc(h_copied, 1)
                    att.scalar(act, g, u, spread_ready)

                skewed(act, S.B // 2, first, nothing)

            @block.vector
            def _(dve):
                chain = Chain(dve, own)
                link = chain.link
                att.start(dve)
                dve.memset(last[:, :], 0.0).then_inc(init, 1)
                dve.wait_ge(init, 1)

                def logits(g, u, m):
                    for k in range(TB):
                        rows.wait_gathered(dve, u, m, k)
                    att.logits(dve, link, g, rows.got[u][0], rows.got[u][1])

                def others(g, u, m):
                    att.coefs(dve, link, g, u)
                    dst = rows.got[u][1]
                    link(dve.tensor_tensor(rest[u][:, :, :], dst[:, :, NW2:TX],
                                           W.bias2[:, :].unsqueeze(1).to_broadcast([P, TB, D]), ALU.add))
                    link(dve.tensor_tensor(own_part[:, :, :], dst[:, :, 0:D], over(att.coef[u][:, 1]), ALU.mult))
                    dve.tensor_tensor(rest[u][:, :, :], rest[u][:, :, :], own_part[:, :, :], ALU.add
                                      ).then_inc(rest_made, 1)
                    ready(dve, rest_made, g)

                def scan(g, u, m):
                    ready(dve, spread_ready, g)
                    ready(dve, h_copied, g)
                    dve.tensor_tensor(val[:, :], p_n[0:D, :], hs[u][:, :], ALU.mult).then_inc(val_made, 1)
                    ready(dve, val_made, g)
                    before(dve, s_ready, g)
                    dve.tensor_tensor_scan(state[:, :], p_k[0:D, :], val[:, :], last[:, 0:1], ALU.mult, ALU.add
                                           ).then_inc(state_made, 1)
                    ready(dve, state_made, g)
                    link(dve.tensor_copy(last[:, :], state[:, BS - 1:BS]))

                def rows_out(g, u, m):
                    ready(dve, s_ready, g)
                    rows.wait_scattered(dve, g)
                    link(dve.tensor_tensor(rows.rows[:, :, :], p_s[:, :, :], over(att.coef[u][:, 0]), ALU.mult))
                    dve.tensor_tensor(rows.rows[:, :, :], rows.rows[:, :, :], rest[u][:, :, :], ALU.add
                                      ).then_inc(rows_made, 1)
                    ready(dve, rows_made, g)

                def step(a, b):
                    on(a, logits)
                    on(a, lambda g, u, m: att.tops(dve, link, g))
                    on(a, lambda g, u, m: att.dens(dve, link, g, u))
                    on(a, lambda g, u, m: att.offs(dve, link, g))
                    on(a, others)
                    on(b, scan)
                    on(b, rows_out)

                interleaved(dve, S.B // 2, step, chain)


def zero_fill(S, K, table, width, filled):
    step = 2 * CJ * width // TB
    flat = table.rearrange("(p g a) w -> p g (a w)", p=P, a=2 * CJ)
    groups = S.NJ // (2 * CJ)

    def run(eng):
        def body(i):
            eng.dma_start(flat[:, bass.ds(i, 1), :].rearrange("p a (r s) -> p (a r) s", s=step),
                          K.zeros[:, 0:step].unsqueeze(1).to_broadcast([P, TB, step])).then_inc(filled, 16)
        turns(eng, groups, body)
        eng.wait_ge(filled, 16 * groups)
    return run


def zero_fills(*fills):
    def run(eng):
        for fill in fills:
            fill(eng)
    return run


def given_order(nc, S, K, rows_in, rows_out, attr_in, attr_out, disorder):
    n = "given"
    with Stage(nc) as c:
        def sb(x, shape, dt=F32):
            return c.enter_context(nc.sbuf_tensor(f"{n}_{x}", shape, dt))

        cur, prv, edge = sb("cur", [S.B, BS, 4], I32), sb("prv", [S.B, BS, 4], I32), sb("edge", [2, 4], I32)
        key, pkey, lower, many = sb("key", [S.B, BS]), sb("pkey", [S.B, BS]), sb("lower", [S.B, BS]), sb("many", [S.B, 1])
        total = c.enter_context(nc.psum_tensor(f"{n}_total", [1, 512], F32))
        edge_made, attr_copied, copied, loaded, own, many_made, total_ready = (c.counter(f"{n}_{x}") for x in (
            "edge_made", "attr_copied", "copied", "loaded", "own", "many_made", "total_ready"))
        with nc.Block() as block:
            @block.gpsimd
            def _(pool):
                pool.memset(edge[:, :], -1).then_inc(edge_made, 1)

            @block.sync
            def _(sp):
                sp.dma_start(rows_out[1:S.EP + 1, :].rearrange("(b s) f -> b (s f)", s=BS),
                             rows_in.rearrange("(b s) f -> b (s f)", s=BS)).then_inc(copied, 16)
                sp.dma_start(attr_out.rearrange("(b s) f -> b (s f)", s=BS), attr_in.rearrange("(b s) f -> b (s f)", s=BS)
                             ).then_inc(attr_copied, 16)
                sp.wait_ge(edge_made, 1)
                sp.dma_start(rows_out[0:1, :], edge[0:1, :]).then_inc(copied, 16)
                sp.dma_start(rows_out[S.EP + 1:S.EP + 2, :], edge[1:2, :]).then_inc(copied, 16)
                sp.wait_ge(copied, 48)
                for off, tile in ((1, cur), (0, prv)):
                    sp.dma_start(tile[:, :, :], rows_out[off:off + S.EP, :].rearrange("(b s) f -> b s f", s=BS)
                                 ).then_inc(loaded, 16)
                sp.wait_ge(attr_copied, 16)

            @block.vector
            def _(dve):
                link = Chain(dve, own).link
                dve.wait_ge(loaded, 32)
                link(dve.tensor_copy(key[:, :], cur[:, :, 0]))
                link(dve.tensor_copy(pkey[:, :], prv[:, :, 0]))
                link(dve.tensor_tensor(lower[:, :], pkey[:, :], key[:, :], ALU.is_gt))
                dve.tensor_reduce(many[:, :], lower[:, :], AX.X, ALU.add).then_inc(many_made, 1)
                dve.wait_ge(total_ready, 1)
                link(dve.tensor_copy(disorder[:, :], total[0:1, 0:1]))

            @block.tensor
            def _(pe):
                pe.wait_ge(many_made, 1)
                pe.matmul(total[0:1, 0:1], many[:, 0:1], K.ones[0:S.B, 0:1], start=True, stop=True
                          ).then_inc(total_ready, 1)


def rows_by_src(nc, S, rows_a, rows_out):
    n = "by_src"
    with Stage(nc) as c:
        def sb(x, shape):
            return c.enter_context(nc.sbuf_tensor(f"{n}_{x}", shape, I32))

        cur, out, slot = sb("cur", [S.B, BS, 4]), sb("out", [S.B, BS, 4]), sb("slot", [S.B, BS])
        loaded, made, stored, zeroed = (c.counter(f"{n}_{x}") for x in (
            "loaded", "made", "stored", "zeroed"))
        with nc.Block() as block:
            @block.sync
            def _(sp):
                sp.dma_start(cur[:, :, :], rows_a[1:S.EP + 1, :].rearrange("(b s) f -> b s f", s=BS)
                             ).then_inc(loaded, 16)
                sp.wait_ge(made, 2)
                sp.dma_start(rows_out.rearrange("(b s) f -> b s f", s=BS), out[:, :, :]).then_inc(stored, 16)
                sp.wait_ge(stored, 16)

            @block.gpsimd
            def _(pool):
                pool.iota(slot[:, :], [[1, BS]], base=0, channel_multiplier=BS).then_inc(zeroed, 1)

            @block.vector
            def _(dve):
                dve.memset(out[:, :, :], 0).then_inc(zeroed, 1)
                dve.wait_ge(zeroed, 2)
                dve.tensor_copy(out[:, :, 2], slot[:, :]).then_inc(made, 1)
                dve.wait_ge(loaded, 16)
                dve.tensor_copy(out[:, :, 0], cur[:, :, 1]).then_inc(made, 1)


def gnn_preln_d4(nc, n, e, inp, out):
    S = Shapes(n, e)

    def dram(name, shape, dt=F32):
        return nc.dram_tensor(name, shape, dt).ap()

    with Stage(nc) as c:
        def sb(x, shape, dt=F32):
            return c.enter_context(nc.sbuf_tensor(x, shape, dt))

        def wt(x, shape):
            return sb(f"weights_{x}", shape)

        class W:
            base_w, base_w2, base_b = wt("base_w", [P, D]), wt("base_w2", [P, 2 * D]), wt("base_b", [P, D])
            gcn_w, gcn_b = wt("gcn_w", [P, 2 * D]), wt("gcn_b", [P, D])
            node_w, node_b = wt("node_w", [P, 2 * EW]), wt("node_b", [P, D])
            msg_b, edge_w, sum_w = wt("msg_b", [P, 2 * MSG]), wt("edge_w", [ED, MSG]), wt("sum_w", [MSG, D])
            conv1, al_w, conv2 = wt("conv1", [P, GF]), wt("al_w", [P, 4 * HEADS]), wt("conv2", [P, HALVES, NW2])
            bias1, nbias1, bias2 = wt("bias1", [P, HALVES]), wt("nbias1", [P, HALVES]), wt("bias2", [P, D])
            spread = wt("spread", [HEADS, HALVES, P])

        K = make_constants(nc, c)
        s2d, d2s = Side(nc, c, "s2d"), Side(nc, c, "d2s")
        pna_weights(nc, S, K, s2d, 0, inp, W)
        pna_weights(nc, S, K, d2s, 1, inp, W)
        gat_weights(nc, S, K, W, inp)

        mid_a, rows_a, mid_b, rows_b = (dram(x, [S.EP + 2, 4], I32) for x in ("mid_a", "rows_a", "mid_b", "rows_b"))
        src_rows = dram("src_rows", [S.EP, 4], I32)
        flags_a, flags_b = dram("flags_a", [2, S.EP]), dram("flags_b", [2, S.EP])
        agg_a, agg_b = dram("agg_a", [S.NP, DAW]), dram("agg_b", [S.NP, DAW])
        gcn_delta, sum_delta = dram("gcn_delta", [S.NP, D]), dram("sum_delta", [S.NP, D])
        filled = [c.counter(f"filled{j}") for j in range(4)]
        index_a, index_b = sb("index_a", [P, S.B, 4 * TB], I32), sb("index_b", [P, S.B, 2 * TB], I32)
        counts_a, counts_b = (Counts(*(sb(f"counts_{o}{j}", [P, S.B, TB])[:, :, :] for j in range(k)))
                              for o, k in (("a", 4), ("b", 3)))
        attr_a = dram("attr_a", [S.EP, ED])
        disorder = sb("disorder", [1, 1], I32)
        given_order(nc, S, K, inp["edge_rows"], rows_a, inp["edge_attr"], attr_a, disorder)
        with nc.If(nc.values_load(disorder[0:1, 0:1], min_val=0, max_val=S.EP) > 0):
            sort_pass(nc, S, K, "sort_a0", inp["edge_rows"], mid_a, 0, S.LO)
            sort_pass(nc, S, K, "sort_a1", mid_a[1:S.EP + 1, :], rows_a, RADIX_BITS, S.HI)
            prepare_order(nc, S, K, "sorted_a", rows_a, [0, 1, "end", 2], index_a, flags_a, counts_a)
            attr_pass(nc, S, inp["edge_attr"], index_a, attr_a)
        prepare_order(nc, S, K, "order_a", rows_a, [0, 1, "end", 2], index_a, flags_a, counts_a)
        rows_by_src(nc, S, rows_a, src_rows)

        sort_pass(nc, S, K, "sort_b0", src_rows, mid_b, 0, S.LO,
                  zero_fills(zero_fill(S, K, agg_a, DAW, filled[0]), zero_fill(S, K, agg_b, DAW, filled[1])))
        sort_pass(nc, S, K, "sort_b1", mid_b[1:S.EP + 1, :], rows_b, RADIX_BITS, S.HI,
                  zero_fills(zero_fill(S, K, gcn_delta, D, filled[2]), zero_fill(S, K, sum_delta, D, filled[3])))
        prepare_order(nc, S, K, "order_b", rows_b, [2, "end"], index_b, flags_b, counts_b)

        h0, msgs = dram("h0", [S.NP, D]), dram("msgs", [S.EP, D])
        norm_pass(nc, S, K, inp["x"], h0)
        pna_pass(nc, S, K, s2d, h0, index_a, [0, 1], 2, flags_a, counts_a, agg_a, (d2s, msgs))
        pna_pass(nc, S, K, d2s, msgs, index_b, [0], 1, flags_b, counts_b, agg_b)

        base1, scaled1 = dram("base1", [S.NP, D]), dram("scaled1", [S.NP, D])
        pna_out_pass(nc, S, K, inp["x"], h0, agg_a, agg_b, W, base1, scaled1)
        sum_pass(nc, S, K, "gcn", scaled1, D, index_a, 1, 2, flags_a, W.gcn_w[0:D, 0:D], gcn_delta, counts_a.dinv)

        base2, ends, factors = dram("base2", [S.NP, D]), dram("ends", [S.NP, 2 * MSG]), dram("factors", [S.EP, MSG])
        gcn_out_pass(nc, S, K, base1, gcn_delta, W, base2, ends)
        message_pass(nc, S, K, ends, attr_a, index_a, W.edge_w[:, :], factors)
        sum_pass(nc, S, K, "fac", factors, MSG, index_b, 0, 1, flags_b, W.sum_w[:, :], sum_delta)

        hx, tx = dram("hx", [S.NP, HX]), dram("tx", [S.NP, TX])
        sums_out_pass(nc, S, K, base2, sum_delta, W, hx, tx, out)
        gat1_pass(nc, S, K, hx, index_a, flags_a, W, tx)
        gat2_pass(nc, S, K, tx, index_a, flags_a, W, out)


def laid_out(inputs):
    a = {k: np.asarray(v) for k, v in inputs.items()}
    n, e = a["x"].shape[0], a["src"].shape[0]
    S = Shapes(n, e)
    T, FI = 4, D // 4

    def twice(v):
        return np.block([[v, np.zeros_like(v)], [np.zeros_like(v), v]])

    def padded(v, rows):
        return np.concatenate([v, np.zeros((rows - v.shape[0], v.shape[1]), v.dtype)])

    edges = np.zeros((S.EP, 4), np.int32)
    edges[:, 0:2], edges[:, 2] = n, np.arange(S.EP)
    edges[:e, 0], edges[:e, 1] = a["dst"], a["src"]
    r = {"edge_rows": edges, "x": padded(a["x"], S.NP), "edge_attr": padded(a["edge_attr_32"], S.EP)}

    for side, swap in (("s2d", 0), ("d2s", 1)):
        def w(k):
            return a[f"L0_gnn_{k}_{side}"]
        pre = np.zeros((P, D), np.float32)
        post = []
        for t in range(T):
            for h in range(2):
                at = (h ^ swap) * D + t * FI
                pre[at:at + FI, t * FI:(t + 1) * FI] = w("pre_W")[t, h * FI:(h + 1) * FI]
        for j in [0, 0] + [1 + 4 * s + agg for s in range(3) for agg in (0, 3, 2, 1)]:
            m = np.zeros((D, D), np.float32)
            for t in range(T):
                m[t * FI:(t + 1) * FI, t * FI:(t + 1) * FI] = w("post_W")[t, j * FI:(j + 1) * FI].T
            post.append(m)
        bias = w("pre_b").reshape(D, 1)
        r.update({f"pre_{side}": np.concatenate([pre, pre], 1), f"preb_{side}": np.concatenate([bias, bias]),
                  f"post_{side}": np.concatenate(post, 1), f"postb_{side}": w("post_b").reshape(D, 1),
                  f"lin_{side}": w("lin_W"), f"linb_{side}": w("lin_b")})
    r.update({"alpha": a["L0_gnn_alpha"], "self_w": a["L0_gnn_lin_self_W"], "self_b": a["L0_gnn_lin_self_b"]})

    gcn = a["L1_gnn_W"].T
    fe, fh = a["L2_gnn_fe_w"].T, a["L2_gnn_fh_w"].T
    node = np.concatenate([fh[0:D], fe[0:D], fe[D:2 * D]], 1)
    r.update({"gcn_w": twice(gcn), "gcn_b": a["L1_gnn_b"],
              "node_w": twice(node), "node_b": a["L2_gnn_fh_b"], "msg_b": a["L2_gnn_fe_b"],
              "edge_w": fe[2 * D:2 * D + ED], "sum_w": fh[D:D + MSG]})

    w1, w2 = a["L3_gnn_W1"], a["L3_gnn_W2"]
    a1 = np.zeros((GF, 2 * HEADS), np.float32)
    for h in range(HEADS):
        a1[h * HC:(h + 1) * HC, h] = a["L3_gnn_a1_src"][h]
        a1[h * HC:(h + 1) * HC, HEADS + h] = a["L3_gnn_a1_dst"][h]
    r.update({"w1": np.concatenate([w1, w1]), "w1t": np.concatenate([w1.T, w1.T], 1), "a1": a1, "w2": w2, "w2t": w2.T,
              "a2": np.concatenate([a["L3_gnn_a2_src"], a["L3_gnn_a2_dst"]]).T,
              "b1": a["L3_gnn_b1"], "b2": a["L3_gnn_b2"]})
    return n, e, {k: np.ascontiguousarray(v) for k, v in r.items()}


def kernel(**inputs):
    import concourse.bacc as _bacc
    from concourse import mybir as _mybir
    from concourse.bass_utils import run_bass_kernel_spmd as _run

    n, e, arrays = laid_out(inputs)
    nc = _bacc.Bacc("TRN2", target_bir_lowering=False, num_devices=1)
    aps = {k: nc.dram_tensor(f"in_{k}", v.shape, _mybir.dt.from_np(v.dtype), kind="ExternalInput").ap()
           for k, v in arrays.items()}
    out = nc.dram_tensor("out_nodes", [Shapes(n, e).NP, D], F32, kind="ExternalOutput").ap()
    gnn_preln_d4(nc, n, e, aps, out)
    r = _run(nc, [{f"in_{k}": v for k, v in arrays.items()}], core_ids=[0])
    return r.results[0]["out_nodes"][:n]
```
